# Optimizing a Trainium2 kernel written in Bass

```python
import numpy as np
import jax
import jax.numpy as jnp

def _softmax(x, axis=-1):
    return jax.nn.softmax(x, axis=axis)

def _gelu(x):
    return jax.nn.gelu(x, approximate=True)

def _silu(x):
    return jax.nn.silu(x)

def _sigmoid(x):
    return jax.nn.sigmoid(x)

def _layernorm(x, axis=-1, eps=1e-05):
    m = jnp.mean(x, axis=axis, keepdims=True)
    v = jnp.var(x, axis=axis, keepdims=True)
    return (x - m) / jnp.sqrt(v + eps)

def _scatter_add(tgt, idx, src, axis=0):
    return tgt.at[idx].add(src)

def _segment_sum(src, seg, n):
    return jax.ops.segment_sum(src, seg, n)
kernel_name = 'mk_lm_tower_d2_tok_ids768_r4_9f5092'

def setup_inputs(seed: int=0):
    np.random.seed(seed)
    _w = jnp.asarray

    def _rec_inputs():
        import jax
        import jax.numpy as jnp
        _rk = jax.random.key(seed)
        x = jax.random.randint(jax.random.fold_in(_rk, 1), (16, 512), 0, 12564, jnp.int32)
        return x
    x = _rec_inputs()

    def _L0_tok_setup():
        import jax, jax.numpy as jnp
        import numpy as np
        VOCAB = 50257
        SEQ = 512
        DIM = 192
        BATCH = 8
        key = jax.random.key(seed)
        k1, k2, k3 = jax.random.split(key, 3)
        tokens = jax.random.randint(k1, (BATCH, SEQ), 0, VOCAB, dtype=jnp.int32)
        W_emb = jax.random.normal(k2, (DIM, VOCAB), dtype=jnp.float32) * 0.02
        W_pos = jax.random.normal(k3, (SEQ, DIM), dtype=jnp.float32) * 0.02
        return {'tokens': tokens, 'W_emb': W_emb, 'W_pos': W_pos}
    _L0_tok_all = _L0_tok_setup()
    _L0_tok_in = {k: v for k, v in _L0_tok_all.items() if k in ('W_emb', 'W_pos')}
    del _L0_tok_all

    def _L0_attn_setup():
        import jax, jax.numpy as jnp
        import numpy as np
        B_, L_, DM, DS, DC, EXP = (2, 1024, 192, 64, 4, 2)
        DI = DM * EXP
        key = jax.random.key(seed)
        ks = jax.random.split(key, 8)
        s = lambda k, shape, scale: jax.random.normal(k, shape, jnp.float32) * scale
        return {'x': jax.random.normal(ks[0], (B_, L_, DM), jnp.float32), 'in_w': s(ks[1], (DM, 2 * DI), DM ** (-0.5)), 'conv_w': s(ks[2], (DI, 1, DC), DC ** (-0.5)), 'conv_b': jnp.zeros((DI,), jnp.float32), 'xproj_w': s(ks[3], (DI, 2 * DS + 1), DI ** (-0.5)), 'A_log': jnp.tile(jnp.log(jnp.arange(1, DS + 1, dtype=jnp.float32))[None, :], (DI, 1)), 'dt_bias': jax.random.uniform(ks[4], (DI,), jnp.float32, float(np.log(0.001)), float(np.log(0.1))), 'D': jnp.ones((DI,), jnp.float32), 'out_w': s(ks[5], (DI, DM), DI ** (-0.5))}
    _L0_attn_all = _L0_attn_setup()
    _L0_attn_in = {k: v for k, v in _L0_attn_all.items() if k in ('in_w', 'conv_w', 'conv_b', 'xproj_w', 'A_log', 'dt_bias', 'D', 'out_w')}
    del _L0_attn_all

    def _L0_ffn_setup():
        import jax, jax.numpy as jnp
        import numpy as np
        S, B, DIM = (256, 4, 192)
        N_EXPERTS = 8
        HID = 512
        key = jax.random.key(seed)
        ks = jax.random.split(key, 6)
        scale = 0.02
        return {'hidden_states': jax.random.normal(ks[0], (S, B, DIM), dtype=jnp.float32), 'router_w': jax.random.normal(ks[1], (DIM, N_EXPERTS), dtype=jnp.float32) * scale, 'router_b': jnp.zeros((N_EXPERTS,), dtype=jnp.float32), 'w1': jax.random.normal(ks[2], (N_EXPERTS, DIM, HID), dtype=jnp.float32) * scale, 'w2': jax.random.normal(ks[3], (N_EXPERTS, DIM, HID), dtype=jnp.float32) * scale, 'w3': jax.random.normal(ks[4], (N_EXPERTS, HID, DIM), dtype=jnp.float32) * scale}
    _L0_ffn_all = _L0_ffn_setup()
    _L0_ffn_in = {k: v for k, v in _L0_ffn_all.items() if k in ('router_w', 'router_b', 'w1', 'w2', 'w3')}
    del _L0_ffn_all

    def _L1_attn_setup():
        import jax, jax.numpy as jnp
        import numpy as np
        EMBED_DIM = 192
        NUM_HEADS = 12
        HEAD_DIM = EMBED_DIM // NUM_HEADS
        key = jax.random.key(seed)
        k_x, k_wqkv, k_bqkv, k_wo, k_bo = jax.random.split(key, 5)
        scale_in = 1.0 / np.sqrt(EMBED_DIM)
        x = jax.random.normal(k_x, (2, 512, EMBED_DIM), dtype=jnp.float32)
        W_qkv = jax.random.uniform(k_wqkv, (EMBED_DIM, 3 * EMBED_DIM), jnp.float32, -scale_in, scale_in)
        b_qkv = jax.random.uniform(k_bqkv, (3 * EMBED_DIM,), jnp.float32, -scale_in, scale_in)
        W_out = jax.random.uniform(k_wo, (EMBED_DIM, EMBED_DIM), jnp.float32, -scale_in, scale_in)
        b_out = jax.random.uniform(k_bo, (EMBED_DIM,), jnp.float32, -scale_in, scale_in)
        return {'x': x, 'W_qkv': W_qkv, 'b_qkv': b_qkv, 'W_out': W_out, 'b_out': b_out}
    _L1_attn_all = _L1_attn_setup()
    _L1_attn_in = {k: v for k, v in _L1_attn_all.items() if k in ('W_qkv', 'b_qkv', 'W_out', 'b_out')}
    del _L1_attn_all

    def _L1_ffn_setup():
        import jax, jax.numpy as jnp
        import numpy as np
        from jax import lax
        DIM = 192
        INTER = 128
        E = 8
        G = 4
        TOPK_G = 2
        TOPK = 2
        ROUTE_SCALE = 1.0

        def _gate(x2, gate_weight, gate_bias):
            T = x2.shape[0]
            scores = jax.nn.sigmoid(x2 @ gate_weight.T)
            s = scores + gate_bias
            sv = s.reshape(T, G, E // G)
            top2, _ = lax.top_k(sv, 2)
            group_scores = top2.sum(-1)
            _, gidx = lax.top_k(group_scores, TOPK_G)
            gmask = jnp.zeros((T, G), bool).at[jnp.arange(T)[:, None], gidx].set(True)
            masked = jnp.where(gmask[:, :, None], sv, -jnp.inf).reshape(T, E)
            _, idx = lax.top_k(masked, TOPK)
            w = jnp.take_along_axis(scores, idx, axis=1)
            w = w / (w.sum(-1, keepdims=True) + 1e-06) * ROUTE_SCALE
            return (w, idx)
        key = jax.random.key(seed)
        ks = jax.random.split(key, 9)
        s = 1.0 / np.sqrt(DIM)
        si = 1.0 / np.sqrt(INTER)
        return {'x': jax.random.normal(ks[0], (4, 1024, DIM), jnp.float32), 'gate_weight': jax.random.uniform(ks[1], (E, DIM), jnp.float32, -s, s), 'gate_bias': jnp.zeros((E,), jnp.float32), 'w1': jax.random.uniform(ks[2], (E, INTER, DIM), jnp.float32, -s, s), 'w2': jax.random.uniform(ks[3], (E, DIM, INTER), jnp.float32, -si, si), 'w3': jax.random.uniform(ks[4], (E, INTER, DIM), jnp.float32, -s, s), 'sw1': jax.random.uniform(ks[5], (INTER, DIM), jnp.float32, -s, s), 'sw2': jax.random.uniform(ks[6], (DIM, INTER), jnp.float32, -si, si), 'sw3': jax.random.uniform(ks[7], (INTER, DIM), jnp.float32, -s, s)}
    _L1_ffn_all = _L1_ffn_setup()
    _L1_ffn_in = {k: v for k, v in _L1_ffn_all.items() if k in ('gate_weight', 'gate_bias', 'w1', 'w2', 'w3', 'sw1', 'sw2', 'sw3')}
    del _L1_ffn_all
    return {'x': x, 'L0_tok_W_emb': _L0_tok_in['W_emb'], 'L0_tok_W_pos': _L0_tok_in['W_pos'], 'L0_attn_in_w': _L0_attn_in['in_w'], 'L0_attn_conv_w': _L0_attn_in['conv_w'], 'L0_attn_conv_b': _L0_attn_in['conv_b'], 'L0_attn_xproj_w': _L0_attn_in['xproj_w'], 'L0_attn_A_log': _L0_attn_in['A_log'], 'L0_attn_dt_bias': _L0_attn_in['dt_bias'], 'L0_attn_D': _L0_attn_in['D'], 'L0_attn_out_w': _L0_attn_in['out_w'], 'L0_ffn_router_w': _L0_ffn_in['router_w'], 'L0_ffn_router_b': _L0_ffn_in['router_b'], 'L0_ffn_w1': _L0_ffn_in['w1'], 'L0_ffn_w2': _L0_ffn_in['w2'], 'L0_ffn_w3': _L0_ffn_in['w3'], 'L1_attn_W_qkv': _L1_attn_in['W_qkv'], 'L1_attn_b_qkv': _L1_attn_in['b_qkv'], 'L1_attn_W_out': _L1_attn_in['W_out'], 'L1_attn_b_out': _L1_attn_in['b_out'], 'L1_ffn_gate_weight': _L1_ffn_in['gate_weight'], 'L1_ffn_gate_bias': _L1_ffn_in['gate_bias'], 'L1_ffn_w1': _L1_ffn_in['w1'], 'L1_ffn_w2': _L1_ffn_in['w2'], 'L1_ffn_w3': _L1_ffn_in['w3'], 'L1_ffn_sw1': _L1_ffn_in['sw1'], 'L1_ffn_sw2': _L1_ffn_in['sw2'], 'L1_ffn_sw3': _L1_ffn_in['sw3']}

def reference(x, L0_tok_W_emb, L0_tok_W_pos, L0_attn_in_w, L0_attn_conv_w, L0_attn_conv_b, L0_attn_xproj_w, L0_attn_A_log, L0_attn_dt_bias, L0_attn_D, L0_attn_out_w, L0_ffn_router_w, L0_ffn_router_b, L0_ffn_w1, L0_ffn_w2, L0_ffn_w3, L1_attn_W_qkv, L1_attn_b_qkv, L1_attn_W_out, L1_attn_b_out, L1_ffn_gate_weight, L1_ffn_gate_bias, L1_ffn_w1, L1_ffn_w2, L1_ffn_w3, L1_ffn_sw1, L1_ffn_sw2, L1_ffn_sw3):
    import jax
    import jax.numpy as jnp

    def _L0_tok_ref(tokens, W_emb, W_pos):
        import jax, jax.numpy as jnp
        import numpy as np
        VOCAB = 50257
        SEQ = 512
        DIM = 192
        BATCH = 8
        tok_emb = jnp.take(W_emb.T, tokens, axis=0)
        return tok_emb + W_pos

    def _L0_attn_ref(x, in_w, conv_w, conv_b, xproj_w, A_log, dt_bias, D, out_w):
        import jax, jax.numpy as jnp
        import numpy as np
        B_, L_, DM, DS, DC, EXP = (2, 1024, 192, 64, 4, 2)
        DI = DM * EXP
        batch, seq_len, _ = x.shape
        d_inner = conv_b.shape[0]
        d_state = A_log.shape[1]
        xz = x @ in_w
        x_ssm, z = (xz[..., :d_inner], xz[..., d_inner:])
        xc = jax.lax.conv_general_dilated(x_ssm.transpose(0, 2, 1), conv_w, (1,), [(conv_w.shape[-1] - 1, 0)], feature_group_count=d_inner, dimension_numbers=('NCH', 'OIH', 'NCH'))
        xc = (xc + conv_b[None, :, None]).transpose(0, 2, 1)
        xc = jax.nn.silu(xc)
        p = xc @ xproj_w
        Bm = p[..., :d_state]
        Cm = p[..., d_state:2 * d_state]
        dt = jax.nn.softplus(p[..., -1:] + dt_bias)
        A = -jnp.exp(A_log)

        def step(h, ins):
            xt, Bt, Ct, dtt = ins
            A_bar = jnp.exp(A * dtt[..., None])
            h = A_bar * h + dtt[..., None] * Bt[:, None, :] * xt[..., None]
            y = jnp.einsum('bn,bdn->bd', Ct, h)
            return (h, y)
        h0 = jnp.zeros((batch, d_inner, d_state), x.dtype)
        ins = (xc.transpose(1, 0, 2), Bm.transpose(1, 0, 2), Cm.transpose(1, 0, 2), dt.transpose(1, 0, 2))
        _, ys = jax.lax.scan(step, h0, ins)
        y = ys.transpose(1, 0, 2)
        y = y + D * xc
        y = y * jax.nn.silu(z)
        return y @ out_w

    def _L0_ffn_ref(hidden_states, router_w, router_b, w1, w2, w3):
        import jax, jax.numpy as jnp
        import numpy as np
        S, B, DIM = (256, 4, 192)
        N_EXPERTS = 8
        HID = 512
        s, b, h = hidden_states.shape
        route = jax.nn.softmax(hidden_states @ router_w + router_b, axis=2)
        max_prob = jnp.max(route, axis=2).reshape(-1, 1)
        max_ind = jnp.argmax(route, axis=2).reshape(-1)
        x = hidden_states.reshape(-1, h)
        out = jnp.zeros_like(x)
        for e in range(N_EXPERTS):
            mask = (max_ind == e)[:, None]
            xe = jnp.where(mask, x, 0.0)
            oe = jax.nn.silu(xe @ w1[e]) * (xe @ w2[e]) @ w3[e]
            out = out + jnp.where(mask, oe, 0.0)
        out = out.astype(jnp.bfloat16) * max_prob
        return out.reshape(s, b, h)

    def _L1_attn_ref(x, W_qkv, b_qkv, W_out, b_out):
        import jax, jax.numpy as jnp
        import numpy as np
        EMBED_DIM = 192
        NUM_HEADS = 12
        HEAD_DIM = EMBED_DIM // NUM_HEADS
        B, S, E = x.shape
        H, D = (NUM_HEADS, HEAD_DIM)
        qkv = x @ W_qkv + b_qkv
        qkv = qkv.reshape(B, S, 3, H, D)
        q, k, v = (qkv[:, :, i].transpose(0, 2, 1, 3) for i in range(3))
        scores = jnp.einsum('bhqd,bhkd->bhqk', q, k) / np.sqrt(D).astype(jnp.float32)
        attn = jax.nn.softmax(scores, axis=-1)
        out = jnp.einsum('bhqk,bhkd->bhqd', attn, v)
        out = out.transpose(0, 2, 1, 3).reshape(B, S, E)
        return out @ W_out + b_out

    def _L1_ffn_ref(x, gate_weight, gate_bias, w1, w2, w3, sw1, sw2, sw3):
        import jax, jax.numpy as jnp
        import numpy as np
        from jax import lax
        DIM = 192
        INTER = 128
        E = 8
        G = 4
        TOPK_G = 2
        TOPK = 2
        ROUTE_SCALE = 1.0

        def _gate(x2, gate_weight, gate_bias):
            T = x2.shape[0]
            scores = jax.nn.sigmoid(x2 @ gate_weight.T)
            s = scores + gate_bias
            sv = s.reshape(T, G, E // G)
            top2, _ = lax.top_k(sv, 2)
            group_scores = top2.sum(-1)
            _, gidx = lax.top_k(group_scores, TOPK_G)
            gmask = jnp.zeros((T, G), bool).at[jnp.arange(T)[:, None], gidx].set(True)
            masked = jnp.where(gmask[:, :, None], sv, -jnp.inf).reshape(T, E)
            _, idx = lax.top_k(masked, TOPK)
            w = jnp.take_along_axis(scores, idx, axis=1)
            w = w / (w.sum(-1, keepdims=True) + 1e-06) * ROUTE_SCALE
            return (w, idx)
        B, S, D = x.shape
        x2 = x.reshape(-1, D)
        T = x2.shape[0]
        weights, indices = _gate(x2, gate_weight, gate_bias)
        cw = jnp.zeros((T, E), x.dtype).at[jnp.arange(T)[:, None], indices].add(weights)
        h1 = jnp.einsum('td,eid->tei', x2, w1)
        h3 = jnp.einsum('td,eid->tei', x2, w3)
        h = jax.nn.silu(h1) * h3
        y = jnp.einsum('tei,edi,te->td', h, w2, cw)
        z = jax.nn.silu(x2 @ sw1.T) * (x2 @ sw3.T) @ sw2.T
        return (y + z).reshape(B, S, D)
    h = _L0_tok_ref(x, L0_tok_W_emb, L0_tok_W_pos)
    h = h + _L0_attn_ref(_layernorm(h, axis=-1), L0_attn_in_w, L0_attn_conv_w, L0_attn_conv_b, L0_attn_xproj_w, L0_attn_A_log, L0_attn_dt_bias, L0_attn_D, L0_attn_out_w)
    h = h + _L0_ffn_ref(_layernorm(h, axis=-1), L0_ffn_router_w, L0_ffn_router_b, L0_ffn_w1, L0_ffn_w2, L0_ffn_w3)
    h = h + _L1_attn_ref(_layernorm(h, axis=-1), L1_attn_W_qkv, L1_attn_b_qkv, L1_attn_W_out, L1_attn_b_out)
    h = h + _L1_ffn_ref(_layernorm(h, axis=-1), L1_ffn_gate_weight, L1_ffn_gate_bias, L1_ffn_w1, L1_ffn_w2, L1_ffn_w3, L1_ffn_sw1, L1_ffn_sw2, L1_ffn_sw3)
    return h

_drawn_inputs = setup_inputs


def setup_inputs(seed=0):
    import zlib

    import numpy as np

    out = dict(_drawn_inputs(seed))
    spreads = {'L0_attn_conv_b': (0.0, 0.1),
     'L0_attn_D': (1.0, 0.2),
     'L0_ffn_router_b': (0.0, 0.748),
     'L1_ffn_gate_bias': (0.0, 0.1)}
    factors = {'L0_ffn_router_w': 3.171, 'L0_ffn_w1': 3.212, 'L0_ffn_w2': 3.132, 'L0_ffn_w3': 3.07}
    for name, (base, spread) in spreads.items():
        noise = np.random.default_rng([zlib.crc32(name.encode()), seed]).standard_normal(out[name].shape)
        drawn = base * np.exp(spread * noise) if base else spread * noise
        out[name] = jnp.asarray(drawn.astype(out[name].dtype))
    for name, factor in factors.items():
        out[name] = (out[name] * factor).astype(out[name].dtype)
    return out
```

```python
from contextlib import ExitStack

import numpy as np

import concourse.bass as bass
from concourse import mybir

F32 = mybir.dt.float32
BF16 = mybir.dt.bfloat16
I32 = mybir.dt.int32
U32 = mybir.dt.uint32
ALU = mybir.AluOpType
ACT = mybir.ActivationFunctionType
AX = mybir.AxisListType

P = 128
NB = 16
T = 512
TC = T // P
D = 192
KP, KT = 96, 2
DI = 384
M3 = DI // P
NS = 64
TAPS = 4
SETS = 4
E = 8
HID = 512
HT = HID // P
INTER = 128
HEADS, HD = 12, 16
HG = 3
EPS = 1e-5
U8 = 8


class Signal:

    def __init__(self, sem, per, start=0):
        self.sem, self.per, self.start = sem, per, start

    def at(self, b, n):
        return b * self.per + (self.start + n)


def tower(nc, tok, emb, pos, in_w, conv_w, conv_b, xproj_w, xproj_dt, a_log, dt_bias, d_skip, out_w,
          router_w, router_b, w1, w2, w3, wq, wk, wv, bq, bk, bv, wo, bo,
          gate_w, gate_b, f1, f3, f2, out):
    ctx = ExitStack()
    with ctx:
        def sb(name, shape, dt=F32):
            return ctx.enter_context(nc.sbuf_tensor(name, shape, dt))

        def ps(name, shape, dt=F32):
            return ctx.enter_context(nc.psum_tensor(name, shape, dt))

        def sig(name, per, start=0):
            return Signal(ctx.enter_context(nc.semaphore(name)), per, start)

        ident = sb("ident", [P, P])
        onehot = sb("onehot", [96, 32, P], BF16)
        neg_half = sb("neg_half", [P, TC])
        idx_all = sb("idx_all", [P, NB * TC], I32)
        pos_sb = sb("pos_sb", [P, TC, D])
        in_w_sb = sb("in_w_sb", [KP, KT, 2 * DI])
        conv_w_sb = sb("conv_w_sb", [P, M3, TAPS])
        conv_b_sb = sb("conv_b_sb", [P, M3])
        conv_wh = sb("conv_wh", [P, M3, TAPS])
        conv_bh = sb("conv_bh", [P, M3])
        xproj_bc = sb("xproj_bc", [P, M3, SETS, 96])
        xproj_q = sb("xproj_q", [P, M3, 1])
        xproj_qr = sb("xproj_qr", [P, M3, P])
        a_log_sb = sb("a_log_sb", [P, M3, NS])
        a_exp = sb("a_exp", [P, M3, NS])
        a_neg = sb("a_neg", [P, M3, NS])
        dt_bias_sb = sb("dt_bias_sb", [P, M3])
        d_skip_sb = sb("d_skip_sb", [P, M3])
        diag_d = sb("diag_d", [P, M3, P])
        out_w_sb = sb("out_w_sb", [P, M3, D])
        router_w_sb = sb("router_w_sb", [KP, KT, E])
        router_b_sb = sb("router_b_sb", [P, E])
        falling = sb("falling", [P, E], F32)
        falling_i = sb("falling_i", [P, E], I32)
        wq_sb = sb("wq_sb", [KP, KT, HG * P])
        wk_sb = sb("wk_sb", [KP, KT, HG * P])
        wv_sb = sb("wv_sb", [KP, KT, D])
        bq_sb = sb("bq_sb", [P, HG])
        bk_sb = sb("bk_sb", [P, HG])
        bv_sb = sb("bv_sb", [P, D])
        wo_sb = sb("wo_sb", [KP, KT, D])
        bo_sb = sb("bo_sb", [P, D])
        gate_w_sb = sb("gate_w_sb", [KP, KT, E])
        gate_b_sb = sb("gate_b_sb", [P, E])
        before = sb("before", [P, E, E])
        f1_sb = sb("f1_sb", [KP, KT, E + 1, INTER])
        f3_sb = sb("f3_sb", [KP, KT, E + 1, INTER])
        f2_sb = sb("f2_sb", [INTER, E + 1, D])

        idx = sb("idx", [P, TC], I32)
        h = sb("h", [P, TC, D])
        stats = sb("stats", [P, TC, 6])
        stat_count = sb("stat_count", [P, 1])
        mv = sb("mv", [P, TC, 2])
        vare = sb("vare", [P, TC])
        rstd = sb("rstd", [P, TC])
        xn = sb("xn", [P, TC, D])
        xnT = sb("xnT", [KP, KT, T])
        xs = sb("xs", [P, M3, TAPS - 1 + T])
        xc = sb("xc", [P, M3, T])
        gz = sb("gz", [P, M3, T])
        dt = sb("dt", [P, M3, T])
        u = sb("u", [P, M3, T])
        bc_s = sb("bc_s", [96, SETS, T], BF16)
        decay = [sb(f"decay{i}", [P, M3, T]) for i in range(2)]
        drive = [sb(f"drive{i}", [P, M3, T]) for i in range(2)]
        state = sb("state", [P, M3, T])
        weighed = [sb(f"weighed{i}", [P, M3, T]) for i in range(2)]
        b_sb = [sb(f"b_sb{i}", [P, T]) for i in range(2)]
        logit = sb("logit", [P, TC, E])
        top = sb("top", [P, TC])
        tie = sb("tie", [P, TC, E])
        rev = sb("rev", [P, TC, E])
        first = sb("first", [P, TC])
        chosen = sb("chosen", [P, TC, E])
        soft = sb("soft", [P, TC, E])
        soft_e = sb("soft_e", [P, TC, E])
        soft_s = sb("soft_s", [P, TC])
        prob = sb("prob", [P, TC])
        w1_sb = [sb(f"w1_sb{i}", [KP, KT, HID]) for i in range(2)]
        w2_sb = [sb(f"w2_sb{i}", [KP, KT, HID]) for i in range(2)]
        w3_sb = [sb(f"w3_sb{i}", [P, HT, D]) for i in range(2)]
        cw = sb("cw", [P, TC, E + 1])
        gate_s = sb("gate_s", [P, TC, E])
        gate_v = sb("gate_v", [P, TC, E])
        group_v = sb("group_v", [P, TC, 4])
        group_on = sb("group_on", [P, TC, 4])
        masked = sb("masked", [P, TC, E])
        rank = sb("rank", [P, TC, E])

        th = drive[0]
        sl = drive[1]

        qT, kT, qa = weighed[0], weighed[1], state
        moe = dt[:].rearrange("p m t -> p (m t)")[:, 0:TC * D].rearrange("p (c d) -> p c d", c=TC)
        moe_b = u[:].rearrange("p m t -> p (m t)")[:, 0:TC * D // 2].bitcast(BF16).rearrange("p (c d) -> p c d", c=TC)
        cmp_gt, cmp_eq = (b_sb[i][:, 0:TC * E * E].rearrange("p (c i j) -> p c i j", c=TC, i=E) for i in range(2))

        psY = ps("psY", [P, M3, T])
        psW = ps("psW", [P, 3, T])
        psB = ps("psB", [P, T])
        psC = ps("psC", [P, T])

        hid = [sb(f"hid{i}", [P, HT, T]) for i in range(2)]
        pT = hid
        vA = sb("vA", [P, TC, HEADS, HD + 1])
        neg_max = sb("neg_max", [P, TC, HG, P])
        r_sum = sb("r_sum", [P, TC, HEADS])
        oa = xn

        loaded = sig("loaded", 0)
        pool_set = sig("pool_set", 0)
        dve_set = sig("dve_set", 0)
        act_set = sig("act_set", 0)
        seq_free = sig("seq_free", 1, 0)
        idx_ready = sig("idx_ready", 1)
        gathered = sig("gathered", 16 * TC)
        h_ready = sig("h_ready", 1)
        LN = 4
        ln_step = sig("ln_step", LN * (2 * TC + 2))
        ln_rstd = sig("ln_rstd", LN)
        ln_xn = sig("ln_xn", LN * TC)
        tr = sig("tr", (LN + 1) * KT)
        xnT_ready = sig("xnT_ready", (LN + 1) * KT)
        proj = sig("proj", 2 * M3)
        xs_ready = sig("xs_ready", M3)
        z_tanh = sig("z_tanh", M3)
        z_gate = sig("z_gate", M3)
        conv = sig("conv", M3 * TAPS)
        conv_tanh = sig("conv_tanh", M3)
        xc_ready = sig("xc_ready", M3)
        xp = sig("xp", SETS + 1)
        split = sig("split", SETS * 5)
        sp_act = sig("sp_act", 4 * M3)
        dt_step = sig("dt_step", 5)
        b_bc = sig("b_bc", NS)
        b_copied = sig("b_copied", NS)
        c_bc = sig("c_bc", NS)
        decayed = sig("decayed", NS)
        driven = sig("driven", NS)
        scanned = sig("scanned", NS)
        weighed_s = sig("weighed_s", NS)
        summed = sig("summed", NS + 1)
        gated = sig("gated", 1)
        outp = sig("outp", 2)
        resid1 = sig("resid1", 2)
        route_mm = sig("route_mm", 1)
        route = sig("route", 8)
        route_exp = sig("route_exp", 1)

        wload = [sig(f"wload{i}", 16 * 3 * E // 2) for i in range(2)]
        hp = sig("hp", E * HT)
        htanh = sig("htanh", E * HT)
        hsilu = sig("hsilu", E * HT)
        hid_ready = sig("hid_ready", E * HT)
        eout = sig("eout", E)
        eacc = sig("eacc", E * TC)
        moe_fin = sig("moe_fin", 2)
        resid2 = sig("resid2", TC)
        qp = sig("qp", HG)
        kp = sig("kp", HG)
        vp = sig("vp", 2)
        q_ready = sig("q_ready", HG)
        k_ready = sig("k_ready", HG)
        v_ready = sig("v_ready", TC)
        s1 = sig("s1", HEADS * TC)
        mx = sig("mx", HEADS * TC)
        mx_tr = sig("mx_tr", HG)
        qa_ready = sig("qa_ready", HG)
        s2 = sig("s2", HEADS * TC)
        pexp = sig("pexp", HEADS * TC)
        pv = sig("pv", HEADS)
        a_norm = sig("a_norm", 6)
        ao = sig("ao", 2)
        resid3 = sig("resid3", 3)
        gate_mm = sig("gate_mm", 1)
        gate_tanh = sig("gate_tanh", 1)
        gate = sig("gate", 23)
        fp = sig("fp", E + 1)
        ftanh = sig("ftanh", E + 1)
        fsilu = sig("fsilu", E + 1)
        fhid = sig("fhid", E + 1)
        fout = sig("fout", E + 1)
        facc = sig("facc", (E + 1) * TC)
        stored = sig("stored", 16)

        n_loads = [0]
        block = ctx.enter_context(nc.Block())

        @block.sync
        def _(sp):
            def load(dst, src):
                sp.dma_start(dst, src).then_inc(loaded.sem, 16)
                n_loads[0] += 1

            load(idx_all[:], tok)
            load(pos_sb[:], pos.rearrange("(c p) d -> p c d", p=P))
            load(in_w_sb[:], in_w.rearrange("(k p) m -> p k m", p=KP))
            load(conv_w_sb[:], conv_w.rearrange("(m p) k -> p m k", p=P))
            load(a_log_sb[:], a_log.rearrange("(m p) n -> p m n", p=P))
            for vec, dst in ((conv_b, conv_b_sb), (dt_bias, dt_bias_sb), (d_skip, d_skip_sb)):
                load(dst[:], vec)
            xproj_v = xproj_w.rearrange("(m p) k -> p m k", p=P)
            for s in range(SETS):
                for r in range(3):
                    load(xproj_bc[:, :, s, 32 * r:32 * r + 32], xproj_v[:, :, 32 * s:32 * s + 32])
            load(xproj_q[:, :, 0], xproj_dt)
            load(out_w_sb[:], out_w.rearrange("(m p) d -> p m d", p=P))
            load(router_w_sb[:], router_w.rearrange("(k p) e -> p k e", p=KP))
            for vec, dst in ((router_b, router_b_sb), (bv, bv_sb), (bo, bo_sb), (gate_b, gate_b_sb)):
                load(dst[:], vec.rearrange("(o n) -> o n", o=1).to_broadcast([P, vec.shape[0]]))
            for w, dst in ((wq, wq_sb), (wk, wk_sb), (wv, wv_sb), (wo, wo_sb), (gate_w, gate_w_sb)):
                load(dst[:], w.rearrange("(k p) m -> p k m", p=KP))
            for vec, dst in ((bq, bq_sb), (bk, bk_sb)):
                load(dst[:], vec)
            for w, dst in ((f1, f1_sb), (f3, f3_sb)):
                for k in range(KT):
                    load(dst[:, k], w[:, k * KP:(k + 1) * KP, :].rearrange("e p i -> p e i"))
            load(f2_sb[:], f2.rearrange("e i d -> i e d"))
            sp.wait_ge(loaded.sem, 16 * n_loads[0])
            sp.sem_inc(seq_free.sem, 1)
            with sp.Fori(0, NB) as b:
                def expert_weights(e):
                    i = e % 2
                    if e >= 2:
                        sp.wait_ge(eout.sem, eout.at(b, e - 1))
                    else:
                        sp.wait_ge(h_ready.sem, h_ready.at(b, 1))
                    sp.dma_start(w1_sb[i][:], w1[e].rearrange("(k p) m -> p k m", p=KP)).then_inc(wload[i].sem, 16)
                    sp.dma_start(w2_sb[i][:], w2[e].rearrange("(k p) m -> p k m", p=KP)).then_inc(wload[i].sem, 16)
                    sp.dma_start(w3_sb[i][:], w3[e].rearrange("(k p) d -> p k d", p=P)).then_inc(wload[i].sem, 16)
                for e in range(E):
                    expert_weights(e)
                sp.wait_ge(facc.sem, facc.at(b, (E + 1) * TC))
                sp.dma_start(out[bass.ds(b, 1)].rearrange("o (c p) d -> p (o c) d", p=P), h[:]).then_inc(stored.sem, 16)
                sp.wait_ge(stored.sem, stored.at(b, 16))
                sp.sem_inc(seq_free.sem, 1)

        ALL_LOADED = 16 * n_loads[0]
        POOL_SETS = 11
        DVE_SETS = 15

        @block.gpsimd
        def _(pool):
            pool.memset(ident[:], 0.0).then_inc(pool_set.sem, 1)
            pool.memset(onehot[:], 0.0).then_inc(pool_set.sem, 1)
            pool.memset(before[:], 1.0).then_inc(pool_set.sem, 1)
            pool.memset(neg_half[:], -0.5).then_inc(pool_set.sem, 1)
            pool.iota(falling_i[:], pattern=[[-1, E]], base=E, channel_multiplier=0).then_inc(pool_set.sem, 1)
            pool.wait_ge(pool_set.sem, 5)
            pool.affine_select(out=ident[:], in_=ident[:], compare_op=ALU.not_equal, fill=1.0, base=0,
                               pattern=[[-1, P]], channel_multiplier=1).then_inc(pool_set.sem, 1)
            pool.affine_select(out=before[:], in_=before[:], compare_op=ALU.is_gt, fill=0.0, base=0,
                               pattern=[[1, E], [-1, E]], channel_multiplier=0).then_inc(pool_set.sem, 1)
            for r in range(3):
                pool.wait_ge(pool_set.sem, 7 + r)
                pool.affine_select(out=onehot[:], in_=onehot[:], compare_op=ALU.not_equal, fill=1.0,
                                   base=-32 * r, pattern=[[-1, 32], [0, P]],
                                   channel_multiplier=1).then_inc(pool_set.sem, 1)
            pool.tensor_copy(falling[:], falling_i[:]).then_inc(pool_set.sem, 1)
            pool.wait_ge(loaded.sem, ALL_LOADED)
            pool.wait_ge(pool_set.sem, POOL_SETS)

            with pool.Fori(0, NB) as b:
                def rstd_of(l):
                    pool.wait_ge(ln_step.sem, ln_step.at(b, (2 * TC + 2) * (l + 1)))
                    pool.tensor_tensor(rstd[:], vare[:], neg_half[:], ALU.pow).then_inc(ln_rstd.sem, 1)

                pool.wait_ge(seq_free.sem, seq_free.at(b, 1))
                pool.tensor_copy(idx[:], idx_all[:, bass.ds(b * TC, TC)]).then_inc(idx_ready.sem, 1)
                pool.wait_ge(pool_set.sem, POOL_SETS)
                pool.wait_ge(idx_ready.sem, idx_ready.at(b, 1))
                for c in range(TC):
                    pool.indirect_dma_start(
                        out=xn[:, c, :], out_offset=None, in_=emb,
                        in_offset=bass.IndirectOffsetOnAxis(ap=idx[:, c:c + 1].bitcast(U32), axis=0),
                    ).then_inc(gathered.sem, 16)
                rstd_of(0)

                def drive_step(n, at):
                    i = n % 2
                    pool.wait_ge(b_copied.sem, at(b_copied, 1))
                    if n >= 2:
                        pool.wait_ge(scanned.sem, at(scanned, -1))
                    pool.tensor_tensor(drive[i][:], u[:], b_sb[i][:].unsqueeze(1).to_broadcast([P, M3, T]),
                                       ALU.mult).then_inc(driven.sem, 1)

                pool.wait_ge(dt_step.sem, dt_step.at(b, 5))
                for n in range(U8):
                    drive_step(n, lambda s, k, n=n: s.at(b, n + k))
                with pool.Fori(1, NS // U8) as j:
                    for n in range(U8):
                        drive_step(n + U8, lambda s, k, n=n: s.at(b, n + k) + j * U8)
                for l in range(1, LN):
                    rstd_of(l)

        @block.scalar
        def _(act):
            act.wait_ge(loaded.sem, ALL_LOADED)
            act.activation(a_exp[:], a_log_sb[:], ACT.Exp).then_inc(act_set.sem, 1)

            with act.Fori(0, NB) as b:
                def copy_transposed(call):
                    for k in range(KT):
                        act.wait_ge(tr.sem, tr.at(b, call * KT + k + 1))
                        act.activation(xnT[:, k, :], psW[0:KP, k, :], ACT.Copy).then_inc(xnT_ready.sem, 1)

                copy_transposed(0)
                for m in range(M3):
                    act.wait_ge(proj.sem, proj.at(b, m + 1))
                    act.activation(xs[:, m, TAPS - 1:], psW[:, m, :], ACT.Copy).then_inc(xs_ready.sem, 1)
                for m in range(M3):
                    act.wait_ge(proj.sem, proj.at(b, M3 + m + 1))
                    act.activation(drive[0][:, m, :], psY[:, m, :], ACT.Tanh, scale=0.5).then_inc(z_tanh.sem, 1)
                for m in range(M3):
                    act.wait_ge(conv.sem, conv.at(b, M3 * (TAPS - 1) + m + 1))
                    act.activation(drive[1][:, m, :], xc[:, m, :], ACT.Tanh).then_inc(conv_tanh.sem, 1)
                act.wait_ge(xp.sem, xp.at(b, SETS + 1))
                for m in range(M3):
                    act.activation(dt[:, m, :], psC[:], ACT.Relu, bias=dt_bias_sb[:, m:m + 1]).then_inc(sp_act.sem, 1)
                for m in range(M3):
                    act.activation(weighed[0][:, m, :], psC[:], ACT.Abs, bias=dt_bias_sb[:, m:m + 1]).then_inc(sp_act.sem, 1)
                act.wait_ge(sp_act.sem, sp_act.at(b, 2 * M3))
                act.wait_ge(xc_ready.sem, xc_ready.at(b, M3))
                for m in range(M3):
                    act.activation(drive[0][:, m, :], weighed[0][:, m, :], ACT.Exp, scale=-1.0).then_inc(sp_act.sem, 1)
                act.wait_ge(sp_act.sem, sp_act.at(b, 3 * M3))
                for m in range(M3):
                    act.activation(drive[1][:, m, :], drive[0][:, m, :], ACT.Ln, bias=1.0).then_inc(sp_act.sem, 1)

                def scan_step(n, at, col):
                    i = n % 2
                    act.wait_ge(b_bc.sem, at(b_bc, 1))
                    if n >= 2:
                        act.wait_ge(driven.sem, at(driven, -1))
                    act.activation(b_sb[i][:], psB[:], ACT.Copy).then_inc(b_copied.sem, 1)
                    if n >= 2:
                        act.wait_ge(scanned.sem, at(scanned, -1))
                    for m in range(M3):
                        last = act.activation(decay[i][:, m, 1:T], dt[:, m, 1:T], ACT.Exp,
                                              scale=a_neg[:, m, col])
                    last.then_inc(decayed.sem, 1)

                act.wait_ge(dt_step.sem, dt_step.at(b, 4))
                for n in range(U8):
                    scan_step(n, lambda s, k, n=n: s.at(b, n + k), slice(n, n + 1))
                with act.Fori(1, NS // U8) as j:
                    for n in range(U8):
                        scan_step(n + U8, lambda s, k, n=n: s.at(b, n + k) + j * U8, bass.ds(j * U8 + n, 1))

                copy_transposed(1)
                act.wait_ge(route.sem, route.at(b, 7))
                act.activation(soft_e[:], soft[:], ACT.Exp).then_inc(route_exp.sem, 1)
                for e in range(E):
                    for t in range(HT):
                        q = e * HT + t
                        act.wait_ge(hp.sem, hp.at(b, q + 1))
                        if q >= 3:
                            act.wait_ge(hsilu.sem, hsilu.at(b, q - 2))
                        act.activation(th[:, q % 3, :], psW[:, q % 2, :], ACT.Tanh, scale=0.5).then_inc(htanh.sem, 1)

                copy_transposed(2)
                for g in range(HG):
                    act.wait_ge(kp.sem, kp.at(b, g + 1))
                    act.activation(kT[:, g, :], psY[:, g, :], ACT.Identity, bias=bk_sb[:, g:g + 1]).then_inc(k_ready.sem, 1)
                for hd in range(HEADS):
                    for c in range(TC):
                        q = hd * TC + c
                        act.wait_ge(s2.sem, s2.at(b, q + 1))
                        if hd >= 2 and c == 0:
                            act.wait_ge(pv.sem, pv.at(b, hd - 1))
                        act.activation(pT[hd % 2][:, c, :], psW[:, q % 3, :], ACT.Exp).then_inc(pexp.sem, 1)
                copy_transposed(3)
                copy_transposed(4)
                act.wait_ge(gate_mm.sem, gate_mm.at(b, 1))
                act.activation(gate_s[:], psB[:, 0:TC * E].rearrange("p (c e) -> p c e", c=TC), ACT.Tanh,
                               scale=0.5).then_inc(gate_tanh.sem, 1)
                for e in range(E + 1):
                    act.wait_ge(fp.sem, fp.at(b, e + 1))
                    if e >= 3:
                        act.wait_ge(fsilu.sem, fsilu.at(b, e - 2))
                    act.activation(th[:, e % 3, :], psW[:, e % 2, :], ACT.Tanh, scale=0.5).then_inc(ftanh.sem, 1)

        @block.vector
        def _(dve):
            dve.memset(xs[:], 0.0).then_inc(dve_set.sem, 1)
            for i in range(2):
                dve.memset(decay[i][:], 0.0).then_inc(dve_set.sem, 1)
            dve.memset(vA[:], 1.0).then_inc(dve_set.sem, 1)
            dve.memset(neg_max[:], 0.0).then_inc(dve_set.sem, 1)
            dve.memset(cw[:], 1.0).then_inc(dve_set.sem, 1)
            dve.wait_ge(loaded.sem, ALL_LOADED)
            dve.wait_ge(pool_set.sem, POOL_SETS)
            dve.tensor_scalar(conv_wh[:], conv_w_sb[:], 0.5, None, ALU.mult).then_inc(dve_set.sem, 1)
            dve.tensor_scalar(conv_bh[:], conv_b_sb[:], 0.5, None, ALU.mult).then_inc(dve_set.sem, 1)
            for m in range(M3):
                dve.tensor_scalar(diag_d[:, m, :], ident[:], d_skip_sb[:, m:m + 1], None, ALU.mult).then_inc(dve_set.sem, 1)
                dve.tensor_copy(xproj_qr[:, m, :], xproj_q[:, m, :].to_broadcast([P, P])).then_inc(dve_set.sem, 1)
            dve.wait_ge(act_set.sem, 1)
            dve.tensor_scalar(a_neg[:], a_exp[:], -1.0, None, ALU.mult).then_inc(dve_set.sem, 1)
            dve.wait_ge(dve_set.sem, DVE_SETS)

            with dve.Fori(0, NB) as b:
                def layer_norm(l):
                    base = (2 * TC + 2) * l
                    for c in range(TC):
                        dve.bn_stats(stats[:, c, :], h[:, c, :]).then_inc(ln_step.sem, 1)
                    dve.wait_ge(ln_step.sem, ln_step.at(b, base + TC))
                    dve.tensor_copy(stat_count[:], stats[:, TC - 1, 0:1]).then_inc(ln_step.sem, 1)
                    for c in range(TC):
                        dve.bn_aggr(mv[:, c, :], stats[:, c, :]).then_inc(ln_step.sem, 1)
                    dve.wait_ge(ln_step.sem, ln_step.at(b, base + 2 * TC + 1))
                    dve.tensor_scalar(vare[:], mv[:, :, 1], EPS, None, ALU.add).then_inc(ln_step.sem, 1)
                    dve.wait_ge(ln_rstd.sem, ln_rstd.at(b, l + 1))
                    for c in range(TC):
                        dve.tensor_scalar(xn[:, c, :], h[:, c, :], mv[:, c, 0:1], rstd[:, c:c + 1],
                                          ALU.subtract, ALU.mult).then_inc(ln_xn.sem, 1)

                dve.wait_ge(gathered.sem, gathered.at(b, 16 * TC))
                dve.tensor_tensor(h[:], xn[:], pos_sb[:], ALU.add).then_inc(h_ready.sem, 1)
                dve.wait_ge(h_ready.sem, h_ready.at(b, 1))
                layer_norm(0)
                for k in range(TAPS):
                    for m in range(M3):
                        if k == 0:
                            dve.wait_ge(xs_ready.sem, xs_ready.at(b, m + 1))
                            dve.tensor_scalar(xc[:, m, :], xs[:, m, 0:T], conv_wh[:, m, 0:1], conv_bh[:, m:m + 1],
                                              ALU.mult, ALU.add).then_inc(conv.sem, 1)
                        else:
                            dve.wait_ge(conv.sem, conv.at(b, M3 * (k - 1) + m + 1))
                            dve.scalar_tensor_tensor(out=xc[:, m, :], in0=xs[:, m, k:k + T],
                                                     scalar=conv_wh[:, m, k:k + 1], in1=xc[:, m, :],
                                                     op0=ALU.mult, op1=ALU.add).then_inc(conv.sem, 1)
                for m in range(M3):
                    dve.wait_ge(z_tanh.sem, z_tanh.at(b, m + 1))
                    dve.scalar_tensor_tensor(out=gz[:, m, :], in0=drive[0][:, m, :], scalar=1.0, in1=psY[:, m, :],
                                             op0=ALU.add, op1=ALU.mult).then_inc(z_gate.sem, 1)
                for m in range(M3):
                    dve.wait_ge(conv_tanh.sem, conv_tanh.at(b, m + 1))
                    dve.scalar_tensor_tensor(out=xc[:, m, :], in0=drive[1][:, m, :], scalar=1.0, in1=xc[:, m, :],
                                             op0=ALU.add, op1=ALU.mult).then_inc(xc_ready.sem, 1)
                bank = [psW[0:96, 0, :], psW[0:96, 1, :], psW[0:96, 2, :], psB[0:96, :]]
                rest = weighed[1]
                for s in range(SETS):
                    dve.wait_ge(xp.sem, xp.at(b, s + 1))
                    dve.tensor_copy(bc_s[:, s, :], bank[s]).then_inc(split.sem, 1)
                    dve.wait_ge(split.sem, split.at(b, 5 * s + 1))
                    dve.tensor_tensor(rest[0:64, 0, :], bank[s][0:64], bc_s[0:64, s, :], ALU.subtract).then_inc(split.sem, 1)
                    dve.wait_ge(split.sem, split.at(b, 5 * s + 2))
                    dve.tensor_copy(bc_s[0:64, s, :], rest[0:64, 0, :]).then_inc(split.sem, 1)
                    dve.wait_ge(split.sem, split.at(b, 5 * s + 3))
                    dve.tensor_tensor(rest[0:32, 1, :], rest[0:32, 0, :], bc_s[0:32, s, :], ALU.subtract).then_inc(split.sem, 1)
                    dve.wait_ge(split.sem, split.at(b, 5 * s + 4))
                    dve.tensor_copy(bc_s[0:32, s, :], rest[0:32, 1, :]).then_inc(split.sem, 1)
                dve.wait_ge(sp_act.sem, sp_act.at(b, 4 * M3))
                dve.tensor_scalar(weighed[0][:], drive[0][:], 1.0, -1.0, ALU.add, ALU.add).then_inc(dt_step.sem, 1)
                dve.tensor_tensor(dt[:], dt[:], drive[1][:], ALU.add).then_inc(dt_step.sem, 1)
                dve.wait_ge(dt_step.sem, dt_step.at(b, 2))
                dve.tensor_tensor(weighed[0][:], drive[0][:], weighed[0][:], ALU.subtract).then_inc(dt_step.sem, 1)
                dve.wait_ge(dt_step.sem, dt_step.at(b, 3))
                dve.tensor_tensor(dt[:], dt[:], weighed[0][:], ALU.add).then_inc(dt_step.sem, 1)
                dve.wait_ge(dt_step.sem, dt_step.at(b, 4))
                dve.wait_ge(xc_ready.sem, xc_ready.at(b, M3))
                dve.tensor_tensor(u[:], dt[:], xc[:], ALU.mult).then_inc(dt_step.sem, 1)

                def scan_step(n, at):
                    i = n % 2
                    dve.wait_ge(decayed.sem, at(decayed, 1))
                    dve.wait_ge(driven.sem, at(driven, 1))
                    if n >= 1:
                        dve.wait_ge(weighed_s.sem, at(weighed_s, 0))
                    flat = lambda t: t[:].rearrange("p m t -> p (m t)")
                    dve.tensor_tensor_scan(flat(state), flat(decay[i]), flat(drive[i]), 0.0,
                                           ALU.mult, ALU.add).then_inc(scanned.sem, 1)
                    dve.wait_ge(scanned.sem, at(scanned, 1))
                    dve.wait_ge(c_bc.sem, at(c_bc, 1))
                    if n >= 2:
                        dve.wait_ge(summed.sem, at(summed, -1) )
                    dve.tensor_tensor(weighed[i][:], state[:], psC[:].unsqueeze(1).to_broadcast([P, M3, T]),
                                      ALU.mult).then_inc(weighed_s.sem, 1)

                for n in range(U8):
                    scan_step(n, lambda s, k, n=n: s.at(b, n + k))
                with dve.Fori(1, NS // U8) as j:
                    for n in range(U8):
                        scan_step(n + U8, lambda s, k, n=n: s.at(b, n + k) + j * U8)

                dve.wait_ge(summed.sem, summed.at(b, NS + 1))
                dve.scalar_tensor_tensor(out=gz[:], in0=psY[:], scalar=0.5, in1=gz[:],
                                         op0=ALU.mult, op1=ALU.mult).then_inc(gated.sem, 1)
                for c2 in range(2):
                    dve.wait_ge(outp.sem, outp.at(b, c2 + 1))
                    dve.tensor_tensor(h[:, 2 * c2:2 * c2 + 2, :], h[:, 2 * c2:2 * c2 + 2, :],
                                      psW[:, c2, 0:2 * D].rearrange("p (c d) -> p c d", c=2), ALU.add).then_inc(resid1.sem, 1)
                dve.wait_ge(resid1.sem, resid1.at(b, 2))
                layer_norm(1)

                bc_e = lambda t: t[:].unsqueeze(2).to_broadcast([P, TC, E])
                dve.wait_ge(route_mm.sem, route_mm.at(b, 1))
                dve.tensor_tensor(logit[:], psB[:, 0:TC * E].rearrange("p (c e) -> p c e", c=TC),
                                  router_b_sb[:].unsqueeze(1).to_broadcast([P, TC, E]), ALU.add).then_inc(route.sem, 1)
                dve.wait_ge(route.sem, route.at(b, 1))
                dve.tensor_reduce(top[:], logit[:], AX.X, ALU.max).then_inc(route.sem, 1)
                dve.wait_ge(route.sem, route.at(b, 2))
                dve.tensor_tensor(tie[:], logit[:], bc_e(top), ALU.is_equal).then_inc(route.sem, 1)
                dve.wait_ge(route.sem, route.at(b, 3))
                dve.tensor_tensor(rev[:], tie[:], falling[:].unsqueeze(1).to_broadcast([P, TC, E]), ALU.mult).then_inc(route.sem, 1)
                dve.wait_ge(route.sem, route.at(b, 4))
                dve.tensor_reduce(first[:], rev[:], AX.X, ALU.max).then_inc(route.sem, 1)
                dve.wait_ge(route.sem, route.at(b, 5))
                dve.tensor_tensor(chosen[:], rev[:], bc_e(first), ALU.is_equal).then_inc(route.sem, 1)
                dve.tensor_tensor(soft[:], logit[:], bc_e(top), ALU.subtract).then_inc(route.sem, 1)
                dve.wait_ge(route_exp.sem, route_exp.at(b, 1))
                dve.tensor_reduce(soft_s[:], soft_e[:], AX.X, ALU.add).then_inc(route.sem, 1)
                dve.wait_ge(route.sem, route.at(b, 8))
                dve.reciprocal(prob[:], soft_s[:]).then_inc(moe_fin.sem, 1)

                def accumulate(e):
                    dve.wait_ge(eout.sem, eout.at(b, e + 1))
                    for c in range(TC):
                        src = psY[:, 1 + c // 2, (c % 2) * D:(c % 2 + 1) * D]
                        if e == 0:
                            dve.tensor_scalar(moe[:, c, :], src, chosen[:, c, e:e + 1], None, ALU.mult).then_inc(eacc.sem, 1)
                        else:
                            dve.wait_ge(eacc.sem, eacc.at(b, TC * (e - 1) + c + 1))
                            dve.scalar_tensor_tensor(out=moe[:, c, :], in0=src, scalar=chosen[:, c, e:e + 1],
                                                     in1=moe[:, c, :], op0=ALU.mult, op1=ALU.add).then_inc(eacc.sem, 1)

                for e in range(E):
                    for t in range(HT):
                        q = e * HT + t
                        dve.wait_ge(htanh.sem, htanh.at(b, q + 1))
                        if q >= 1:
                            dve.wait_ge(hid_ready.sem, hid_ready.at(b, q))
                        dve.scalar_tensor_tensor(out=sl[:, 0, :], in0=th[:, q % 3, :], scalar=1.0, in1=psW[:, q % 2, :],
                                                 op0=ALU.add, op1=ALU.mult).then_inc(hsilu.sem, 1)
                        dve.wait_ge(hsilu.sem, hsilu.at(b, q + 1))
                        if e >= 2 and t == 0:
                            dve.wait_ge(eout.sem, eout.at(b, e - 1))
                        h2 = psW[:, 2, :] if q % 2 == 0 else psY[:, 0, :]
                        dve.scalar_tensor_tensor(out=hid[e % 2][:, t, :], in0=sl[:, 0, :], scalar=0.5, in1=h2,
                                                 op0=ALU.mult, op1=ALU.mult).then_inc(hid_ready.sem, 1)
                    if e >= 1:
                        accumulate(e - 1)
                accumulate(E - 1)
                dve.wait_ge(eacc.sem, eacc.at(b, E * TC))
                dve.tensor_copy(moe_b, moe).then_inc(moe_fin.sem, 1)
                dve.wait_ge(moe_fin.sem, moe_fin.at(b, 2))
                for c in range(TC):
                    dve.scalar_tensor_tensor(out=h[:, c, :], in0=moe_b[:, c, :], scalar=prob[:, c:c + 1], in1=h[:, c, :],
                                             op0=ALU.mult, op1=ALU.add).then_inc(resid2.sem, 1)
                dve.wait_ge(resid2.sem, resid2.at(b, TC))
                layer_norm(2)

                for g in range(HG):
                    dve.wait_ge(qp.sem, qp.at(b, g + 1))
                    dve.tensor_scalar(qT[:, g, :], psW[:, g, :], bq_sb[:, g:g + 1], HD ** -0.5,
                                      ALU.add, ALU.mult).then_inc(q_ready.sem, 1)
                for c in range(TC):
                    if c % 2 == 0:
                        dve.wait_ge(vp.sem, vp.at(b, c // 2 + 1))
                    src = (psB, psC)[c // 2][:, (c % 2) * D:(c % 2 + 1) * D]
                    dve.tensor_tensor(vA[:, c, :, 0:HD], src.rearrange("p (h d) -> p h d", d=HD),
                                      bv_sb[:].rearrange("p (h d) -> p h d", d=HD), ALU.add).then_inc(v_ready.sem, 1)
                for hd in range(HEADS):
                    for c in range(TC):
                        q = hd * TC + c
                        col = 32 * (hd % 4) + HD
                        dve.wait_ge(s1.sem, s1.at(b, q + 1))
                        dve.tensor_reduce(neg_max[:, c, hd // 4, col:col + 1], psW[:, q % 3, :], AX.X, ALU.max,
                                          negate=True).then_inc(mx.sem, 1)
                for g in range(HG):
                    dve.wait_ge(mx_tr.sem, mx_tr.at(b, g + 1))
                    dve.tensor_tensor(qa[:, g, :], qT[:, g, :], psY[:, g, :], ALU.add).then_inc(qa_ready.sem, 1)
                dve.wait_ge(pv.sem, pv.at(b, HEADS))
                for c2 in range(2):
                    o = (psB, psC)[c2][:, 0:2 * HEADS * (HD + 1)].rearrange("p (c h d) -> p c h d", c=2, h=HEADS)
                    dve.reciprocal(r_sum[:, 2 * c2:2 * c2 + 2, :], o[:, :, :, HD]).then_inc(a_norm.sem, 1)
                    dve.wait_ge(a_norm.sem, a_norm.at(b, 3 * c2 + 1))
                    for c in range(2):
                        dve.tensor_tensor(oa[:, 2 * c2 + c, :].rearrange("p (h d) -> p h d", d=HD), o[:, c, :, 0:HD],
                                          r_sum[:, 2 * c2 + c, :].unsqueeze(2).to_broadcast([P, HEADS, HD]),
                                          ALU.mult).then_inc(a_norm.sem, 1)
                dve.tensor_tensor(h[:], h[:], bo_sb[:].unsqueeze(1).to_broadcast([P, TC, D]), ALU.add).then_inc(resid3.sem, 1)
                dve.wait_ge(resid3.sem, resid3.at(b, 1))
                for c2 in range(2):
                    dve.wait_ge(ao.sem, ao.at(b, c2 + 1))
                    dve.tensor_tensor(h[:, 2 * c2:2 * c2 + 2, :], h[:, 2 * c2:2 * c2 + 2, :],
                                      psY[:, c2, 0:2 * D].rearrange("p (c d) -> p c d", c=2), ALU.add).then_inc(resid3.sem, 1)
                dve.wait_ge(resid3.sem, resid3.at(b, 3))
                layer_norm(3)

                step = [0]

                def gate_step(ins):
                    step[0] += 1
                    ins.then_inc(gate.sem, 1)
                    dve.wait_ge(gate.sem, gate.at(b, step[0]))

                def best_two(v, n, on):
                    vi = v.unsqueeze(3).to_broadcast([P, TC, n, n])
                    vj = v.unsqueeze(2).to_broadcast([P, TC, n, n])
                    gt, eq = cmp_gt[:, :, 0:n, 0:n], cmp_eq[:, :, 0:n, 0:n]
                    dve.tensor_tensor(gt, vj, vi, ALU.is_gt).then_inc(gate.sem, 1)
                    step[0] += 1
                    gate_step(dve.tensor_tensor(eq, vj, vi, ALU.is_equal))
                    gate_step(dve.tensor_tensor(eq, eq, before[:, 0:n, 0:n].unsqueeze(1).to_broadcast([P, TC, n, n]), ALU.mult))
                    gate_step(dve.tensor_tensor(gt, gt, eq, ALU.add))
                    gate_step(dve.tensor_reduce(rank[:, :, 0:n], gt, AX.X, ALU.add))
                    gate_step(dve.tensor_scalar(on, rank[:, :, 0:n], 2.0, None, ALU.is_lt))

                dve.wait_ge(gate_tanh.sem, gate_tanh.at(b, 1))
                gate_step(dve.tensor_scalar(gate_s[:], gate_s[:], 0.5, 0.5, ALU.mult, ALU.add))
                gate_step(dve.tensor_tensor(gate_v[:], gate_s[:], gate_b_sb[:].unsqueeze(1).to_broadcast([P, TC, E]), ALU.add))
                gate_step(dve.tensor_tensor(group_v[:], gate_v[:, :, 0::2], gate_v[:, :, 1::2], ALU.add))
                best_two(group_v[:], 4, group_on[:])
                pair = lambda t: t[:].rearrange("p c (g e) -> p c g e", e=2)
                on4 = group_on[:].unsqueeze(3).to_broadcast([P, TC, 4, 2])
                gate_step(dve.tensor_tensor(pair(masked), pair(gate_v), on4, ALU.mult))
                gate_step(dve.tensor_scalar(group_v[:], group_on[:], -1.0, 1e30, ALU.add, ALU.mult))
                gate_step(dve.tensor_tensor(pair(masked), pair(masked),
                                            group_v[:].unsqueeze(3).to_broadcast([P, TC, 4, 2]), ALU.add))
                best_two(masked[:], E, cw[:, :, 0:E])
                gate_step(dve.tensor_tensor(cw[:, :, 0:E], cw[:, :, 0:E], gate_s[:], ALU.mult))
                gate_step(dve.tensor_reduce(top[:], cw[:, :, 0:E], AX.X, ALU.add))
                gate_step(dve.tensor_scalar(top[:], top[:], 1e-6, None, ALU.add))
                gate_step(dve.reciprocal(first[:], top[:]))
                gate_step(dve.tensor_tensor(cw[:, :, 0:E], cw[:, :, 0:E], bc_e(first), ALU.mult))
                assert step[0] == gate.per, step[0]

                def accumulate2(e):
                    dve.wait_ge(fout.sem, fout.at(b, e + 1))
                    for c in range(TC):
                        src = psY[:, 1 + c // 2, (c % 2) * D:(c % 2 + 1) * D]
                        if e >= 1:
                            dve.wait_ge(facc.sem, facc.at(b, TC * (e - 1) + c + 1))
                        dve.scalar_tensor_tensor(out=h[:, c, :], in0=src, scalar=cw[:, c, e:e + 1],
                                                 in1=h[:, c, :], op0=ALU.mult, op1=ALU.add).then_inc(facc.sem, 1)

                for e in range(E + 1):
                    dve.wait_ge(ftanh.sem, ftanh.at(b, e + 1))
                    if e >= 1:
                        dve.wait_ge(fhid.sem, fhid.at(b, e))
                    dve.scalar_tensor_tensor(out=sl[:, 0, :], in0=th[:, e % 3, :], scalar=1.0, in1=psW[:, e % 2, :],
                                             op0=ALU.add, op1=ALU.mult).then_inc(fsilu.sem, 1)
                    dve.wait_ge(fsilu.sem, fsilu.at(b, e + 1))
                    if e >= 2:
                        dve.wait_ge(fout.sem, fout.at(b, e - 1))
                    h2 = psW[:, 2, :] if e % 2 == 0 else psY[:, 0, :]
                    dve.scalar_tensor_tensor(out=hid[e % 2][:, 0, :], in0=sl[:, 0, :], scalar=0.5, in1=h2,
                                             op0=ALU.mult, op1=ALU.mult).then_inc(fhid.sem, 1)
                    if e >= 1:
                        accumulate2(e - 1)
                accumulate2(E)
                dve.wait_ge(facc.sem, facc.at(b, (E + 1) * TC))

        @block.tensor
        def _(pe):
            pe.wait_ge(loaded.sem, ALL_LOADED)
            pe.wait_ge(pool_set.sem, POOL_SETS)
            pe.wait_ge(dve_set.sem, DVE_SETS)

            with pe.Fori(0, NB) as b:
                def transposes():
                    for k in range(KT):
                        for c in range(TC):
                            mm = pe.transpose(psW[0:KP, k, c * P:(c + 1) * P], xn[:, c, k * KP:(k + 1) * KP], ident[:])
                        mm.then_inc(tr.sem, 1)

                def transpose_norm(l):
                    pe.wait_ge(ln_xn.sem, ln_xn.at(b, TC * (l + 1)))
                    transposes()

                transpose_norm(0)
                pe.wait_ge(xnT_ready.sem, xnT_ready.at(b, KT))
                for m in range(2 * M3):
                    dst = psW[:, m, :] if m < M3 else psY[:, m - M3, :]
                    for k in range(KT):
                        mm = pe.matmul(dst, in_w_sb[:, k, m * P:(m + 1) * P], xnT[:, k, :], start=(k == 0), stop=(k == KT - 1))
                    mm.then_inc(proj.sem, 1)
                pe.wait_ge(xc_ready.sem, xc_ready.at(b, M3))
                for s in range(SETS + 1):
                    if s < SETS:
                        dst, w = (psW[0:96, s, :] if s < 3 else psB[0:96, :]), xproj_bc[:, :, s, :]
                    else:
                        dst, w = psC[:], xproj_qr[:]
                    for m in range(M3):
                        mm = pe.matmul(dst, w[:, m, :], xc[:, m, :], start=(m == 0), stop=(m == M3 - 1))
                    mm.then_inc(xp.sem, 1)

                def broadcast_b(n, at, half, row):
                    if n >= 1:
                        pe.wait_ge(b_copied.sem, at(b_copied, 0))
                    pe.matmul(psB[:], onehot[:, row, :], bc_s[:, half, :], start=True, stop=True).then_inc(b_bc.sem, 1)

                def broadcast_c(n, at, half, row):
                    if n >= 1:
                        pe.wait_ge(weighed_s.sem, at(weighed_s, 0))
                    pe.matmul(psC[:], onehot[:, row, :], bc_s[:, 2 + half, :], start=True, stop=True).then_inc(c_bc.sem, 1)

                def add_state(n, at):
                    i = n % 2
                    pe.wait_ge(weighed_s.sem, at(weighed_s, 1))
                    for m in range(M3):
                        mm = pe.matmul(psY[:, m, :], ident[:], weighed[i][:, m, :], start=(n == 0), stop=False,
                                       skip_group_check=True)
                    mm.then_inc(summed.sem, 1)

                pe.wait_ge(split.sem, split.at(b, 5 * SETS))
                pe.wait_ge(sp_act.sem, sp_act.at(b, 2 * M3))
                pe.wait_ge(z_gate.sem, z_gate.at(b, M3))
                for n in range(NS):
                    at = lambda s, k, n=n: s.at(b, n + k)
                    broadcast_b(n, at, n // 32, n % 32)
                    broadcast_c(n, at, n // 32, n % 32)
                    if n >= 1:
                        add_state(n - 1, lambda s, k, n=n: s.at(b, n - 1 + k))
                add_state(NS - 1, lambda s, k: s.at(b, NS - 1 + k))
                for m in range(M3):
                    mm = pe.matmul(psY[:, m, :], diag_d[:, m, :], xc[:, m, :], start=False, stop=True, skip_group_check=True)
                mm.then_inc(summed.sem, 1)
                pe.wait_ge(gated.sem, gated.at(b, 1))
                for c in range(TC):
                    for m in range(M3):
                        mm = pe.matmul(psW[:, c // 2, (c % 2) * D:(c % 2 + 1) * D], gz[:, m, c * P:(c + 1) * P],
                                       out_w_sb[:, m, :], start=(m == 0), stop=(m == M3 - 1))
                    if c % 2:
                        mm.then_inc(outp.sem, 1)

                transpose_norm(1)
                pe.wait_ge(xnT_ready.sem, xnT_ready.at(b, 2 * KT))

                def logits(w, done):
                    for c in range(TC):
                        for k in range(KT):
                            mm = pe.matmul(psB[:, c * E:(c + 1) * E], xnT[:, k, c * P:(c + 1) * P], w[:, k, :],
                                           start=(k == 0), stop=(k == KT - 1))
                    mm.then_inc(done, 1)

                logits(router_w_sb, route_mm.sem)

                def expert_out(e):
                    pe.wait_ge(hid_ready.sem, hid_ready.at(b, HT * (e + 1)))
                    if e >= 1:
                        pe.wait_ge(eacc.sem, eacc.at(b, TC * e))
                    for c in range(TC):
                        for t in range(HT):
                            mm = pe.matmul(psY[:, 1 + c // 2, (c % 2) * D:(c % 2 + 1) * D],
                                           hid[e % 2][:, t, c * P:(c + 1) * P], w3_sb[e % 2][:, t, :],
                                           start=(t == 0), stop=(t == HT - 1))
                    mm.then_inc(eout.sem, 1)

                for e in range(E):
                    pe.wait_ge(wload[e % 2].sem, wload[e % 2].at(b, 48 * (e // 2 + 1)))
                    for t in range(HT):
                        q = e * HT + t
                        if q >= 2:
                            pe.wait_ge(hid_ready.sem, hid_ready.at(b, q - 1))
                        h2 = psW[:, 2, :] if q % 2 == 0 else psY[:, 0, :]
                        for w, dst in ((w1_sb, psW[:, q % 2, :]), (w2_sb, h2)):
                            for k in range(KT):
                                mm = pe.matmul(dst, w[e % 2][:, k, t * P:(t + 1) * P], xnT[:, k, :],
                                               start=(k == 0), stop=(k == KT - 1))
                        mm.then_inc(hp.sem, 1)
                        if t == 1 and e >= 1:
                            expert_out(e - 1)
                expert_out(E - 1)

                transpose_norm(2)
                pe.wait_ge(xnT_ready.sem, xnT_ready.at(b, 3 * KT))
                pe.wait_ge(eacc.sem, eacc.at(b, E * TC))
                for w, dst, done in ((wk_sb, psY, kp), (wq_sb, psW, qp)):
                    for g in range(HG):
                        for k in range(KT):
                            mm = pe.matmul(dst[:, g, :], w[:, k, g * P:(g + 1) * P], xnT[:, k, :],
                                           start=(k == 0), stop=(k == KT - 1))
                        mm.then_inc(done.sem, 1)
                for c in range(TC):
                    for k in range(KT):
                        mm = pe.matmul((psB, psC)[c // 2][:, (c % 2) * D:(c % 2 + 1) * D], xnT[:, k, c * P:(c + 1) * P],
                                       wv_sb[:, k, :], start=(k == 0), stop=(k == KT - 1))
                    if c % 2:
                        mm.then_inc(vp.sem, 1)
                pe.wait_ge(q_ready.sem, q_ready.at(b, HG))
                pe.wait_ge(k_ready.sem, k_ready.at(b, HG))
                for hd in range(HEADS):
                    r = 32 * (hd % 4)
                    for c in range(TC):
                        q = hd * TC + c
                        if q >= 3:
                            pe.wait_ge(mx.sem, mx.at(b, q - 2))
                        pe.matmul(psW[:, q % 3, :], qT[r:r + 32, hd // 4, c * P:(c + 1) * P], kT[r:r + 32, hd // 4, :],
                                  start=True, stop=True).then_inc(s1.sem, 1)
                pe.wait_ge(mx.sem, mx.at(b, HEADS * TC))
                for g in range(HG):
                    for c in range(TC):
                        mm = pe.transpose(psY[:, g, c * P:(c + 1) * P], neg_max[:, c, g, :], ident[:])
                    mm.then_inc(mx_tr.sem, 1)
                pe.wait_ge(v_ready.sem, v_ready.at(b, TC))

                def weighted_values(hd):
                    pe.wait_ge(pexp.sem, pexp.at(b, TC * (hd + 1)))
                    for qc in range(TC):
                        at0 = (qc % 2) * HEADS * (HD + 1) + hd * (HD + 1)
                        for kc in range(TC):
                            mm = pe.matmul((psB, psC)[qc // 2][:, at0:at0 + HD + 1], pT[hd % 2][:, kc, qc * P:(qc + 1) * P],
                                           vA[:, kc, hd, :], start=(kc == 0), stop=(kc == TC - 1))
                    mm.then_inc(pv.sem, 1)

                for hd in range(HEADS):
                    r = 32 * (hd % 4)
                    pe.wait_ge(qa_ready.sem, qa_ready.at(b, hd // 4 + 1))
                    for c in range(TC):
                        q = hd * TC + c
                        if q >= 3:
                            pe.wait_ge(pexp.sem, pexp.at(b, q - 2))
                        pe.matmul(psW[:, q % 3, :], kT[r:r + 32, hd // 4, c * P:(c + 1) * P], qa[r:r + 32, hd // 4, :],
                                  start=True, stop=True).then_inc(s2.sem, 1)
                    if hd >= 1:
                        weighted_values(hd - 1)
                weighted_values(HEADS - 1)
                pe.wait_ge(a_norm.sem, a_norm.at(b, 6))
                transposes()
                pe.wait_ge(xnT_ready.sem, xnT_ready.at(b, 4 * KT))
                for c in range(TC):
                    for k in range(KT):
                        mm = pe.matmul(psY[:, c // 2, (c % 2) * D:(c % 2 + 1) * D], xnT[:, k, c * P:(c + 1) * P],
                                       wo_sb[:, k, :], start=(k == 0), stop=(k == KT - 1))
                    if c % 2:
                        mm.then_inc(ao.sem, 1)

                transpose_norm(3)
                pe.wait_ge(xnT_ready.sem, xnT_ready.at(b, 5 * KT))
                logits(gate_w_sb, gate_mm.sem)

                def expert_out2(e):
                    pe.wait_ge(fhid.sem, fhid.at(b, e + 1))
                    if e >= 1:
                        pe.wait_ge(facc.sem, facc.at(b, TC * e))
                    for c in range(TC):
                        mm = pe.matmul(psY[:, 1 + c // 2, (c % 2) * D:(c % 2 + 1) * D],
                                       hid[e % 2][:, 0, c * P:(c + 1) * P], f2_sb[:, e, :], start=True, stop=True)
                    mm.then_inc(fout.sem, 1)

                for e in range(E + 1):
                    if e >= 2:
                        pe.wait_ge(fhid.sem, fhid.at(b, e - 1))
                    h2 = psW[:, 2, :] if e % 2 == 0 else psY[:, 0, :]
                    for w, dst in ((f1_sb, psW[:, e % 2, :]), (f3_sb, h2)):
                        for k in range(KT):
                            mm = pe.matmul(dst, w[:, k, e, :], xnT[:, k, :], start=(k == 0), stop=(k == KT - 1))
                    mm.then_inc(fp.sem, 1)
                    if e >= 1:
                        expert_out2(e - 1)
                expert_out2(E)


def kernel(x, L0_tok_W_emb, L0_tok_W_pos, L0_attn_in_w, L0_attn_conv_w, L0_attn_conv_b, L0_attn_xproj_w,
           L0_attn_A_log, L0_attn_dt_bias, L0_attn_D, L0_attn_out_w, L0_ffn_router_w, L0_ffn_router_b,
           L0_ffn_w1, L0_ffn_w2, L0_ffn_w3, L1_attn_W_qkv, L1_attn_b_qkv, L1_attn_W_out, L1_attn_b_out,
           L1_ffn_gate_weight, L1_ffn_gate_bias, L1_ffn_w1, L1_ffn_w2, L1_ffn_w3,
           L1_ffn_sw1, L1_ffn_sw2, L1_ffn_sw3):
    import concourse.bacc as bacc
    from concourse.bass_utils import run_bass_kernel_spmd

    def slots(a):
        wide = np.zeros(a.shape[:-1] + (HEADS, 32), a.dtype)
        wide[..., 0:HD] = np.asarray(a).reshape(a.shape[:-1] + (HEADS, HD))
        return wide.reshape(a.shape[:-1] + (HEADS * 32,))

    W, bias = np.asarray(L1_attn_W_qkv), np.asarray(L1_attn_b_qkv)
    bk = slots(bias[D:2 * D])
    bk.reshape(HEADS, 32)[:, HD] = 1.0
    by_tile = lambda v: np.asarray(v).reshape(-1, P).T
    ffn = lambda w, s: np.concatenate([np.asarray(w), np.asarray(s)[None]], 0).transpose(0, 2, 1)
    arrays = {
        "tok": np.asarray(x).reshape(NB * TC, P).T,
        "emb": np.asarray(L0_tok_W_emb).T,
        "pos": L0_tok_W_pos, "in_w": L0_attn_in_w, "conv_w": np.asarray(L0_attn_conv_w).reshape(DI, TAPS),
        "conv_b": by_tile(L0_attn_conv_b), "xproj_w": L0_attn_xproj_w,
        "xproj_dt": by_tile(np.asarray(L0_attn_xproj_w)[:, 2 * NS]), "a_log": L0_attn_A_log,
        "dt_bias": by_tile(L0_attn_dt_bias), "d_skip": by_tile(L0_attn_D), "out_w": L0_attn_out_w,
        "router_w": L0_ffn_router_w, "router_b": L0_ffn_router_b,
        "w1": L0_ffn_w1, "w2": L0_ffn_w2, "w3": L0_ffn_w3,
        "wq": slots(W[:, 0:D]), "wk": slots(W[:, D:2 * D]), "wv": W[:, 2 * D:],
        "bq": by_tile(slots(bias[0:D])), "bk": by_tile(bk), "bv": bias[2 * D:],
        "wo": L1_attn_W_out, "bo": L1_attn_b_out,
        "gate_w": np.asarray(L1_ffn_gate_weight).T, "gate_b": L1_ffn_gate_bias,
        "f1": ffn(L1_ffn_w1, L1_ffn_sw1), "f3": ffn(L1_ffn_w3, L1_ffn_sw3), "f2": ffn(L1_ffn_w2, L1_ffn_sw2),
    }
    arrays = {k: np.ascontiguousarray(a) for k, a in arrays.items()}
    nc = bacc.Bacc("TRN2", target_bir_lowering=False, num_devices=1)
    args = [nc.dram_tensor(k, a.shape, mybir.dt.from_np(a.dtype), kind="ExternalInput").ap()
            for k, a in arrays.items()]
    out = nc.dram_tensor("y", (NB, T, D), F32, kind="ExternalOutput").ap()
    tower(nc, *args, out)
    r = run_bass_kernel_spmd(nc, [arrays], core_ids=[0])
    return r.results[0]["y"]
```

```python
from contextlib import ExitStack

import numpy as np

import concourse.bass as bass
from concourse import mybir

F32 = mybir.dt.float32
BF16 = mybir.dt.bfloat16
I32 = mybir.dt.int32
U32 = mybir.dt.uint32
ALU = mybir.AluOpType
ACT = mybir.ActivationFunctionType
AX = mybir.AxisListType

P = 128
NB = 16
T = 512
TC = T // P
D = 192
KP, KT = 96, 2
DI = 384
M3 = DI // P
NS = 64
TAPS = 4
SETS = 4
E = 8
HID = 512
HT = HID // P
ROWS = NB * T + P
NT = NB * TC + E
INTER = 128
HEADS, HD = 12, 16
HG = 3
HK = 6
EPS = 1e-5
U8 = 8


LAST = NB


class Signal:

    def __init__(self, sem, per):
        self.sem, self.per = sem, per

    def at(self, b, n):
        return b * self.per + n


def in_register(eng, value):
    return value if isinstance(value, int) else eng.to_reg(value)


PRODUCTS = ((0, 0), (0, 1), (1, 0), (1, 1), (0, 2), (2, 0))


def tower(nc, tok, emb, pos, in_w, conv_w, conv_b, xproj_w, xproj_dt, a_log, dt_bias, d_skip, out_w,
          router_w, router_b, w1, w2, w3, wq, wk, wv, bq, bk, bv, wo, bo,
          gate_w, gate_b, f1, f3, f2, out):
    ctx = ExitStack()
    with ctx:
        def alloc(scope):
            return lambda name, shape, dt=F32: scope.enter_context(nc.sbuf_tensor(name, shape, dt))

        def ps(name, shape, dt=F32):
            return ctx.enter_context(nc.psum_tensor(name, shape, dt))

        def sig(name, per):
            return Signal(ctx.enter_context(nc.semaphore(name)), per)

        h_dram = nc.dram_tensor("h_dram", (NB + 1, T, D), F32, kind="Internal").ap()
        x_sorted = nc.dram_tensor("x_sorted", (E * ROWS + P, D + 1), F32, kind="Internal").ap()
        y_tok = nc.dram_tensor("y_tok", (NB + 1, T, D), F32, kind="Internal").ap()

        y_rows = y_tok.rearrange("b t d -> (b t) d")
        parts_dram = nc.dram_tensor("parts_dram", (2, 3, D, T), BF16, kind="Internal").ap()
        nm_dram = nc.dram_tensor("nm_dram", (3 * HEADS, T), BF16, kind="Internal").ap()

        sb = alloc(ctx)
        ident = sb("ident", [P, P])
        neg_half = sb("neg_half", [P, TC])
        blank = sb("blank", [P, D + 1])
        prob_all = sb("prob_all", [P, NB * TC])
        count = sb("count", [P, E])
        before = sb("before", [P, E, E])
        table_r = sb("table_r", [1, NT], I32)
        table_e = sb("table_e", [1, NT], I32)
        tail = sb("tail", [1, E], I32)
        no_number = sb("no_number", [P, 1], I32)
        h = sb("h", [P, TC, D])
        stats = sb("stats", [P, TC, 6])
        stat_count = sb("stat_count", [P, 1])
        mv = sb("mv", [P, TC, 2])
        vare = sb("vare", [P, TC])
        rstd = sb("rstd", [P, TC])
        xn = sb("xn", [P, TC, D])
        xnT = sb("xnT", [KP, KT, T])
        w2_sb = sb("w2_sb", [KP, KT, E * HID])
        w3_sb = sb("w3_sb", [P, HT, E * D])

        scope1 = ExitStack()
        sb = alloc(scope1)
        onehot = sb("onehot", [96, 32, P], BF16)
        tri = sb("tri", [P, P], BF16)
        ones = sb("ones", [P, P], BF16)
        idx_all = sb("idx_all", [P, (NB + 1) * TC], I32)
        pos_sb = sb("pos_sb", [P, TC, D])
        in_w_sb = sb("in_w_sb", [KP, KT, 2 * DI])
        conv_w_sb = sb("conv_w_sb", [P, M3, TAPS])
        conv_b_sb = sb("conv_b_sb", [P, M3])
        conv_wh = sb("conv_wh", [P, M3, TAPS])
        conv_bh = sb("conv_bh", [P, M3])
        xproj_bc = sb("xproj_bc", [P, M3, SETS, 96])
        xproj_q = sb("xproj_q", [P, M3, 1])
        xproj_qr = sb("xproj_qr", [P, M3, P])
        a_log_sb = sb("a_log_sb", [P, M3, NS])
        a_exp = sb("a_exp", [P, M3, NS])
        a_neg = sb("a_neg", [P, M3, NS])
        dt_bias_sb = sb("dt_bias_sb", [P, M3])
        d_skip_sb = sb("d_skip_sb", [P, M3])
        diag_d = sb("diag_d", [P, M3, P])
        out_w_sb = sb("out_w_sb", [P, M3, D])
        router_w_sb = sb("router_w_sb", [KP, KT, E])
        router_b_sb = sb("router_b_sb", [P, E])
        falling_i = sb("falling_i", [P, E], I32)
        falling = sb("falling", [P, E])
        idx = sb("idx", [P, TC], I32)
        rows_in = sb("rows_in", [P, TC, D])
        xr = sb("xr", [P, TC, D + 1])
        token = sb("token", [P, TC])
        token_i = sb("token_i", [P, TC], I32)
        xs = sb("xs", [P, M3, TAPS - 1 + T])
        xc = sb("xc", [P, M3, T])
        gz = sb("gz", [P, M3, T])
        dt = sb("dt", [P, M3, T])
        u = sb("u", [P, M3, T])
        bc_s = sb("bc_s", [96, SETS, T], BF16)
        decay = [sb(f"decay{i}", [P, M3, T]) for i in range(2)]
        drive = [sb(f"drive{i}", [P, M3, T]) for i in range(2)]
        state = sb("state", [P, M3, T])
        weighed = [sb(f"weighed{i}", [P, M3, T]) for i in range(2)]
        b_sb = [sb(f"b_sb{i}", [P, T]) for i in range(2)]
        logit = sb("logit", [P, TC, E])
        top = sb("top", [P, TC])
        tie = sb("tie", [P, TC, E])
        rev = sb("rev", [P, TC, E])
        first = sb("first", [P, TC])
        chosen = sb("chosen", [P, TC, E])
        chosen_b = sb("chosen_b", [P, TC, E], BF16)
        soft = sb("soft", [P, TC, E])
        soft_e = sb("soft_e", [P, TC, E])
        soft_s = sb("soft_s", [P, TC])
        ahead = sb("ahead", [P, TC, E])
        place = sb("place", [P, TC])
        region = sb("region", [P, TC])
        slot = sb("slot", [P, TC], I32)
        flat = lambda t: t[:].rearrange("p m t -> p (m t)")
        wide = lambda t, o=0: flat(t)[:, o:o + NT * E].rearrange("p (s e) -> p s e", e=E)
        t_full, t_begin, t_end = b_sb[0][:, 0:E], b_sb[0][:, E:2 * E], b_sb[0][:, 2 * E:3 * E]
        t_off, t_tail = b_sb[0][:, 3 * E:4 * E], b_sb[0][:, 4 * E:5 * E]
        t_pre = b_sb[0][:, 64:128].rearrange("p (i j) -> p i j", i=E)
        t_regions = b_sb[0][:, 128:136]
        t_row, t_exp, t_valid = b_sb[0][:, 192:192 + NT], b_sb[0][:, 288:288 + NT], b_sb[0][:, 384:384 + NT]
        t_num_i = u[:, 0, 0:NT].bitcast(I32)
        t_num = u[:, 1, 0:NT]
        t_cmp, t_a, t_b = wide(state), wide(drive[0]), wide(drive[1])
        scope1.close()

        scope3 = ctx.enter_context(ExitStack())
        sb = alloc(scope3)
        wq_sb = sb("wq_sb", [KP, KT, D])
        wk_sb = sb("wk_sb", [KP, KT, D])
        wv_sb = sb("wv_sb", [KP, KT, D])
        bqk_sb = sb("bqk_sb", [KP, 2, KT])
        bv_sb = sb("bv_sb", [P, D])
        wo_sb = sb("wo_sb", [KP, KT, D])
        bo_sb = sb("bo_sb", [P, D])
        gate_w_sb = sb("gate_w_sb", [KP, KT, E])
        gate_b_sb = sb("gate_b_sb", [P, E])
        f1_sb = sb("f1_sb", [KP, KT, E + 1, INTER])
        f3_sb = sb("f3_sb", [KP, KT, E + 1, INTER])
        f2_sb = sb("f2_sb", [INTER, E + 1, D])

        scope2 = ExitStack()
        sb = alloc(scope2)
        w1_sb = sb("w1_sb", [KP, KT, E * HID])
        xt_in = [sb(f"xt_in{i}", [P, D + 1]) for i in range(2)]
        xt_num = [sb(f"xt_num{i}", [P, 1], I32) for i in range(2)]
        xt_T = [sb(f"xt_T{i}", [KP, KT * P]) for i in range(2)]
        xt_th = [sb(f"xt_th{i}", [P, HID]) for i in range(2)]
        xt_sl = sb("xt_sl", [P, HID])
        xt_hid = [sb(f"xt_hid{i}", [P, HID]) for i in range(2)]
        xt_hT = [sb(f"xt_hT{i}", [P, HT * P]) for i in range(2)]
        xt_y = [sb(f"xt_y{i}", [P, D]) for i in range(2)]
        scope2.close()

        sb = alloc(scope3)
        h_in = sb("h_in", [P, TC, D])
        y_in = sb("y_in", [P, TC, D])
        prob_cur = sb("prob_cur", [P, TC])
        y_b = sb("y_b", [P, TC, D], BF16)
        parts = sb("parts", [KP, 3, KT, T], BF16)
        qs = sb("qs", [99, HEADS, T], BF16)
        ks = sb("ks", [99, HEADS, T], BF16)
        vA = sb("vA", [P, TC, HEADS, 32])
        pT = [sb(f"pT{i}", [P, TC, T]) for i in range(2)]
        qk_f = pT[0][0:KP, 0:KT, :]
        qk_r = pT[1][0:KP, 0:KT, :]
        neg_max = sb("neg_max", [P, TC, HEADS])
        nm_r = sb("nm_r", [P, TC, HEADS])
        nm_p = sb("nm_p", [P, TC, 3, HEADS], BF16)
        nm_T = sb("nm_T", [3 * HEADS, T], BF16)
        identb = sb("identb", [P, P], BF16)
        og = sb("og", [P, HG, T])
        r_sum = sb("r_sum", [P, TC, HEADS])
        cw = sb("cw", [P, TC, E + 1])
        gate_s = sb("gate_s", [P, TC, E])
        gate_v = sb("gate_v", [P, TC, E])
        group_v = sb("group_v", [P, TC, 4])
        group_on = sb("group_on", [P, TC, 4])
        masked = sb("masked", [P, TC, E])
        cmp_gt = sb("cmp_gt", [P, TC, E, E])
        cmp_eq = sb("cmp_eq", [P, TC, E, E])
        rank = sb("rank", [P, TC, E])
        w_sum = sb("w_sum", [P, TC])
        w_inv = sb("w_inv", [P, TC])
        th = sb("th", [P, 3, T])
        sl = sb("sl", [P, T])
        hid = [sb(f"hid{i}", [P, T]) for i in range(2)]

        psY = ps("psY", [P, M3, T])
        psW = ps("psW", [P, 3, T])
        psB = ps("psB", [P, T])
        psC = ps("psC", [P, T])

        loaded = sig("loaded", 0)
        loaded2 = sig("loaded2", 0)
        loaded3 = sig("loaded3", 0)
        filled = sig("filled", 0)
        pool_set = sig("pool_set", 0)
        dve_set = sig("dve_set", 0)
        dve_set3 = sig("dve_set3", 0)
        act_set = sig("act_set", 0)

        class Norm:

            def __init__(self, name, calls):
                self.step = sig(name + "_step", 2 * (2 * TC + 2))
                self.rstd = sig(name + "_rstd", 2)
                self.xn = sig(name + "_xn", 2 * TC)
                self.tr = sig(name + "_tr", calls * KT)
                self.T = sig(name + "_T", calls * KT)

        n1, n3 = Norm("n1", 2), Norm("n3", 3)
        idx_ready = sig("idx_ready", 1)
        gathered = sig("gathered", 16 * TC)
        h_ready = sig("h_ready", 1)
        proj = sig("proj", 2 * M3)
        xs_ready = sig("xs_ready", M3)
        z_tanh = sig("z_tanh", M3)
        z_gate = sig("z_gate", M3)
        conv = sig("conv", M3 * TAPS)
        conv_tanh = sig("conv_tanh", M3)
        xc_ready = sig("xc_ready", M3)
        xp = sig("xp", SETS + 1)
        split = sig("split", SETS * 5)
        sp_act = sig("sp_act", 4 * M3)
        dt_step = sig("dt_step", 5)
        b_bc = sig("b_bc", NS)
        b_copied = sig("b_copied", NS)
        c_bc = sig("c_bc", NS)
        decayed = sig("decayed", NS)
        driven = sig("driven", NS)
        scanned = sig("scanned", NS)
        weighed_s = sig("weighed_s", NS)
        summed = sig("summed", NS + 1)
        gated = sig("gated", 1)
        outp = sig("outp", 2)
        resid1 = sig("resid1", 2)
        route_mm = sig("route_mm", 1)
        route = sig("route", 16)
        route_exp = sig("route_exp", 1)
        ranked = sig("ranked", 1)
        numbered = sig("numbered", 2)
        h_free = sig("h_free", 1)
        h_free3 = sig("h_free3", 1)
        h_saved = sig("h_saved", 16)
        x_saved = sig("x_saved", 16 * TC)
        tab = sig("tab", 0)
        xt_loaded = [sig(f"xt_loaded{i}", 16) for i in range(2)]
        xt_tr = sig("xt_tr", 1)
        xt_c = sig("xt_c", 1)
        xt_hp = sig("xt_hp", 1)
        xt_tanh = sig("xt_tanh", 1)
        xt_silu = sig("xt_silu", 1)
        xt_h = sig("xt_h", 1)
        xt_htr = sig("xt_htr", 1)
        xt_hc = sig("xt_hc", 1)
        xt_out = sig("xt_out", 1)
        xt_yc = sig("xt_yc", 1)
        xt_num_c = sig("xt_num_c", 1)
        xt_saved = sig("xt_saved", 16)
        h_back = sig("h_back", 16)
        y_back = sig("y_back", 16)
        resid2 = sig("resid2", 2 + TC)
        qkp = sig("qkp", 4)
        vp = sig("vp", 2)
        qk_step = sig("qk_step", 2 * 7)
        parts_out = sig("parts_out", 16 * 2)
        q_sent = sig("q_sent", 16 * 6)
        k_sent = sig("k_sent", 16 * 6)
        v_ready = sig("v_ready", TC)
        s1 = sig("s1", HEADS * TC)
        mx = sig("mx", HEADS * TC)
        nm_step = sig("nm_step", 5)
        nm_tr = sig("nm_tr", 1)
        nm_c = sig("nm_c", 1)
        nm_out = sig("nm_out", 16)
        nm_sent = sig("nm_sent", 16)
        s2 = sig("s2", HEADS * TC)
        pexp = sig("pexp", HEADS * TC)
        pv = sig("pv", HEADS)
        og_c = sig("og_c", HG)
        og_tr = sig("og_tr", TC)
        a_norm = sig("a_norm", 2 * TC)
        ao = sig("ao", 2)
        resid3 = sig("resid3", 3)
        gate_mm = sig("gate_mm", 1)
        gate_tanh = sig("gate_tanh", 1)
        gate = sig("gate", 23)
        fp = sig("fp", E + 1)
        ftanh = sig("ftanh", E + 1)
        fsilu = sig("fsilu", E + 1)
        fhid = sig("fhid", E + 1)
        fout = sig("fout", E + 1)
        facc = sig("facc", (E + 1) * TC)
        stored = sig("stored", 16)

        n_loads, n_loads3 = [0], [0]
        FILLS = 3
        POOL_SETS = 18
        DVE_SETS = 15
        DVE_SETS3 = 6
        TAB_STEPS = 25
        block = ctx.enter_context(nc.Block())

        def tile_turns(eng, turn, pair):
            for s in range(2):
                turn(s, s, True, None)
            with eng.Fori(1, NT // 2 - 1) as j:
                pair[0] = j
                for i in range(2):
                    turn(j * 2 + i, i, False, None)
            for s in range(NT - 2, NT):
                turn(s, s % 2, False, NT - 1 - s)

        @block.sync
        def _(sp):
            def load(dst, src):
                sp.dma_start(dst, src).then_inc(loaded.sem, 16)
                n_loads[0] += 1

            load(idx_all[:, 0:NB * TC], tok)
            load(pos_sb[:], pos.rearrange("(c p) d -> p c d", p=P))
            load(in_w_sb[:], in_w.rearrange("(k p) m -> p k m", p=KP))
            load(conv_w_sb[:], conv_w.rearrange("(m p) k -> p m k", p=P))
            load(a_log_sb[:], a_log.rearrange("(m p) n -> p m n", p=P))
            for vec, dst in ((conv_b, conv_b_sb), (dt_bias, dt_bias_sb), (d_skip, d_skip_sb)):
                load(dst[:], vec)
            xproj_v = xproj_w.rearrange("(m p) k -> p m k", p=P)
            for s in range(SETS):
                for r in range(3):
                    load(xproj_bc[:, :, s, 32 * r:32 * r + 32], xproj_v[:, :, 32 * s:32 * s + 32])
            load(xproj_q[:, :, 0], xproj_dt)
            load(out_w_sb[:], out_w.rearrange("(m p) d -> p m d", p=P))
            load(router_w_sb[:], router_w.rearrange("(k p) e -> p k e", p=KP))
            load(router_b_sb[:], router_b.rearrange("(o n) -> o n", o=1).to_broadcast([P, E]))
            def load_wide(w, dst):
                for k in range(KT):
                    sp.dma_start(dst[:, k, :].rearrange("p (e m) -> p e m", e=E),
                                 w[:, k * KP:(k + 1) * KP, :].rearrange("e p m -> p e m")).then_inc(loaded2.sem, 16)

            load_wide(w2, w2_sb)
            for t in range(HT):
                sp.dma_start(w3_sb[:, t, :].rearrange("p (e d) -> p e d", e=E),
                             w3[:, t * P:(t + 1) * P, :].rearrange("e p d -> p e d")).then_inc(loaded2.sem, 16)
            sp.wait_ge(pool_set.sem, POOL_SETS)
            sp.dma_start(h_dram[LAST].rearrange("(c p) d -> p c d", p=P),
                         blank[:, 0:D].unsqueeze(1).to_broadcast([P, TC, D])).then_inc(filled.sem, 16)
            sp.dma_start(y_tok[LAST].rearrange("(c p) d -> p c d", p=P),
                         blank[:, 0:D].unsqueeze(1).to_broadcast([P, TC, D])).then_inc(filled.sem, 16)
            sp.dma_start(x_sorted[E * ROWS:E * ROWS + P, :], blank[:]).then_inc(filled.sem, 16)

            sp.wait_ge(filled.sem, 16 * FILLS)
            sp.sem_inc(h_free.sem, 1)
            with sp.Fori(0, NB) as b:
                sp.wait_ge(resid1.sem, resid1.at(b, 2))
                sp.dma_start(h_dram[bass.ds(b, 1)].rearrange("o (c p) d -> p (o c) d", p=P), h[:]).then_inc(h_saved.sem, 16)
                sp.wait_ge(x_saved.sem, x_saved.at(b, 16 * TC))
                sp.wait_ge(h_saved.sem, h_saved.at(b, 16))
                sp.sem_inc(h_free.sem, 1)

            sp.wait_ge(tab.sem, TAB_STEPS)
            sp.wait_ge(x_saved.sem, 16 * TC * LAST)
            sp.wait_ge(h_saved.sem, 16 * LAST)

            load_wide(w1, w1_sb)

            def load3(dst, src):
                sp.dma_start(dst, src).then_inc(loaded3.sem, 16)
                n_loads3[0] += 1

            for e in range(E):
                row = sp.value_load(tail[0:1, e:e + 1], min_val=e * ROWS, max_val=e * ROWS + NB * T)
                sp.dma_start(x_sorted[bass.ds(row, P), :], blank[:]).then_inc(filled.sem, 16)
            for vec, dst in ((bv, bv_sb), (bo, bo_sb), (gate_b, gate_b_sb)):
                load3(dst[:], vec.rearrange("(o n) -> o n", o=1).to_broadcast([P, vec.shape[0]]))
            for w, dst in ((wq, wq_sb), (wk, wk_sb), (wv, wv_sb), (wo, wo_sb), (gate_w, gate_w_sb)):
                load3(dst[:], w.rearrange("(k p) m -> p k m", p=KP))
            load3(bqk_sb[:, 0, :], bq)
            load3(bqk_sb[:, 1, :], bk)
            for w, dst in ((f1, f1_sb), (f3, f3_sb)):
                for k in range(KT):
                    load3(dst[:, k], w[:, k * KP:(k + 1) * KP, :].rearrange("e p i -> p e i"))
            load3(f2_sb[:], f2.rearrange("e i d -> i e d"))
            sp.wait_ge(filled.sem, 16 * (FILLS + E))

            def load_tile(s, i, first):
                row = sp.value_load(table_r[0:1, bass.ds(s, 1)], min_val=0, max_val=E * ROWS)
                if not first:
                    sp.wait_ge(xt_tr.sem, xt_tr.at(s, -1))
                    sp.wait_ge(xt_num_c.sem, xt_num_c.at(s, -1))
                sp.dma_start(xt_in[i][:], x_sorted[bass.ds(row, P), :]).then_inc(xt_loaded[i].sem, 16)

            def turn(s, i, first, last):
                if last is None:
                    load_tile(s + 2, i, False)

            load_tile(0, 0, True)
            load_tile(1, 1, True)
            tile_turns(sp, turn, [None])
            sp.wait_ge(xt_saved.sem, 16 * NT)

            def fetch(b):
                sp.dma_start(h_in[:], h_dram[bass.ds(b, 1)].rearrange("o (c p) d -> p (o c) d", p=P)).then_inc(h_back.sem, 16)
                sp.dma_start(y_in[:], y_tok[bass.ds(b, 1)].rearrange("o (c p) d -> p (o c) d", p=P)).then_inc(y_back.sem, 16)

            fetch(0)
            sp.sem_inc(h_free3.sem, 1)
            with sp.Fori(0, NB) as b:
                sp.wait_ge(resid2.sem, resid2.at(b, 2 + TC))
                fetch(b + 1)
                for which, (dst, sent) in enumerate(((qs, q_sent), (ks, k_sent))):
                    sp.wait_ge(qk_step.sem, qk_step.at(b, 7 * which + 7))
                    sp.dma_start(parts_dram[which].rearrange("r (k p) t -> p (r k) t", p=KP),
                                 parts[:].rearrange("p r k t -> p (r k) t")).then_inc(parts_out.sem, 16)
                    sp.wait_ge(parts_out.sem, parts_out.at(b, 16 * which + 16))
                    for j, pair in enumerate(PRODUCTS):
                        sp.dma_start(dst[HD * j:HD * (j + 1), :, :],
                                     parts_dram[which, pair[which]].rearrange("(h d) t -> d h t", d=HD)).then_inc(sent.sem, 16)
                sp.wait_ge(nm_c.sem, nm_c.at(b, 1))
                sp.dma_start(nm_dram, nm_T[:]).then_inc(nm_out.sem, 16)
                sp.wait_ge(nm_out.sem, nm_out.at(b, 16))
                sp.dma_start(qs[96:99, :, :], nm_dram.rearrange("(r h) t -> r h t", r=3)).then_inc(nm_sent.sem, 16)
                sp.wait_ge(facc.sem, facc.at(b, (E + 1) * TC))
                sp.dma_start(out[bass.ds(b, 1)].rearrange("o (c p) d -> p (o c) d", p=P), h[:]).then_inc(stored.sem, 16)
                sp.wait_ge(stored.sem, stored.at(b, 16))
                sp.sem_inc(h_free3.sem, 1)
            sp.wait_ge(stored.sem, 16 * LAST)
            sp.wait_ge(h_back.sem, 16 * (LAST + 1))
            sp.wait_ge(y_back.sem, 16 * (LAST + 1))

        ALL_LOADED = 16 * n_loads[0]
        ALL_LOADED2 = 16 * (2 * KT + HT)
        ALL_LOADED3 = 16 * n_loads3[0]

        @block.gpsimd
        def _(pool):
            pool.memset(ident[:], 0.0).then_inc(pool_set.sem, 1)
            pool.memset(onehot[:], 0.0).then_inc(pool_set.sem, 1)
            pool.memset(before[:], 1.0).then_inc(pool_set.sem, 1)
            pool.memset(tri[:], 1.0).then_inc(pool_set.sem, 1)
            pool.memset(neg_half[:], -0.5).then_inc(pool_set.sem, 1)
            pool.memset(blank[:, 0:D], 0.0).then_inc(pool_set.sem, 1)
            pool.iota(blank[:, D:D + 1].bitcast(I32), pattern=[[0, 1]], base=NB * T, channel_multiplier=1).then_inc(pool_set.sem, 1)
            pool.iota(token_i[:], pattern=[[P, TC]], base=0, channel_multiplier=1).then_inc(pool_set.sem, 1)
            pool.iota(falling_i[:], pattern=[[-1, E]], base=E, channel_multiplier=0).then_inc(pool_set.sem, 1)
            pool.wait_ge(pool_set.sem, 9)
            pool.affine_select(out=ident[:], in_=ident[:], compare_op=ALU.not_equal, fill=1.0, base=0,
                               pattern=[[-1, P]], channel_multiplier=1).then_inc(pool_set.sem, 1)
            pool.affine_select(out=before[:], in_=before[:], compare_op=ALU.is_gt, fill=0.0, base=0,
                               pattern=[[1, E], [-1, E]], channel_multiplier=0).then_inc(pool_set.sem, 1)
            pool.affine_select(out=tri[:], in_=tri[:], compare_op=ALU.is_gt, fill=0.0, base=0,
                               pattern=[[1, P]], channel_multiplier=-1).then_inc(pool_set.sem, 1)
            for r in range(3):
                pool.wait_ge(pool_set.sem, 12 + r)
                pool.affine_select(out=onehot[:], in_=onehot[:], compare_op=ALU.not_equal, fill=1.0,
                                   base=-32 * r, pattern=[[-1, 32], [0, P]],
                                   channel_multiplier=1).then_inc(pool_set.sem, 1)
            pool.tensor_copy(falling[:], falling_i[:]).then_inc(pool_set.sem, 1)
            pool.tensor_copy(token[:], token_i[:]).then_inc(pool_set.sem, 1)
            pool.memset(no_number[:], 0).then_inc(pool_set.sem, 1)
            pool.wait_ge(loaded.sem, ALL_LOADED)
            pool.wait_ge(pool_set.sem, POOL_SETS)
            pool.wait_ge(dve_set.sem, DVE_SETS)

            def rstd_of(norm, b, l):
                pool.wait_ge(norm.step.sem, norm.step.at(b, (2 * TC + 2) * (l + 1)))
                pool.tensor_tensor(rstd[:], vare[:], neg_half[:], ALU.pow).then_inc(norm.rstd.sem, 1)

            def gather_embedding(b, first=False):
                if not first:
                    pool.wait_ge(gathered.sem, gathered.at(b, 0))
                pool.tensor_copy(idx[:], idx_all[:, bass.ds(b * TC, TC)]).then_inc(idx_ready.sem, 1)
                copied = in_register(pool, idx_ready.at(b, 1))
                pool.wait_ge(pool_set.sem, POOL_SETS)
                pool.wait_ge(idx_ready.sem, copied)
                for c in range(TC):
                    pool.indirect_dma_start(
                        out=rows_in[:, c, :], out_offset=None, in_=emb,
                        in_offset=bass.IndirectOffsetOnAxis(ap=idx[:, c:c + 1].bitcast(U32), axis=0),
                    ).then_inc(gathered.sem, 16)

            gather_embedding(0, True)
            with pool.Fori(0, NB) as b:
                rstd_of(n1, b, 0)
                gather_embedding(b + 1)

                def drive_step(n, at):
                    i = n % 2
                    pool.wait_ge(b_copied.sem, at(b_copied, 1))
                    if n >= 2:
                        pool.wait_ge(scanned.sem, at(scanned, -1))
                    pool.tensor_tensor(drive[i][:], u[:], b_sb[i][:].unsqueeze(1).to_broadcast([P, M3, T]),
                                       ALU.mult).then_inc(driven.sem, 1)

                pool.wait_ge(dt_step.sem, dt_step.at(b, 5))
                for n in range(U8):
                    drive_step(n, lambda s, k, n=n: s.at(b, n + k))
                with pool.Fori(1, NS // U8) as j:
                    for n in range(U8):
                        drive_step(n + U8, lambda s, k, n=n: s.at(b, n + k) + j * U8)
                rstd_of(n1, b, 1)
                pool.wait_ge(numbered.sem, numbered.at(b, 1))
                placed = in_register(pool, route.at(b, 15))
                pool.wait_ge(pool_set.sem, POOL_SETS)
                pool.wait_ge(route.sem, placed)
                for c in range(TC):
                    pool.indirect_dma_start(
                        out=x_sorted, out_offset=bass.IndirectOffsetOnAxis(ap=slot[:, c:c + 1].bitcast(U32), axis=0),
                        in_=xr[:, c, :], in_offset=None).then_inc(x_saved.sem, 16)
            pool.wait_ge(gathered.sem, 16 * TC * (LAST + 1))

            pair = [None]

            def turn(s, i, first, last):
                pool.wait_ge(xt_loaded[i].sem, 16 * (s // 2 + 1) if isinstance(s, int) else xt_loaded[i].at(pair[0], 16))
                if not (first and i == 0):
                    pool.wait_ge(xt_saved.sem, xt_saved.at(s, 0))
                pool.tensor_tensor(xt_num[i][:], xt_in[i][:, D:D + 1].bitcast(I32), no_number[:], ALU.add).then_inc(xt_num_c.sem, 1)
                done = in_register(pool, xt_yc.at(s, 1))
                pool.wait_ge(pool_set.sem, POOL_SETS)
                pool.wait_ge(xt_num_c.sem, done)
                pool.wait_ge(xt_yc.sem, done)
                pool.indirect_dma_start(
                    out=y_rows, out_offset=bass.IndirectOffsetOnAxis(ap=xt_num[i][:].bitcast(U32), axis=0),
                    in_=xt_y[i][:], in_offset=None).then_inc(xt_saved.sem, 16)

            pool.wait_ge(tab.sem, TAB_STEPS)
            tile_turns(pool, turn, pair)

            pool.wait_ge(xt_saved.sem, 16 * NT)
            with pool.Fori(0, NB) as b:
                rstd_of(n3, b, 0)
                rstd_of(n3, b, 1)

        @block.scalar
        def _(act):
            act.wait_ge(loaded.sem, ALL_LOADED)
            act.activation(a_exp[:], a_log_sb[:], ACT.Exp).then_inc(act_set.sem, 1)
            act.wait_ge(dve_set.sem, DVE_SETS)

            def copy_transposed(norm, b, call):
                for k in range(KT):
                    act.wait_ge(norm.tr.sem, norm.tr.at(b, call * KT + k + 1))
                    act.activation(xnT[:, k, :], psW[0:KP, k, :], ACT.Copy).then_inc(norm.T.sem, 1)

            with act.Fori(0, NB) as b:
                copy_transposed(n1, b, 0)
                for m in range(M3):
                    act.wait_ge(proj.sem, proj.at(b, m + 1))
                    act.activation(xs[:, m, TAPS - 1:], psW[:, m, :], ACT.Copy).then_inc(xs_ready.sem, 1)
                for m in range(M3):
                    act.wait_ge(proj.sem, proj.at(b, M3 + m + 1))
                    act.activation(drive[0][:, m, :], psY[:, m, :], ACT.Tanh, scale=0.5).then_inc(z_tanh.sem, 1)
                for m in range(M3):
                    act.wait_ge(conv.sem, conv.at(b, M3 * (TAPS - 1) + m + 1))
                    act.activation(drive[1][:, m, :], xc[:, m, :], ACT.Tanh).then_inc(conv_tanh.sem, 1)
                act.wait_ge(xp.sem, xp.at(b, SETS + 1))
                for m in range(M3):
                    act.activation(dt[:, m, :], psC[:], ACT.Relu, bias=dt_bias_sb[:, m:m + 1]).then_inc(sp_act.sem, 1)
                for m in range(M3):
                    act.activation(weighed[0][:, m, :], psC[:], ACT.Abs, bias=dt_bias_sb[:, m:m + 1]).then_inc(sp_act.sem, 1)
                act.wait_ge(sp_act.sem, sp_act.at(b, 2 * M3))
                act.wait_ge(xc_ready.sem, xc_ready.at(b, M3))
                act.wait_ge(z_gate.sem, z_gate.at(b, M3))
                for m in range(M3):
                    act.activation(drive[0][:, m, :], weighed[0][:, m, :], ACT.Exp, scale=-1.0).then_inc(sp_act.sem, 1)
                act.wait_ge(sp_act.sem, sp_act.at(b, 3 * M3))
                for m in range(M3):
                    act.activation(drive[1][:, m, :], drive[0][:, m, :], ACT.Ln, bias=1.0).then_inc(sp_act.sem, 1)

                def scan_step(n, at, col):
                    i = n % 2
                    act.wait_ge(b_bc.sem, at(b_bc, 1))
                    if n >= 2:
                        act.wait_ge(driven.sem, at(driven, -1))
                    act.activation(b_sb[i][:], psB[:], ACT.Copy).then_inc(b_copied.sem, 1)
                    if n >= 2:
                        act.wait_ge(scanned.sem, at(scanned, -1))
                    for m in range(M3):
                        last = act.activation(decay[i][:, m, 1:T], dt[:, m, 1:T], ACT.Exp,
                                              scale=a_neg[:, m, col])
                    last.then_inc(decayed.sem, 1)

                act.wait_ge(dt_step.sem, dt_step.at(b, 4))
                for n in range(U8):
                    scan_step(n, lambda s, k, n=n: s.at(b, n + k), slice(n, n + 1))
                with act.Fori(1, NS // U8) as j:
                    for n in range(U8):
                        scan_step(n + U8, lambda s, k, n=n: s.at(b, n + k) + j * U8, bass.ds(j * U8 + n, 1))
                copy_transposed(n1, b, 1)
                act.wait_ge(route.sem, route.at(b, 7))
                act.activation(soft_e[:], soft[:], ACT.Exp).then_inc(route_exp.sem, 1)

            act.wait_ge(tab.sem, TAB_STEPS)

            def tile_copy(s, i, first):
                act.wait_ge(xt_tr.sem, xt_tr.at(s, 1))
                if not first:
                    act.wait_ge(xt_hp.sem, xt_hp.at(s, -1))
                act.activation(xt_T[i][:], psY[0:KP, 0, 0:KT * P], ACT.Copy).then_inc(xt_c.sem, 1)

            def tile_tanh(s, i, first):
                act.wait_ge(xt_hp.sem, xt_hp.at(s, 1))
                if not first:
                    act.wait_ge(xt_silu.sem, xt_silu.at(s, -1))
                act.activation(xt_th[i][:], psW[:, 0, :] if i == 0 else psW[:, 2, :], ACT.Tanh, scale=0.5).then_inc(xt_tanh.sem, 1)

            def turn(s, i, first, last):
                if last is None or last >= 1:
                    tile_tanh(s + 1, 1 - i, first and i == 0)
                if last is None:
                    tile_copy(s + 2, i, False)
                act.wait_ge(xt_htr.sem, xt_htr.at(s, 1))
                if not first:
                    act.wait_ge(xt_out.sem, xt_out.at(s, -1))
                act.activation(xt_hT[i][:], psB[:], ACT.Copy).then_inc(xt_hc.sem, 1)
                act.wait_ge(xt_out.sem, xt_out.at(s, 1))
                if not first:
                    act.wait_ge(xt_saved.sem, xt_saved.at(s, -16))
                act.activation(xt_y[i][:], psY[:, 1 + i, 0:D], ACT.Copy).then_inc(xt_yc.sem, 1)

            tile_copy(0, 0, True)
            tile_copy(1, 1, True)
            tile_tanh(0, 0, True)
            tile_turns(act, turn, [None])

            act.wait_ge(loaded3.sem, ALL_LOADED3)
            act.wait_ge(dve_set3.sem, DVE_SETS3)
            with act.Fori(0, NB) as b:
                copy_transposed(n3, b, 0)
                act.wait_ge(nm_tr.sem, nm_tr.at(b, 1))
                act.activation(nm_T[:], psY[0:3 * HEADS, 0, 0:T // 2].bitcast(BF16), ACT.Copy).then_inc(nm_c.sem, 1)
                for hd in range(HEADS):
                    for c in range(TC):
                        q = hd * TC + c
                        act.wait_ge(s2.sem, s2.at(b, q + 1))
                        if hd >= 2 and c == 0:
                            act.wait_ge(pv.sem, pv.at(b, hd - 1))
                        act.activation(pT[hd % 2][:, c, :], psW[:, q % 3, :], ACT.Exp).then_inc(pexp.sem, 1)
                copy_transposed(n3, b, 1)
                copy_transposed(n3, b, 2)
                act.wait_ge(gate_mm.sem, gate_mm.at(b, 1))
                act.activation(gate_s[:], psB[:, 0:TC * E].rearrange("p (c e) -> p c e", c=TC), ACT.Tanh,
                               scale=0.5).then_inc(gate_tanh.sem, 1)
                for e in range(E + 1):
                    act.wait_ge(fp.sem, fp.at(b, e + 1))
                    if e >= 3:
                        act.wait_ge(fsilu.sem, fsilu.at(b, e - 2))
                    act.activation(th[:, e % 3, :], psW[:, e % 2, :], ACT.Tanh, scale=0.5).then_inc(ftanh.sem, 1)

        @block.vector
        def _(dve):
            dve.memset(xs[:], 0.0).then_inc(dve_set.sem, 1)
            for i in range(2):
                dve.memset(decay[i][:], 0.0).then_inc(dve_set.sem, 1)
            dve.memset(ones[:], 1.0).then_inc(dve_set.sem, 1)
            dve.memset(count[:], 0.0).then_inc(dve_set.sem, 1)
            dve.memset(idx_all[:, NB * TC:], 0).then_inc(dve_set.sem, 1)
            dve.wait_ge(loaded.sem, ALL_LOADED)
            dve.wait_ge(pool_set.sem, POOL_SETS)
            dve.tensor_scalar(conv_wh[:], conv_w_sb[:], 0.5, None, ALU.mult).then_inc(dve_set.sem, 1)
            dve.tensor_scalar(conv_bh[:], conv_b_sb[:], 0.5, None, ALU.mult).then_inc(dve_set.sem, 1)
            for m in range(M3):
                dve.tensor_scalar(diag_d[:, m, :], ident[:], d_skip_sb[:, m:m + 1], None, ALU.mult).then_inc(dve_set.sem, 1)
                dve.tensor_copy(xproj_qr[:, m, :], xproj_q[:, m, :].to_broadcast([P, P])).then_inc(dve_set.sem, 1)
            dve.wait_ge(act_set.sem, 1)
            dve.tensor_scalar(a_neg[:], a_exp[:], -1.0, None, ALU.mult).then_inc(dve_set.sem, 1)
            dve.wait_ge(dve_set.sem, DVE_SETS)

            def layer_norm(norm, b, l, dst):
                base = (2 * TC + 2) * l
                for c in range(TC):
                    dve.bn_stats(stats[:, c, :], h[:, c, :]).then_inc(norm.step.sem, 1)
                dve.wait_ge(norm.step.sem, norm.step.at(b, base + TC))
                dve.tensor_copy(stat_count[:], stats[:, TC - 1, 0:1]).then_inc(norm.step.sem, 1)
                for c in range(TC):
                    dve.bn_aggr(mv[:, c, :], stats[:, c, :]).then_inc(norm.step.sem, 1)
                dve.wait_ge(norm.step.sem, norm.step.at(b, base + 2 * TC + 1))
                dve.tensor_scalar(vare[:], mv[:, :, 1], EPS, None, ALU.add).then_inc(norm.step.sem, 1)
                dve.wait_ge(norm.rstd.sem, norm.rstd.at(b, l + 1))
                for c in range(TC):
                    dve.tensor_scalar(dst[:, c, 0:D], h[:, c, :], mv[:, c, 0:1], rstd[:, c:c + 1],
                                      ALU.subtract, ALU.mult).then_inc(norm.xn.sem, 1)

            bc_e = lambda t: t[:].unsqueeze(2).to_broadcast([P, TC, E])

            with dve.Fori(0, NB) as b:
                dve.wait_ge(gathered.sem, gathered.at(b, 16 * TC))
                dve.wait_ge(h_free.sem, h_free.at(b, 1))
                dve.tensor_tensor(h[:], rows_in[:], pos_sb[:], ALU.add).then_inc(h_ready.sem, 1)
                dve.wait_ge(h_ready.sem, h_ready.at(b, 1))
                layer_norm(n1, b, 0, xn)
                for k in range(TAPS):
                    for m in range(M3):
                        if k == 0:
                            dve.wait_ge(xs_ready.sem, xs_ready.at(b, m + 1))
                            dve.tensor_scalar(xc[:, m, :], xs[:, m, 0:T], conv_wh[:, m, 0:1], conv_bh[:, m:m + 1],
                                              ALU.mult, ALU.add).then_inc(conv.sem, 1)
                        else:
                            dve.wait_ge(conv.sem, conv.at(b, M3 * (k - 1) + m + 1))
                            dve.scalar_tensor_tensor(out=xc[:, m, :], in0=xs[:, m, k:k + T],
                                                     scalar=conv_wh[:, m, k:k + 1], in1=xc[:, m, :],
                                                     op0=ALU.mult, op1=ALU.add).then_inc(conv.sem, 1)
                for m in range(M3):
                    dve.wait_ge(conv_tanh.sem, conv_tanh.at(b, m + 1))
                    dve.scalar_tensor_tensor(out=xc[:, m, :], in0=drive[1][:, m, :], scalar=1.0, in1=xc[:, m, :],
                                             op0=ALU.add, op1=ALU.mult).then_inc(xc_ready.sem, 1)
                for m in range(M3):
                    dve.wait_ge(z_tanh.sem, z_tanh.at(b, m + 1))
                    dve.scalar_tensor_tensor(out=gz[:, m, :], in0=drive[0][:, m, :], scalar=1.0, in1=psY[:, m, :],
                                             op0=ALU.add, op1=ALU.mult).then_inc(z_gate.sem, 1)
                bank = [psW[0:96, 0, :], psW[0:96, 1, :], psW[0:96, 2, :], psB[0:96, :]]
                rest = weighed[1]
                for s in range(SETS):
                    dve.wait_ge(xp.sem, xp.at(b, s + 1))
                    dve.tensor_copy(bc_s[:, s, :], bank[s]).then_inc(split.sem, 1)
                    dve.wait_ge(split.sem, split.at(b, 5 * s + 1))
                    dve.tensor_tensor(rest[0:64, 0, :], bank[s][0:64], bc_s[0:64, s, :], ALU.subtract).then_inc(split.sem, 1)
                    dve.wait_ge(split.sem, split.at(b, 5 * s + 2))
                    dve.tensor_copy(bc_s[0:64, s, :], rest[0:64, 0, :]).then_inc(split.sem, 1)
                    dve.wait_ge(split.sem, split.at(b, 5 * s + 3))
                    dve.tensor_tensor(rest[0:32, 1, :], rest[0:32, 0, :], bc_s[0:32, s, :], ALU.subtract).then_inc(split.sem, 1)
                    dve.wait_ge(split.sem, split.at(b, 5 * s + 4))
                    dve.tensor_copy(bc_s[0:32, s, :], rest[0:32, 1, :]).then_inc(split.sem, 1)
                dve.wait_ge(sp_act.sem, sp_act.at(b, 4 * M3))
                dve.tensor_scalar(weighed[0][:], drive[0][:], 1.0, -1.0, ALU.add, ALU.add).then_inc(dt_step.sem, 1)
                dve.tensor_tensor(dt[:], dt[:], drive[1][:], ALU.add).then_inc(dt_step.sem, 1)
                dve.wait_ge(dt_step.sem, dt_step.at(b, 2))
                dve.tensor_tensor(weighed[0][:], drive[0][:], weighed[0][:], ALU.subtract).then_inc(dt_step.sem, 1)
                dve.wait_ge(dt_step.sem, dt_step.at(b, 3))
                dve.tensor_tensor(dt[:], dt[:], weighed[0][:], ALU.add).then_inc(dt_step.sem, 1)
                dve.wait_ge(dt_step.sem, dt_step.at(b, 4))
                dve.wait_ge(xc_ready.sem, xc_ready.at(b, M3))
                dve.tensor_tensor(u[:], dt[:], xc[:], ALU.mult).then_inc(dt_step.sem, 1)

                def scan_step(n, at):
                    i = n % 2
                    dve.wait_ge(decayed.sem, at(decayed, 1))
                    dve.wait_ge(driven.sem, at(driven, 1))
                    if n >= 1:
                        dve.wait_ge(weighed_s.sem, at(weighed_s, 0))
                    dve.tensor_tensor_scan(flat(state), flat(decay[i]), flat(drive[i]), 0.0,
                                           ALU.mult, ALU.add).then_inc(scanned.sem, 1)
                    dve.wait_ge(scanned.sem, at(scanned, 1))
                    dve.wait_ge(c_bc.sem, at(c_bc, 1))
                    if n >= 2:
                        dve.wait_ge(summed.sem, at(summed, -1))
                    dve.tensor_tensor(weighed[i][:], state[:], psC[:].unsqueeze(1).to_broadcast([P, M3, T]),
                                      ALU.mult).then_inc(weighed_s.sem, 1)

                for n in range(U8):
                    scan_step(n, lambda s, k, n=n: s.at(b, n + k))
                with dve.Fori(1, NS // U8) as j:
                    for n in range(U8):
                        scan_step(n + U8, lambda s, k, n=n: s.at(b, n + k) + j * U8)

                dve.wait_ge(summed.sem, summed.at(b, NS + 1))
                dve.scalar_tensor_tensor(out=gz[:], in0=psY[:], scalar=0.5, in1=gz[:],
                                         op0=ALU.mult, op1=ALU.mult).then_inc(gated.sem, 1)
                for c2 in range(2):
                    dve.wait_ge(outp.sem, outp.at(b, c2 + 1))
                    dve.tensor_tensor(h[:, 2 * c2:2 * c2 + 2, :], h[:, 2 * c2:2 * c2 + 2, :],
                                      psW[:, c2, 0:2 * D].rearrange("p (c d) -> p c d", c=2), ALU.add).then_inc(resid1.sem, 1)
                dve.wait_ge(resid1.sem, resid1.at(b, 2))
                dve.tensor_copy(xr[:, :, D:D + 1].bitcast(I32), token[:].unsqueeze(2)).then_inc(numbered.sem, 1)
                dve.wait_ge(numbered.sem, numbered.at(b, 1))
                dve.tensor_scalar(token[:], token[:], float(T), None, ALU.add).then_inc(numbered.sem, 1)
                layer_norm(n1, b, 1, xr)

                dve.wait_ge(route_mm.sem, route_mm.at(b, 1))
                dve.tensor_tensor(logit[:], psB[:, 0:TC * E].rearrange("p (c e) -> p c e", c=TC),
                                  router_b_sb[:].unsqueeze(1).to_broadcast([P, TC, E]), ALU.add).then_inc(route.sem, 1)
                dve.wait_ge(route.sem, route.at(b, 1))
                dve.tensor_reduce(top[:], logit[:], AX.X, ALU.max).then_inc(route.sem, 1)
                dve.wait_ge(route.sem, route.at(b, 2))
                dve.tensor_tensor(tie[:], logit[:], bc_e(top), ALU.is_equal).then_inc(route.sem, 1)
                dve.wait_ge(route.sem, route.at(b, 3))
                dve.tensor_tensor(rev[:], tie[:], falling[:].unsqueeze(1).to_broadcast([P, TC, E]), ALU.mult).then_inc(route.sem, 1)
                dve.wait_ge(route.sem, route.at(b, 4))
                dve.tensor_reduce(first[:], rev[:], AX.X, ALU.max).then_inc(route.sem, 1)
                dve.wait_ge(route.sem, route.at(b, 5))
                dve.tensor_tensor(chosen[:], rev[:], bc_e(first), ALU.is_equal).then_inc(route.sem, 1)
                dve.tensor_tensor(soft[:], logit[:], bc_e(top), ALU.subtract).then_inc(route.sem, 1)
                dve.wait_ge(route.sem, route.at(b, 7))
                dve.tensor_copy(chosen_b[:], chosen[:]).then_inc(route.sem, 1)
                dve.wait_ge(route_exp.sem, route_exp.at(b, 1))
                dve.tensor_reduce(soft_s[:], soft_e[:], AX.X, ALU.add).then_inc(route.sem, 1)
                dve.wait_ge(route.sem, route.at(b, 9))
                dve.reciprocal(prob_all[:, bass.ds(b * TC, TC)], soft_s[:]).then_inc(route.sem, 1)
                dve.wait_ge(ranked.sem, ranked.at(b, 1))
                dve.tensor_tensor(ahead[:], psC[:, 0:TC * E].rearrange("p (c e) -> p c e", c=TC),
                                  count[:].unsqueeze(1).to_broadcast([P, TC, E]), ALU.add).then_inc(route.sem, 1)
                dve.wait_ge(route.sem, route.at(b, 11))
                dve.tensor_tensor(ahead[:], ahead[:], chosen[:], ALU.mult).then_inc(route.sem, 1)
                dve.tensor_scalar(region[:], first[:], -float(ROWS), float(E * ROWS), ALU.mult, ALU.add).then_inc(route.sem, 1)
                dve.wait_ge(route.sem, route.at(b, 13))
                dve.tensor_reduce(place[:], ahead[:], AX.X, ALU.add).then_inc(route.sem, 1)
                dve.wait_ge(route.sem, route.at(b, 14))
                dve.tensor_tensor(slot[:], place[:], region[:], ALU.add).then_inc(route.sem, 1)
                dve.tensor_tensor(count[:], count[:], psC[:, TC * E:(TC + 1) * E], ALU.add).then_inc(route.sem, 1)
                dve.wait_ge(route.sem, route.at(b, 16))
                dve.wait_ge(numbered.sem, numbered.at(b, 2))

            step = [0]

            def tab_step(ins):
                step[0] += 1
                ins.then_inc(tab.sem, 1)
                dve.wait_ge(tab.sem, step[0])

            dve.wait_ge(x_saved.sem, 16 * TC * LAST)
            dve.wait_ge(h_saved.sem, 16 * LAST)
            e_of = lambda v: v.unsqueeze(1).to_broadcast([P, NT, E])
            s_of = lambda v: v.unsqueeze(2).to_broadcast([P, NT, E])
            tab_step(dve.tensor_tensor_scan(t_num, ones[:, 0:NT], ones[:, 0:NT], -1.0, ALU.mult, ALU.add))
            tab_step(dve.tensor_scalar(t_regions, falling[:], -float(ROWS), float(E * ROWS), ALU.mult, ALU.add))
            tab_step(dve.tensor_scalar(t_row, t_num, float(P), None, ALU.mult))
            tab_step(dve.tensor_tensor(t_cmp, e_of(count[:]), s_of(t_row), ALU.is_gt))
            tab_step(dve.tensor_reduce(t_full, t_cmp.rearrange("p s e -> p e s"), AX.X, ALU.add))
            tab_step(dve.tensor_tensor(t_pre, t_full.unsqueeze(1).to_broadcast([P, E, E]), before[:], ALU.mult))
            tab_step(dve.tensor_reduce(t_begin, t_pre, AX.X, ALU.add))
            tab_step(dve.tensor_tensor(t_end, t_begin, t_full, ALU.add))
            tab_step(dve.tensor_tensor(t_a, s_of(t_num), e_of(t_begin), ALU.is_ge))
            tab_step(dve.tensor_tensor(t_b, s_of(t_num), e_of(t_end), ALU.is_lt))
            tab_step(dve.tensor_tensor(t_a, t_a, t_b, ALU.mult))
            tab_step(dve.tensor_reduce(t_valid, t_a, AX.X, ALU.add))
            tab_step(dve.scalar_tensor_tensor(out=t_off, in0=t_begin, scalar=-float(P), in1=t_regions, op0=ALU.mult, op1=ALU.add))
            tab_step(dve.tensor_tensor(t_b, s_of(t_row), e_of(t_off), ALU.add))
            tab_step(dve.tensor_tensor(t_b, t_b, t_a, ALU.mult))
            tab_step(dve.tensor_reduce(t_row, t_b, AX.X, ALU.add))
            tab_step(dve.tensor_scalar(t_valid, t_valid, -float(E * ROWS), float(E * ROWS), ALU.mult, ALU.add))
            tab_step(dve.tensor_tensor(t_row, t_row, t_valid, ALU.add))
            tab_step(dve.tensor_scalar(t_off, falling[:], -1.0, float(E), ALU.mult, ALU.add))
            tab_step(dve.tensor_tensor(t_b, t_a, e_of(t_off), ALU.mult))
            tab_step(dve.tensor_reduce(t_exp, t_b, AX.X, ALU.add))
            tab_step(dve.tensor_tensor(t_tail, count[:], t_regions, ALU.add))
            tab_step(dve.tensor_copy(table_r[:], t_row[0:1, :]))
            tab_step(dve.tensor_copy(table_e[:], t_exp[0:1, :]))
            tab_step(dve.tensor_copy(tail[:], t_tail[0:1, :]))
            assert step[0] == TAB_STEPS

            def tile_hidden(s, i, first):
                h1, h2 = (psW[:, 0, :], psW[:, 1, :]) if i == 0 else (psW[:, 2, :], psC[:])
                dve.wait_ge(xt_tanh.sem, xt_tanh.at(s, 1))
                if not (first and i == 0):
                    dve.wait_ge(xt_h.sem, xt_h.at(s, 0))
                dve.scalar_tensor_tensor(out=xt_sl[:], in0=xt_th[i][:], scalar=1.0, in1=h1,
                                         op0=ALU.add, op1=ALU.mult).then_inc(xt_silu.sem, 1)
                dve.wait_ge(xt_silu.sem, xt_silu.at(s, 1))
                if not first:
                    dve.wait_ge(xt_htr.sem, xt_htr.at(s, -1))
                dve.scalar_tensor_tensor(out=xt_hid[i][:], in0=xt_sl[:], scalar=0.5, in1=h2,
                                         op0=ALU.mult, op1=ALU.mult).then_inc(xt_h.sem, 1)

            def turn(s, i, first, last):
                if last is None or last >= 1:
                    tile_hidden(s + 1, 1 - i, first and i == 0)

            tile_hidden(0, 0, True)
            tile_turns(dve, turn, [None])

            dve.wait_ge(xt_saved.sem, 16 * NT)
            dve.wait_ge(loaded3.sem, ALL_LOADED3)
            dve.memset(vA[:], 0.0).then_inc(dve_set3.sem, 1)
            dve.memset(ks[96:99, :, :], 1.0).then_inc(dve_set3.sem, 1)
            dve.memset(cw[:], 1.0).then_inc(dve_set3.sem, 1)
            dve.tensor_copy(identb[:], ident[:]).then_inc(dve_set3.sem, 1)
            dve.tensor_scalar(bqk_sb[:, 0, :], bqk_sb[:, 0, :], HD ** -0.5, None, ALU.mult).then_inc(dve_set3.sem, 1)
            dve.wait_ge(dve_set3.sem, 5)
            dve.memset(vA[:, :, :, HD:HD + 1], 1.0).then_inc(dve_set3.sem, 1)
            dve.wait_ge(dve_set3.sem, DVE_SETS3)

            with dve.Fori(0, NB) as b:
                dve.wait_ge(y_back.sem, y_back.at(b, 16))
                dve.tensor_copy(y_b[:], y_in[:]).then_inc(resid2.sem, 1)
                dve.tensor_copy(prob_cur[:], prob_all[:, bass.ds(b * TC, TC)]).then_inc(resid2.sem, 1)
                dve.wait_ge(resid2.sem, resid2.at(b, 2))
                dve.wait_ge(h_back.sem, h_back.at(b, 16))
                dve.wait_ge(h_free3.sem, h_free3.at(b, 1))
                for c in range(TC):
                    dve.scalar_tensor_tensor(out=h[:, c, :], in0=y_b[:, c, :], scalar=prob_cur[:, c:c + 1], in1=h_in[:, c, :],
                                             op0=ALU.mult, op1=ALU.add).then_inc(resid2.sem, 1)
                dve.wait_ge(resid2.sem, resid2.at(b, 2 + TC))
                layer_norm(n3, b, 0, xn)

                for which in range(2):
                    base = 7 * which
                    for k in range(KT):
                        dve.wait_ge(qkp.sem, qkp.at(b, 2 * which + k + 1))
                        if which == 1 and k == 0:
                            dve.wait_ge(parts_out.sem, parts_out.at(b, 16))
                        dve.tensor_scalar(qk_f[:, k, :], psY[0:KP, k, :] if which == 0 else (psY[0:KP, 2, :], psW[0:KP, 2, :])[k],
                                          HD ** -0.5 if which == 0 else 1.0, bqk_sb[:, which, k:k + 1],
                                          ALU.mult, ALU.add).then_inc(qk_step.sem, 1)
                    dve.wait_ge(qk_step.sem, qk_step.at(b, base + 2))
                    dve.tensor_copy(parts[:, 0, :, :], qk_f).then_inc(qk_step.sem, 1)
                    dve.wait_ge(qk_step.sem, qk_step.at(b, base + 3))
                    dve.tensor_tensor(qk_r, qk_f, parts[:, 0, :, :], ALU.subtract).then_inc(qk_step.sem, 1)
                    dve.wait_ge(qk_step.sem, qk_step.at(b, base + 4))
                    dve.tensor_copy(parts[:, 1, :, :], qk_r).then_inc(qk_step.sem, 1)
                    dve.wait_ge(qk_step.sem, qk_step.at(b, base + 5))
                    dve.tensor_tensor(qk_f, qk_r, parts[:, 1, :, :], ALU.subtract).then_inc(qk_step.sem, 1)
                    dve.wait_ge(qk_step.sem, qk_step.at(b, base + 6))
                    dve.tensor_copy(parts[:, 2, :, :], qk_f).then_inc(qk_step.sem, 1)
                for c in range(TC):
                    if c % 2 == 0:
                        dve.wait_ge(vp.sem, vp.at(b, c // 2 + 1))
                    src = (psB, psC)[c // 2][:, (c % 2) * D:(c % 2 + 1) * D]
                    dve.tensor_tensor(vA[:, c, :, 0:HD], src.rearrange("p (h d) -> p h d", d=HD),
                                      bv_sb[:].rearrange("p (h d) -> p h d", d=HD), ALU.add).then_inc(v_ready.sem, 1)
                for hd in range(HEADS):
                    for c in range(TC):
                        q = hd * TC + c
                        dve.wait_ge(s1.sem, s1.at(b, q + 1))
                        dve.tensor_reduce(neg_max[:, c, hd:hd + 1], psW[:, q % 3, :], AX.X, ALU.max,
                                          negate=True).then_inc(mx.sem, 1)
                dve.wait_ge(mx.sem, mx.at(b, HEADS * TC))
                dve.tensor_copy(nm_p[:, :, 0, :], neg_max[:]).then_inc(nm_step.sem, 1)
                dve.wait_ge(nm_step.sem, nm_step.at(b, 1))
                dve.tensor_tensor(nm_r[:], neg_max[:], nm_p[:, :, 0, :], ALU.subtract).then_inc(nm_step.sem, 1)
                dve.wait_ge(nm_step.sem, nm_step.at(b, 2))
                dve.tensor_copy(nm_p[:, :, 1, :], nm_r[:]).then_inc(nm_step.sem, 1)
                dve.wait_ge(nm_step.sem, nm_step.at(b, 3))
                dve.tensor_tensor(neg_max[:], nm_r[:], nm_p[:, :, 1, :], ALU.subtract).then_inc(nm_step.sem, 1)
                dve.wait_ge(nm_step.sem, nm_step.at(b, 4))
                dve.tensor_copy(nm_p[:, :, 2, :], neg_max[:]).then_inc(nm_step.sem, 1)

                for g in range(HG):
                    dve.wait_ge(pv.sem, pv.at(b, 4 * (g + 1)))
                    dve.tensor_copy(og[:, g, :], (psB, psC)[g % 2][:]).then_inc(og_c.sem, 1)
                o_bank = (psY[:, 0], psY[:, 1], psY[:, 2], psC[:])
                for c in range(TC):
                    o = o_bank[c][:, 0:HG * P].rearrange("p (h d) -> p h d", d=32)
                    dve.wait_ge(og_tr.sem, og_tr.at(b, c + 1))
                    dve.reciprocal(r_sum[:, c, :], o[:, :, HD]).then_inc(a_norm.sem, 1)
                    dve.wait_ge(a_norm.sem, a_norm.at(b, 2 * c + 1))
                    dve.tensor_tensor(xn[:, c, :].rearrange("p (h d) -> p h d", d=HD), o[:, :, 0:HD],
                                      r_sum[:, c, :].unsqueeze(2).to_broadcast([P, HEADS, HD]),
                                      ALU.mult).then_inc(a_norm.sem, 1)
                dve.tensor_tensor(h[:], h[:], bo_sb[:].unsqueeze(1).to_broadcast([P, TC, D]), ALU.add).then_inc(resid3.sem, 1)
                dve.wait_ge(resid3.sem, resid3.at(b, 1))
                for c2 in range(2):
                    dve.wait_ge(ao.sem, ao.at(b, c2 + 1))
                    dve.tensor_tensor(h[:, 2 * c2:2 * c2 + 2, :], h[:, 2 * c2:2 * c2 + 2, :],
                                      psY[:, c2, 0:2 * D].rearrange("p (c d) -> p c d", c=2), ALU.add).then_inc(resid3.sem, 1)
                dve.wait_ge(resid3.sem, resid3.at(b, 3))
                layer_norm(n3, b, 1, xn)

                step = [0]

                def gate_step(ins):
                    step[0] += 1
                    ins.then_inc(gate.sem, 1)
                    dve.wait_ge(gate.sem, gate.at(b, step[0]))

                def best_two(v, n, on):
                    vi = v.unsqueeze(3).to_broadcast([P, TC, n, n])
                    vj = v.unsqueeze(2).to_broadcast([P, TC, n, n])
                    gt, eq = cmp_gt[:, :, 0:n, 0:n], cmp_eq[:, :, 0:n, 0:n]
                    dve.tensor_tensor(gt, vj, vi, ALU.is_gt).then_inc(gate.sem, 1)
                    step[0] += 1
                    gate_step(dve.tensor_tensor(eq, vj, vi, ALU.is_equal))
                    gate_step(dve.tensor_tensor(eq, eq, before[:, 0:n, 0:n].unsqueeze(1).to_broadcast([P, TC, n, n]), ALU.mult))
                    gate_step(dve.tensor_tensor(gt, gt, eq, ALU.add))
                    gate_step(dve.tensor_reduce(rank[:, :, 0:n], gt, AX.X, ALU.add))
                    gate_step(dve.tensor_scalar(on, rank[:, :, 0:n], 2.0, None, ALU.is_lt))

                dve.wait_ge(gate_tanh.sem, gate_tanh.at(b, 1))
                gate_step(dve.tensor_scalar(gate_s[:], gate_s[:], 0.5, 0.5, ALU.mult, ALU.add))
                gate_step(dve.tensor_tensor(gate_v[:], gate_s[:], gate_b_sb[:].unsqueeze(1).to_broadcast([P, TC, E]), ALU.add))
                gate_step(dve.tensor_tensor(group_v[:], gate_v[:, :, 0::2], gate_v[:, :, 1::2], ALU.add))
                best_two(group_v[:], 4, group_on[:])
                pair = lambda t: t[:].rearrange("p c (g e) -> p c g e", e=2)
                on4 = group_on[:].unsqueeze(3).to_broadcast([P, TC, 4, 2])
                gate_step(dve.tensor_tensor(pair(masked), pair(gate_v), on4, ALU.mult))
                gate_step(dve.tensor_scalar(group_v[:], group_on[:], -1.0, 1e30, ALU.add, ALU.mult))
                gate_step(dve.tensor_tensor(pair(masked), pair(masked),
                                            group_v[:].unsqueeze(3).to_broadcast([P, TC, 4, 2]), ALU.add))
                best_two(masked[:], E, cw[:, :, 0:E])
                gate_step(dve.tensor_tensor(cw[:, :, 0:E], cw[:, :, 0:E], gate_s[:], ALU.mult))
                gate_step(dve.tensor_reduce(w_sum[:], cw[:, :, 0:E], AX.X, ALU.add))
                gate_step(dve.tensor_scalar(w_sum[:], w_sum[:], 1e-6, None, ALU.add))
                gate_step(dve.reciprocal(w_inv[:], w_sum[:]))
                gate_step(dve.tensor_tensor(cw[:, :, 0:E], cw[:, :, 0:E], bc_e(w_inv), ALU.mult))
                assert step[0] == gate.per, step[0]

                def accumulate2(e):
                    dve.wait_ge(fout.sem, fout.at(b, e + 1))
                    for c in range(TC):
                        src = psY[:, 1 + c // 2, (c % 2) * D:(c % 2 + 1) * D]
                        if e >= 1:
                            dve.wait_ge(facc.sem, facc.at(b, TC * (e - 1) + c + 1))
                        dve.scalar_tensor_tensor(out=h[:, c, :], in0=src, scalar=cw[:, c, e:e + 1],
                                                 in1=h[:, c, :], op0=ALU.mult, op1=ALU.add).then_inc(facc.sem, 1)

                for e in range(E + 1):
                    dve.wait_ge(ftanh.sem, ftanh.at(b, e + 1))
                    if e >= 1:
                        dve.wait_ge(fhid.sem, fhid.at(b, e))
                    dve.scalar_tensor_tensor(out=sl[:], in0=th[:, e % 3, :], scalar=1.0, in1=psW[:, e % 2, :],
                                             op0=ALU.add, op1=ALU.mult).then_inc(fsilu.sem, 1)
                    dve.wait_ge(fsilu.sem, fsilu.at(b, e + 1))
                    if e >= 2:
                        dve.wait_ge(fout.sem, fout.at(b, e - 1))
                    h2 = psW[:, 2, :] if e % 2 == 0 else psY[:, 0, :]
                    dve.scalar_tensor_tensor(out=hid[e % 2][:], in0=sl[:], scalar=0.5, in1=h2,
                                             op0=ALU.mult, op1=ALU.mult).then_inc(fhid.sem, 1)
                    if e >= 1:
                        accumulate2(e - 1)
                accumulate2(E)
                dve.wait_ge(facc.sem, facc.at(b, (E + 1) * TC))

        @block.tensor
        def _(pe):
            pe.wait_ge(loaded.sem, ALL_LOADED)
            pe.wait_ge(pool_set.sem, POOL_SETS)
            pe.wait_ge(dve_set.sem, DVE_SETS)

            def transposes(norm, src):
                for k in range(KT):
                    for c in range(TC):
                        mm = pe.transpose(psW[0:KP, k, c * P:(c + 1) * P], src[:, c, k * KP:(k + 1) * KP], ident[:])
                    mm.then_inc(norm.tr.sem, 1)

            def logits(w, done):
                for c in range(TC):
                    for k in range(KT):
                        mm = pe.matmul(psB[:, c * E:(c + 1) * E], xnT[:, k, c * P:(c + 1) * P], w[:, k, :],
                                       start=(k == 0), stop=(k == KT - 1))
                mm.then_inc(done, 1)

            with pe.Fori(0, NB) as b:
                pe.wait_ge(n1.xn.sem, n1.xn.at(b, TC))
                transposes(n1, xn)
                pe.wait_ge(n1.T.sem, n1.T.at(b, KT))
                for m in range(2 * M3):
                    dst = psW[:, m, :] if m < M3 else psY[:, m - M3, :]
                    for k in range(KT):
                        mm = pe.matmul(dst, in_w_sb[:, k, m * P:(m + 1) * P], xnT[:, k, :], start=(k == 0), stop=(k == KT - 1))
                    mm.then_inc(proj.sem, 1)
                pe.wait_ge(xc_ready.sem, xc_ready.at(b, M3))
                for s in range(SETS + 1):
                    if s < SETS:
                        dst, w = (psW[0:96, s, :] if s < 3 else psB[0:96, :]), xproj_bc[:, :, s, :]
                    else:
                        dst, w = psC[:], xproj_qr[:]
                    for m in range(M3):
                        mm = pe.matmul(dst, w[:, m, :], xc[:, m, :], start=(m == 0), stop=(m == M3 - 1))
                    mm.then_inc(xp.sem, 1)

                def broadcast_b(n, at, half, row):
                    if n >= 1:
                        pe.wait_ge(b_copied.sem, at(b_copied, 0))
                    pe.matmul(psB[:], onehot[:, row, :], bc_s[:, half, :], start=True, stop=True).then_inc(b_bc.sem, 1)

                def broadcast_c(n, at, half, row):
                    if n >= 1:
                        pe.wait_ge(weighed_s.sem, at(weighed_s, 0))
                    pe.matmul(psC[:], onehot[:, row, :], bc_s[:, 2 + half, :], start=True, stop=True).then_inc(c_bc.sem, 1)

                def add_state(n, at):
                    i = n % 2
                    pe.wait_ge(weighed_s.sem, at(weighed_s, 1))
                    for m in range(M3):
                        mm = pe.matmul(psY[:, m, :], ident[:], weighed[i][:, m, :], start=(n == 0), stop=False,
                                       skip_group_check=True)
                    mm.then_inc(summed.sem, 1)

                pe.wait_ge(split.sem, split.at(b, 5 * SETS))
                pe.wait_ge(sp_act.sem, sp_act.at(b, 2 * M3))
                pe.wait_ge(z_gate.sem, z_gate.at(b, M3))
                for n in range(-2, NS):
                    at = lambda s, k, n=n: s.at(b, n + k)
                    if n + 2 < NS:
                        broadcast_b(n + 2, lambda s, k, n=n: s.at(b, n + 2 + k), (n + 2) // 32, (n + 2) % 32)
                    if n >= 0:
                        broadcast_c(n, at, n // 32, n % 32)
                    if n >= 1:
                        add_state(n - 1, lambda s, k, n=n: s.at(b, n - 1 + k))
                add_state(NS - 1, lambda s, k: s.at(b, NS - 1 + k))
                for m in range(M3):
                    mm = pe.matmul(psY[:, m, :], diag_d[:, m, :], xc[:, m, :], start=False, stop=True, skip_group_check=True)
                mm.then_inc(summed.sem, 1)
                pe.wait_ge(gated.sem, gated.at(b, 1))
                for c in range(TC):
                    for m in range(M3):
                        mm = pe.matmul(psW[:, c // 2, (c % 2) * D:(c % 2 + 1) * D], gz[:, m, c * P:(c + 1) * P],
                                       out_w_sb[:, m, :], start=(m == 0), stop=(m == M3 - 1))
                    if c % 2:
                        mm.then_inc(outp.sem, 1)
                pe.wait_ge(n1.xn.sem, n1.xn.at(b, 2 * TC))
                transposes(n1, xr)
                pe.wait_ge(n1.T.sem, n1.T.at(b, 2 * KT))
                logits(router_w_sb, route_mm.sem)
                pe.wait_ge(route.sem, route.at(b, 8))
                for c in range(TC + 1):
                    for c1 in range(min(c, TC - 1) + 1):
                        mm = pe.matmul(psC[:, c * E:(c + 1) * E], tri[:] if c1 == c else ones[:], chosen_b[:, c1, :],
                                       start=(c1 == 0), stop=(c1 == min(c, TC - 1)))
                mm.then_inc(ranked.sem, 1)

            pe.wait_ge(tab.sem, TAB_STEPS)
            pe.wait_ge(loaded2.sem, ALL_LOADED2)

            pair = [None]

            def expert_of(s):
                return pe.value_load(table_e[0:1, bass.ds(s, 1)], min_val=0, max_val=E - 1)

            def tile_transpose(s, i, first):
                pe.wait_ge(xt_loaded[i].sem, 16 * (s // 2 + 1) if isinstance(s, int) else xt_loaded[i].at(pair[0], 32))
                if not (first and i == 0):
                    pe.wait_ge(xt_c.sem, xt_c.at(s, 0))
                for k in range(KT):
                    mm = pe.transpose(psY[0:KP, 0, k * P:(k + 1) * P], xt_in[i][:, k * KP:(k + 1) * KP], ident[:])
                mm.then_inc(xt_tr.sem, 1)

            def tile_products(s, i, first):
                e = expert_of(s)
                pe.wait_ge(xt_c.sem, xt_c.at(s, 1))
                if not first:
                    pe.wait_ge(xt_h.sem, xt_h.at(s, -1))
                h1, h2 = (psW[:, 0, :], psW[:, 1, :]) if i == 0 else (psW[:, 2, :], psC[:])
                for w, dst in ((w1_sb, h1), (w2_sb, h2)):
                    for k in range(KT):
                        mm = pe.matmul(dst, xt_T[i][:, k * P:(k + 1) * P], w[:, k, bass.ds(e * HID, HID)],
                                       start=(k == 0), stop=(k == KT - 1))
                mm.then_inc(xt_hp.sem, 1)

            def turn(s, i, first, last):
                if last is None or last >= 1:
                    tile_products(s + 1, 1 - i, first and i == 0)
                if last is None:
                    tile_transpose(s + 2, i, False)
                pe.wait_ge(xt_h.sem, xt_h.at(s, 1))
                if not (first and i == 0):
                    pe.wait_ge(xt_hc.sem, xt_hc.at(s, 0))
                for t in range(HT):
                    mm = pe.transpose(psB[:, t * P:(t + 1) * P], xt_hid[i][:, t * P:(t + 1) * P], ident[:])
                mm.then_inc(xt_htr.sem, 1)
                e = expert_of(s)
                pe.wait_ge(xt_hc.sem, xt_hc.at(s, 1))
                if not first:
                    pe.wait_ge(xt_yc.sem, xt_yc.at(s, -1))
                for t in range(HT):
                    mm = pe.matmul(psY[:, 1 + i, 0:D], xt_hT[i][:, t * P:(t + 1) * P], w3_sb[:, t, bass.ds(e * D, D)],
                                   start=(t == 0), stop=(t == HT - 1))
                mm.then_inc(xt_out.sem, 1)

            tile_transpose(0, 0, True)
            tile_transpose(1, 1, True)
            tile_products(0, 0, True)
            tile_turns(pe, turn, pair)

            pe.wait_ge(dve_set3.sem, DVE_SETS3)
            pe.wait_ge(loaded3.sem, ALL_LOADED3)
            pe.wait_ge(xt_yc.sem, NT)
            with pe.Fori(0, NB) as b:
                pe.wait_ge(n3.xn.sem, n3.xn.at(b, TC))
                transposes(n3, xn)
                pe.wait_ge(n3.T.sem, n3.T.at(b, KT))
                for w, dst in ((wq_sb, (psY[0:KP, 0, :], psY[0:KP, 1, :])), (wk_sb, (psY[0:KP, 2, :], psW[0:KP, 2, :]))):
                    for m in range(KT):
                        for k in range(KT):
                            mm = pe.matmul(dst[m], w[:, k, m * KP:(m + 1) * KP], xnT[:, k, :], start=(k == 0), stop=(k == KT - 1))
                        mm.then_inc(qkp.sem, 1)
                for c in range(TC):
                    for k in range(KT):
                        mm = pe.matmul((psB, psC)[c // 2][:, (c % 2) * D:(c % 2 + 1) * D], xnT[:, k, c * P:(c + 1) * P],
                                       wv_sb[:, k, :], start=(k == 0), stop=(k == KT - 1))
                    if c % 2:
                        mm.then_inc(vp.sem, 1)
                pe.wait_ge(q_sent.sem, q_sent.at(b, 16 * 6))
                pe.wait_ge(k_sent.sem, k_sent.at(b, 16 * 6))
                for hd in range(HEADS):
                    for c in range(TC):
                        q = hd * TC + c
                        if q >= 3:
                            pe.wait_ge(mx.sem, mx.at(b, q - 2))
                        pe.matmul(psW[:, q % 3, :], qs[0:96, hd, c * P:(c + 1) * P], ks[0:96, hd, :],
                                  start=True, stop=True).then_inc(s1.sem, 1)
                split_up = in_register(pe, nm_step.at(b, 5))
                pe.wait_ge(pool_set.sem, POOL_SETS)
                pe.wait_ge(nm_step.sem, split_up)
                nm_ps = psY[0:3 * HEADS, 0, 0:T // 2].bitcast(BF16)
                for c in range(TC):
                    mm = pe.transpose(nm_ps[:, c * P:(c + 1) * P], nm_p[:, c, :, :].rearrange("p r h -> p (r h)"), identb[:])
                mm.then_inc(nm_tr.sem, 1)
                pe.wait_ge(v_ready.sem, v_ready.at(b, TC))
                pe.wait_ge(nm_sent.sem, nm_sent.at(b, 16))

                def weighted_values(hd):
                    g, r = hd // 4, 32 * (hd % 4)
                    pe.wait_ge(pexp.sem, pexp.at(b, TC * (hd + 1)))
                    if hd == 8:
                        pe.wait_ge(og_c.sem, og_c.at(b, 1))
                    for kc in range(TC):
                        mm = pe.matmul((psB, psC)[g % 2][r:r + 32, :], vA[:, kc, hd, :], pT[hd % 2][:, kc, :],
                                       start=(kc == 0), stop=(kc == TC - 1))
                    mm.then_inc(pv.sem, 1)

                for hd in range(HEADS):
                    for c in range(TC):
                        q = hd * TC + c
                        if q >= 3:
                            pe.wait_ge(pexp.sem, pexp.at(b, q - 2))
                        pe.matmul(psW[:, q % 3, :], ks[0:99, hd, c * P:(c + 1) * P], qs[0:99, hd, :],
                                  start=True, stop=True).then_inc(s2.sem, 1)
                    if hd >= 1:
                        weighted_values(hd - 1)
                weighted_values(HEADS - 1)
                pe.wait_ge(og_c.sem, og_c.at(b, HG))
                o_bank = (psY[:, 0], psY[:, 1], psY[:, 2], psC[:])
                for c in range(TC):
                    for g in range(HG):
                        mm = pe.transpose(o_bank[c][:, g * P:(g + 1) * P], og[:, g, c * P:(c + 1) * P], ident[:])
                    mm.then_inc(og_tr.sem, 1)
                pe.wait_ge(a_norm.sem, a_norm.at(b, 2 * TC))
                transposes(n3, xn)
                pe.wait_ge(n3.T.sem, n3.T.at(b, 2 * KT))
                for c in range(TC):
                    for k in range(KT):
                        mm = pe.matmul(psY[:, c // 2, (c % 2) * D:(c % 2 + 1) * D], xnT[:, k, c * P:(c + 1) * P],
                                       wo_sb[:, k, :], start=(k == 0), stop=(k == KT - 1))
                    if c % 2:
                        mm.then_inc(ao.sem, 1)
                pe.wait_ge(n3.xn.sem, n3.xn.at(b, 2 * TC))
                transposes(n3, xn)
                pe.wait_ge(n3.T.sem, n3.T.at(b, 3 * KT))
                logits(gate_w_sb, gate_mm.sem)

                def expert_out2(e):
                    pe.wait_ge(fhid.sem, fhid.at(b, e + 1))
                    if e >= 1:
                        pe.wait_ge(facc.sem, facc.at(b, TC * e))
                    for c in range(TC):
                        mm = pe.matmul(psY[:, 1 + c // 2, (c % 2) * D:(c % 2 + 1) * D],
                                       hid[e % 2][:, c * P:(c + 1) * P], f2_sb[:, e, :], start=True, stop=True)
                    mm.then_inc(fout.sem, 1)

                for e in range(E + 1):
                    if e >= 2:
                        pe.wait_ge(fhid.sem, fhid.at(b, e - 1))
                    h2 = psW[:, 2, :] if e % 2 == 0 else psY[:, 0, :]
                    for w, dst in ((f1_sb, psW[:, e % 2, :]), (f3_sb, h2)):
                        for k in range(KT):
                            mm = pe.matmul(dst, w[:, k, e, :], xnT[:, k, :], start=(k == 0), stop=(k == KT - 1))
                    mm.then_inc(fp.sem, 1)
                    if e >= 1:
                        expert_out2(e - 1)
                expert_out2(E)


def kernel(x, L0_tok_W_emb, L0_tok_W_pos, L0_attn_in_w, L0_attn_conv_w, L0_attn_conv_b, L0_attn_xproj_w,
           L0_attn_A_log, L0_attn_dt_bias, L0_attn_D, L0_attn_out_w, L0_ffn_router_w, L0_ffn_router_b,
           L0_ffn_w1, L0_ffn_w2, L0_ffn_w3, L1_attn_W_qkv, L1_attn_b_qkv, L1_attn_W_out, L1_attn_b_out,
           L1_ffn_gate_weight, L1_ffn_gate_bias, L1_ffn_w1, L1_ffn_w2, L1_ffn_w3,
           L1_ffn_sw1, L1_ffn_sw2, L1_ffn_sw3):
    import concourse.bacc as bacc
    from concourse.bass_utils import run_bass_kernel_spmd

    W, bias = np.asarray(L1_attn_W_qkv), np.asarray(L1_attn_b_qkv)
    by_tile = lambda v, p=P: np.asarray(v).reshape(-1, p).T
    ffn = lambda w, s: np.concatenate([np.asarray(w), np.asarray(s)[None]], 0).transpose(0, 2, 1)
    arrays = {
        "tok": np.asarray(x).reshape(NB * TC, P).T,
        "emb": np.asarray(L0_tok_W_emb).T,
        "pos": L0_tok_W_pos, "in_w": L0_attn_in_w, "conv_w": np.asarray(L0_attn_conv_w).reshape(DI, TAPS),
        "conv_b": by_tile(L0_attn_conv_b), "xproj_w": L0_attn_xproj_w,
        "xproj_dt": by_tile(np.asarray(L0_attn_xproj_w)[:, 2 * NS]), "a_log": L0_attn_A_log,
        "dt_bias": by_tile(L0_attn_dt_bias), "d_skip": by_tile(L0_attn_D), "out_w": L0_attn_out_w,
        "router_w": L0_ffn_router_w, "router_b": L0_ffn_router_b,
        "w1": L0_ffn_w1, "w2": L0_ffn_w2, "w3": L0_ffn_w3,
        "wq": W[:, 0:D], "wk": W[:, D:2 * D], "wv": W[:, 2 * D:],
        "bq": by_tile(bias[0:D], KP), "bk": by_tile(bias[D:2 * D], KP), "bv": bias[2 * D:],
        "wo": L1_attn_W_out, "bo": L1_attn_b_out,
        "gate_w": np.asarray(L1_ffn_gate_weight).T, "gate_b": L1_ffn_gate_bias,
        "f1": ffn(L1_ffn_w1, L1_ffn_sw1), "f3": ffn(L1_ffn_w3, L1_ffn_sw3), "f2": ffn(L1_ffn_w2, L1_ffn_sw2),
    }
    arrays = {k: np.ascontiguousarray(a) for k, a in arrays.items()}
    nc = bacc.Bacc("TRN2", target_bir_lowering=False, num_devices=1)
    args = [nc.dram_tensor(k, a.shape, mybir.dt.from_np(a.dtype), kind="ExternalInput").ap()
            for k, a in arrays.items()]
    out = nc.dram_tensor("y", (NB, T, D), F32, kind="ExternalOutput").ap()
    tower(nc, *args, out)
    r = run_bass_kernel_spmd(nc, [arrays], core_ids=[0])
    return r.results[0]["y"]
```

```python
from contextlib import ExitStack

import numpy as np

import concourse.bass as bass
from concourse import mybir

F32 = mybir.dt.float32
BF16 = mybir.dt.bfloat16
I32 = mybir.dt.int32
U32 = mybir.dt.uint32
ALU = mybir.AluOpType
ACT = mybir.ActivationFunctionType
AX = mybir.AxisListType

P = 128
NB = 16
T = 512
TC = T // P
D = 192
KP, KT = 96, 2
DI = 384
M3 = DI // P
NS = 64
TAPS = 4
SETS = 4
E = 8
HID = 512
HT = HID // P
ROWS = NB * T + P
AHEAD = 4
NT = NB * TC + E
INTER = 128
HEADS, HD = 12, 16
HPG, HG = 4, 3
EPS = 1e-5
U8 = 8
RING = 4

LAST = NB


class Signal:

    def __init__(self, sem, per):
        self.sem, self.per = sem, per

    def at(self, b, n):
        return b * self.per + n


EARLY_HEADS = 3
EARLY_EXPERT = E + 1 - EARLY_HEADS * TC // 2
MAXIMA_AFTER = {0: 1, 4: 2}


def in_register(eng, value):
    return value if isinstance(value, int) else eng.to_reg(value)


PRODUCTS = ((0, 0), (0, 1), (1, 0), (1, 1), (0, 2), (2, 0))


def tower(nc, tok, emb, pos, in_w, conv_w, conv_b, xproj_w, xproj_dt, a_log, dt_bias, d_skip, out_w,
          router_w, router_b, w1, w2, w3, wq, wk, wv, bq, bk, bv, wo, bo,
          gate_w, gate_b, f1, f3, f2, out):
    ctx = ExitStack()
    with ctx:
        def alloc(scope):
            return lambda name, shape, dt=F32: scope.enter_context(nc.sbuf_tensor(name, shape, dt))

        def ps(name, shape, dt=F32):
            return ctx.enter_context(nc.psum_tensor(name, shape, dt))

        def sig(name, per):
            return Signal(ctx.enter_context(nc.semaphore(name)), per)

        h_dram = nc.dram_tensor("h_dram", (NB + 1, T, D), F32, kind="Internal").ap()
        x_sorted = nc.dram_tensor("x_sorted", (E * ROWS + P, D + 1), F32, kind="Internal").ap()
        y_tok = nc.dram_tensor("y_tok", (NB + 1, T, D), F32, kind="Internal").ap()

        y_rows = y_tok.rearrange("b t d -> (b t) d")
        parts_dram = nc.dram_tensor("parts_dram", (2, 3, D, T), BF16, kind="Internal").ap()
        nm_dram = nc.dram_tensor("nm_dram", (HG, 3 * HPG, T), BF16, kind="Internal").ap()

        sb = alloc(ctx)
        ident = sb("ident", [P, P])
        neg_half = sb("neg_half", [P, TC])
        blank = sb("blank", [P, D + 1])
        prob_all = sb("prob_all", [P, (NB + 1) * TC])
        count = sb("count", [P, E])
        before = sb("before", [P, E, E])
        table_r = sb("table_r", [1, NT], I32)
        table_e = sb("table_e", [1, NT], I32)
        tail = sb("tail", [1, E], I32)
        no_number = sb("no_number", [P, 1], I32)
        h = sb("h", [P, TC, D])
        stats = sb("stats", [P, TC, 6])
        stat_count = sb("stat_count", [P, 1])
        mv = sb("mv", [P, TC, 2])
        vare = sb("vare", [P, TC])
        rstd = sb("rstd", [P, TC])
        xn = sb("xn", [P, TC, D])
        xnT = sb("xnT", [KP, KT, T])
        w3_sb = sb("w3_sb", [P, HT, E * D])

        scope1 = ExitStack()
        sb = alloc(scope1)
        onehot = sb("onehot", [96, 32, P], BF16)
        tri = sb("tri", [P, P], BF16)
        ones = sb("ones", [P, P], BF16)
        idx_all = sb("idx_all", [P, (NB + 2) * TC], I32)
        pos_sb = sb("pos_sb", [P, TC, D])
        in_w_sb = sb("in_w_sb", [KP, KT, 2 * DI])
        conv_w_sb = sb("conv_w_sb", [P, M3, TAPS])
        conv_b_sb = sb("conv_b_sb", [P, M3])
        conv_wh = sb("conv_wh", [P, M3, TAPS])
        conv_bh = sb("conv_bh", [P, M3])
        xproj_bc = sb("xproj_bc", [P, M3, SETS, 96])
        xproj_q = sb("xproj_q", [P, M3, 1])
        xproj_qr = sb("xproj_qr", [P, M3, P])
        a_log_sb = sb("a_log_sb", [P, M3, NS])
        a_exp = sb("a_exp", [P, M3, NS])
        a_neg = sb("a_neg", [P, M3, NS])
        dt_bias_sb = sb("dt_bias_sb", [P, M3])
        d_skip_sb = sb("d_skip_sb", [P, M3])
        diag_d = sb("diag_d", [P, M3, P])
        out_w_sb = sb("out_w_sb", [P, M3, D])
        router_w_sb = sb("router_w_sb", [KP, KT, E])
        router_b_sb = sb("router_b_sb", [P, E])
        falling_i = sb("falling_i", [P, E], I32)
        falling = sb("falling", [P, E])
        idx = sb("idx", [P, TC], I32)
        rows_in = sb("rows_in", [P, TC, D])
        xr = sb("xr", [P, TC, D + 1])
        token = sb("token", [P, TC])
        token_i = sb("token_i", [P, TC], I32)
        xs = sb("xs", [P, M3, TAPS - 1 + T])
        xc = sb("xc", [P, M3, T])
        gz = sb("gz", [P, M3, T])
        gz_next = sb("gz_next", [P, M3, T])
        h_next = sb("h_next", [P, TC, D])
        relu_x = sb("relu_x", [P, M3, T])
        work_a = sb("work_a", [P, M3, T])
        work_b = sb("work_b", [P, M3, T])
        correction = sb("correction", [P, M3, T])
        rest = sb("rest", [64, 2, T])
        dt = sb("dt", [P, M3, T])
        u = sb("u", [P, M3, T])
        bc_s = sb("bc_s", [96, SETS, T], BF16)
        decay = [sb(f"decay{i}", [P, M3, T]) for i in range(2)]
        drive = [sb(f"drive{i}", [P, M3, T]) for i in range(2)]
        state = [sb(f"state{i}", [P, M3, T]) for i in range(RING)]
        b_sb = [sb(f"b_sb{i}", [P, T]) for i in range(2)]
        logit = sb("logit", [P, TC, E])
        top = sb("top", [P, TC])
        tie = sb("tie", [P, TC, E])
        rev = sb("rev", [P, TC, E])
        first = sb("first", [P, TC])
        chosen = sb("chosen", [P, TC, E])
        chosen_b = sb("chosen_b", [P, TC, E], BF16)
        soft = sb("soft", [P, TC, E])
        soft_e = sb("soft_e", [P, TC, E])
        soft_s = sb("soft_s", [P, TC])
        ahead = sb("ahead", [P, TC, E])
        place = sb("place", [P, TC])
        region = sb("region", [P, TC])
        slot = sb("slot", [P, TC], I32)
        flat = lambda t: t[:].rearrange("p m t -> p (m t)")
        wide = lambda t, o=0: flat(t)[:, o:o + NT * E].rearrange("p (s e) -> p s e", e=E)
        t_full, t_begin, t_end = b_sb[0][:, 0:E], b_sb[0][:, E:2 * E], b_sb[0][:, 2 * E:3 * E]
        t_off, t_tail = b_sb[0][:, 3 * E:4 * E], b_sb[0][:, 4 * E:5 * E]
        t_pre = b_sb[0][:, 64:128].rearrange("p (i j) -> p i j", i=E)
        t_regions = b_sb[0][:, 128:136]
        t_row, t_exp, t_valid = b_sb[0][:, 192:192 + NT], b_sb[0][:, 288:288 + NT], b_sb[0][:, 384:384 + NT]
        t_num_i = u[:, 0, 0:NT].bitcast(I32)
        t_num = u[:, 1, 0:NT]
        t_cmp, t_a, t_b = wide(state[0]), wide(drive[0]), wide(drive[1])
        scope1.close()

        scope3 = ctx.enter_context(ExitStack())
        sb = alloc(scope3)
        wq_sb = sb("wq_sb", [KP, KT, D])
        wk_sb = sb("wk_sb", [KP, KT, D])
        wv_sb = sb("wv_sb", [KP, KT, D])
        bqk_sb = sb("bqk_sb", [KP, 2, KT])
        bv_sb = sb("bv_sb", [P, D])
        wo_sb = sb("wo_sb", [KP, KT, D])
        bo_sb = sb("bo_sb", [P, D])
        gate_w_sb = sb("gate_w_sb", [KP, KT, E])
        gate_b_sb = sb("gate_b_sb", [P, E])
        f1_sb = sb("f1_sb", [KP, KT, E + 1, INTER])
        f3_sb = sb("f3_sb", [KP, KT, E + 1, INTER])
        f2_sb = sb("f2_sb", [INTER, E + 1, D])

        scope2 = ExitStack()
        sb = alloc(scope2)
        w1_sb = sb("w1_sb", [KP, KT, E * HID])
        w2_sb = sb("w2_sb", [KP, KT, E * HID])
        xt_in = [sb(f"xt_in{i}", [P, D + 1]) for i in range(AHEAD)]
        xt_num = [sb(f"xt_num{i}", [P, 1], I32) for i in range(AHEAD)]
        xt_T = [sb(f"xt_T{i}", [KP, KT * P]) for i in range(2)]
        xt_th = [sb(f"xt_th{i}", [P, HID]) for i in range(2)]
        xt_sl = sb("xt_sl", [P, HID])
        xt_hid = [sb(f"xt_hid{i}", [P, HID]) for i in range(2)]
        xt_hT = [sb(f"xt_hT{i}", [P, HT * P]) for i in range(2)]
        xt_y = [sb(f"xt_y{i}", [P, D]) for i in range(2)]
        scope2.close()

        sb = alloc(scope3)
        h_in = sb("h_in", [P, TC, D])
        xqT = sb("xqT", [KP, KT, T])
        y_in = sb("y_in", [P, TC, D])
        prob_cur = sb("prob_cur", [P, TC])
        y_b = sb("y_b", [P, TC, D], BF16)
        parts = sb("parts", [KP, 3, KT, T], BF16)
        qs = sb("qs", [99, HEADS, T], BF16)
        ks = sb("ks", [99, HEADS, T], BF16)
        vA = sb("vA", [P, TC, HEADS, 32])
        pT = [sb(f"pT{i}", [P, TC, T]) for i in range(2)]
        qk_f = sb("qk_f", [KP, KT, T])
        qk_r = sb("qk_r", [KP, KT, T])
        neg_max = sb("neg_max", [P, TC, HEADS])
        nm_r = sb("nm_r", [P, TC, HEADS])
        nm_p = sb("nm_p", [P, TC, HG, 3, HPG], BF16)
        nm_T = sb("nm_T", [3 * HPG, T], BF16)
        identb = sb("identb", [P, P], BF16)
        og = sb("og", [P, HG, T])
        r_sum = sb("r_sum", [P, TC, HEADS])
        cw = sb("cw", [P, TC, E + 1])
        gate_s = sb("gate_s", [P, TC, E])
        gate_v = sb("gate_v", [P, TC, E])
        group_v = sb("group_v", [P, TC, 4])
        group_on = sb("group_on", [P, TC, 4])
        masked = sb("masked", [P, TC, E])
        cmp_gt = sb("cmp_gt", [P, TC, E, E])
        cmp_eq = sb("cmp_eq", [P, TC, E, E])
        rank = sb("rank", [P, TC, E])
        w_sum = sb("w_sum", [P, TC])
        w_inv = sb("w_inv", [P, TC])
        th = sb("th", [P, 3, T])
        sl = sb("sl", [P, T])
        hid = [sb(f"hid{i}", [P, T]) for i in range(2)]

        psY = ps("psY", [P, M3, T])
        psW = ps("psW", [P, 3, T])
        psB = ps("psB", [P, T])
        psC = ps("psC", [P, T])

        loaded = sig("loaded", 0)
        loaded2 = sig("loaded2", 0)
        loaded3 = sig("loaded3", 0)
        filled = sig("filled", 0)
        pool_set = sig("pool_set", 0)
        dve_set = sig("dve_set", 0)
        dve_set3 = sig("dve_set3", 0)
        act_set = sig("act_set", 0)

        class Norm:

            def __init__(self, name, layers, calls):
                self.step = sig(name + "_step", layers * (2 * TC + 2))
                self.rstd = sig(name + "_rstd", layers)
                self.xn = sig(name + "_xn", layers * TC)
                self.tr = sig(name + "_tr", calls * KT)
                self.T = sig(name + "_T", calls * KT)

        n1, n2, n3, n4 = Norm("n1", 1, 1), Norm("n2", 1, 1), Norm("n3", 1, 1), Norm("n4", 1, 2)
        idx_ready = sig("idx_ready", 1)
        gathered = sig("gathered", 16 * TC)
        h_ready = sig("h_ready", 1)
        h_copied = sig("h_copied", 1)
        proj = sig("proj", 2 * M3)
        xs_ready = sig("xs_ready", M3)
        z_tanh = sig("z_tanh", M3)
        z_gate = sig("z_gate", M3)
        conv_first = sig("conv_first", M3)
        conv = sig("conv", M3 * (TAPS - 1))
        conv_tanh = sig("conv_tanh", M3)
        xc_ready = sig("xc_ready", M3)
        xp = sig("xp", SETS + 1)
        first_part_s = sig("first_part", SETS)
        split = sig("split", SETS * 4)
        sp_act = sig("sp_act", 4 * M3)
        gz_ready = sig("gz_ready", 1)
        dt_step = sig("dt_step", 5)
        b_bc = sig("b_bc", NS)
        b_copied = sig("b_copied", NS)
        c_bc = sig("c_bc", NS)
        decayed = sig("decayed", NS)
        driven = sig("driven", NS)
        scanned = sig("scanned", NS)
        weighed_s = sig("weighed_s", NS)
        summed = sig("summed", NS)
        gated = sig("gated", 1)
        outp = sig("outp", 2)
        resid1 = sig("resid1", 2)
        route_mm = sig("route_mm", 1)
        route = sig("route", 16)
        route_exp = sig("route_exp", 1)
        ranked = sig("ranked", 1)
        numbered = sig("numbered", 2)
        h_free = sig("h_free", 1)
        xr_free = sig("xr_free", 1)
        h_free3 = sig("h_free3", 1)
        h_saved = sig("h_saved", 16)
        x_saved = sig("x_saved", 16 * TC)
        tab = sig("tab", 0)
        xt_loaded = [sig(f"xt_loaded{i}", 16) for i in range(AHEAD)]
        xt_tr = sig("xt_tr", 1)
        xt_c = sig("xt_c", 1)
        xt_hp = sig("xt_hp", 1)
        xt_tanh = sig("xt_tanh", 1)
        xt_silu = sig("xt_silu", 1)
        xt_h = sig("xt_h", 1)
        xt_htr = sig("xt_htr", 1)
        xt_hc = sig("xt_hc", 1)
        xt_out = sig("xt_out", 1)
        xt_yc = sig("xt_yc", 1)
        xt_num_c = sig("xt_num_c", 1)
        xt_saved = sig("xt_saved", 16)
        h_back = sig("h_back", 16)
        y_back = sig("y_back", 16)
        resid2 = sig("resid2", 2 + TC)
        qkp = sig("qkp", 4)
        vp = sig("vp", 2)
        qk_step = sig("qk_step", 2 * 7)
        parts_out = sig("parts_out", 16 * 2)
        q_sent = sig("q_sent", 16 * 6)
        k_sent = sig("k_sent", 16 * 6)
        v_ready = sig("v_ready", TC)
        s1 = sig("s1", HEADS * TC)
        mx = sig("mx", HEADS * TC)
        nm_step = sig("nm_step", 5 * HG)
        nm_tr = sig("nm_tr", HG)
        nm_c = sig("nm_c", HG)
        nm_out = sig("nm_out", 16 * HG)
        nm_sent = sig("nm_sent", 16 * HG)
        s2 = sig("s2", HEADS * TC)
        pexp = sig("pexp", HEADS * TC)
        pv = sig("pv", HEADS)
        og_c = sig("og_c", HG)
        og_tr = sig("og_tr", TC)
        a_norm = sig("a_norm", 2 * TC)
        ao = sig("ao", 2)
        resid3 = sig("resid3", 3)
        gate_mm = sig("gate_mm", 1)
        gate_tanh = sig("gate_tanh", 1)
        gate = sig("gate", 23)
        fp = sig("fp", E + 1)
        ftanh = sig("ftanh", E + 1)
        fsilu = sig("fsilu", E + 1)
        fhid = sig("fhid", E + 1)
        fout = sig("fout", E + 1)
        facc = sig("facc", (E + 1) * TC)
        stored = sig("stored", 16)

        n_loads, n_loads3 = [0], [0]
        FILLS = 3
        POOL_SETS = 18
        DVE_SETS = 16
        DVE_SETS3 = 6
        TAB_STEPS = 25
        block = ctx.enter_context(nc.Block())

        def tile_turns(eng, turn, group):
            for s in range(AHEAD):
                turn(s, s, None)
            with eng.Fori(1, NT // AHEAD - 1) as j:
                group[0] = j
                for i in range(AHEAD):
                    turn(j * AHEAD + i, i, None)
            for s in range(NT - AHEAD, NT):
                turn(s, s % AHEAD, NT - 1 - s)

        def early(s, n):
            return isinstance(s, int) and s < n

        def loaded_upto(s, i, group, more):
            return 16 * (s // AHEAD + 1) if isinstance(s, int) else xt_loaded[i].at(group[0], 16 + 16 * more)

        def scores_bank(hd, c):
            bank = (hd * TC + c) % 2
            return (psB, psC)[bank][:] if hd < EARLY_HEADS else psY[:, bank, :]

        def early_tiles(e):
            q = 2 * (e - EARLY_EXPERT)
            return [divmod(i, TC) for i in (q, q + 1)] if e >= EARLY_EXPERT else []

        Q_BANKS = (psY[0:KP, 0, :], psY[0:KP, 1, :])
        K_BANKS = (psB[0:KP, :], psC[0:KP, :])
        V_BANKS = (psY[:, 2, :], psW[:, 2, :])
        XP_B0, XP_DT, XP_C0, XP_B1, XP_C1 = range(1, SETS + 2)

        SPLITS = ((0, psW[0:96, 0, :], XP_B0), (2, psW[0:96, 1, :], XP_C0),
                  (1, psW[0:96, 0, :], XP_B1), (3, psW[0:96, 1, :], XP_C1))

        @block.sync
        def _(sp):
            def load(dst, src):
                sp.dma_start(dst, src).then_inc(loaded.sem, 16)
                n_loads[0] += 1

            load(idx_all[:, 0:NB * TC], tok)
            load(pos_sb[:], pos.rearrange("(c p) d -> p c d", p=P))
            load(in_w_sb[:], in_w.rearrange("(k p) m -> p k m", p=KP))
            load(conv_w_sb[:], conv_w.rearrange("(m p) k -> p m k", p=P))
            load(a_log_sb[:], a_log.rearrange("(m p) n -> p m n", p=P))
            for vec, dst in ((conv_b, conv_b_sb), (dt_bias, dt_bias_sb), (d_skip, d_skip_sb)):
                load(dst[:], vec)
            xproj_v = xproj_w.rearrange("(m p) k -> p m k", p=P)
            for s in range(SETS):
                for r in range(3):
                    load(xproj_bc[:, :, s, 32 * r:32 * r + 32], xproj_v[:, :, 32 * s:32 * s + 32])
            load(xproj_q[:, :, 0], xproj_dt)
            load(out_w_sb[:], out_w.rearrange("(m p) d -> p m d", p=P))
            load(router_w_sb[:], router_w.rearrange("(k p) e -> p k e", p=KP))
            load(router_b_sb[:], router_b.rearrange("(o n) -> o n", o=1).to_broadcast([P, E]))
            sp.wait_ge(pool_set.sem, POOL_SETS)
            sp.dma_start(h_dram[LAST].rearrange("(c p) d -> p c d", p=P),
                         blank[:, 0:D].unsqueeze(1).to_broadcast([P, TC, D])).then_inc(filled.sem, 16)
            sp.dma_start(y_tok[LAST].rearrange("(c p) d -> p c d", p=P),
                         blank[:, 0:D].unsqueeze(1).to_broadcast([P, TC, D])).then_inc(filled.sem, 16)
            sp.dma_start(x_sorted[E * ROWS:E * ROWS + P, :], blank[:]).then_inc(filled.sem, 16)

            sp.wait_ge(filled.sem, 16 * FILLS)
            sp.sem_inc(h_free.sem, 1)
            sp.sem_inc(xr_free.sem, 1)
            with sp.Fori(0, NB) as b:
                sp.wait_ge(resid1.sem, resid1.at(b, 2))
                sp.dma_start(h_dram[bass.ds(b, 1)].rearrange("o (c p) d -> p (o c) d", p=P), h[:]).then_inc(h_saved.sem, 16)
                sp.wait_ge(h_saved.sem, h_saved.at(b, 16))
                sp.sem_inc(h_free.sem, 1)
                sp.wait_ge(x_saved.sem, x_saved.at(b, 16 * TC))
                sp.sem_inc(xr_free.sem, 1)

            sp.wait_ge(tab.sem, TAB_STEPS)
            sp.wait_ge(x_saved.sem, 16 * TC * LAST)
            sp.wait_ge(h_saved.sem, 16 * LAST)

            for w, dst in ((w1, w1_sb), (w2, w2_sb)):
                for k in range(KT):
                    sp.dma_start(dst[:, k, :].rearrange("p (e m) -> p e m", e=E),
                                 w[:, k * KP:(k + 1) * KP, :].rearrange("e p m -> p e m")).then_inc(loaded2.sem, 16)
            for t in range(HT):
                sp.dma_start(w3_sb[:, t, :].rearrange("p (e d) -> p e d", e=E),
                             w3[:, t * P:(t + 1) * P, :].rearrange("e p d -> p e d")).then_inc(loaded2.sem, 16)

            def load3(dst, src):
                sp.dma_start(dst, src).then_inc(loaded3.sem, 16)
                n_loads3[0] += 1

            for e in range(E):
                row = sp.value_load(tail[0:1, e:e + 1], min_val=e * ROWS, max_val=e * ROWS + NB * T)
                sp.dma_start(x_sorted[bass.ds(row, P), :], blank[:]).then_inc(filled.sem, 16)
            for vec, dst in ((bv, bv_sb), (bo, bo_sb), (gate_b, gate_b_sb)):
                load3(dst[:], vec.rearrange("(o n) -> o n", o=1).to_broadcast([P, vec.shape[0]]))
            for w, dst in ((wq, wq_sb), (wk, wk_sb), (wv, wv_sb), (wo, wo_sb), (gate_w, gate_w_sb)):
                load3(dst[:], w.rearrange("(k p) m -> p k m", p=KP))
            load3(bqk_sb[:, 0, :], bq)
            load3(bqk_sb[:, 1, :], bk)
            for w, dst in ((f1, f1_sb), (f3, f3_sb)):
                for k in range(KT):
                    load3(dst[:, k], w[:, k * KP:(k + 1) * KP, :].rearrange("e p i -> p e i"))
            load3(f2_sb[:], f2.rearrange("e i d -> i e d"))
            sp.wait_ge(filled.sem, 16 * (FILLS + E))

            def load_tile(s, i):
                row = sp.value_load(table_r[0:1, bass.ds(s, 1)], min_val=0, max_val=E * ROWS)
                if not early(s, AHEAD):
                    sp.wait_ge(xt_tr.sem, xt_tr.at(s, 1 - AHEAD))
                    sp.wait_ge(xt_num_c.sem, xt_num_c.at(s, 1 - AHEAD))
                sp.dma_start(xt_in[i][:], x_sorted[bass.ds(row, P), :]).then_inc(xt_loaded[i].sem, 16)

            def turn(s, i, last):
                if last is None:
                    load_tile(s + AHEAD, i)

            for s in range(AHEAD):
                load_tile(s, s)
            tile_turns(sp, turn, [None])
            sp.wait_ge(xt_saved.sem, 16 * NT)

            def fetch(b):
                sp.dma_start(h_in[:], h_dram[bass.ds(b, 1)].rearrange("o (c p) d -> p (o c) d", p=P)).then_inc(h_back.sem, 16)
                sp.dma_start(y_in[:], y_tok[bass.ds(b, 1)].rearrange("o (c p) d -> p (o c) d", p=P)).then_inc(y_back.sem, 16)

            def save_parts(b, which):
                sp.wait_ge(qk_step.sem, qk_step.at(b, 7 * which + 7))
                sp.dma_start(parts_dram[which].rearrange("r (k p) t -> p (r k) t", p=KP),
                             parts[:].rearrange("p r k t -> p (r k) t")).then_inc(parts_out.sem, 16)

            def lay_out_parts(b):
                sp.wait_ge(parts_out.sem, parts_out.at(b, 16 * 2))
                for which, (dst, sent) in enumerate(((qs, q_sent), (ks, k_sent))):
                    for j, pair in enumerate(PRODUCTS):
                        sp.dma_start(dst[HD * j:HD * (j + 1), :, :],
                                     parts_dram[which, pair[which]].rearrange("(h d) t -> d h t", d=HD)).then_inc(sent.sem, 16)

            fetch(0)
            sp.sem_inc(h_free3.sem, 1)
            for which in range(2):
                save_parts(0, which)
            lay_out_parts(0)
            with sp.Fori(0, NB) as b:
                for g in range(HG):
                    if g == HG - 1:
                        sp.wait_ge(resid3.sem, resid3.at(b, 1))
                        fetch(b + 1)
                    sp.wait_ge(nm_c.sem, nm_c.at(b, g + 1))
                    sp.dma_start(nm_dram[g], nm_T[:]).then_inc(nm_out.sem, 16)
                    sp.wait_ge(nm_out.sem, nm_out.at(b, 16 * (g + 1)))
                    sp.dma_start(qs[96:99, HPG * g:HPG * (g + 1), :],
                                 nm_dram[g].rearrange("(r h) t -> r h t", r=3)).then_inc(nm_sent.sem, 16)
                for which in range(2):
                    save_parts(b + 1, which)
                sp.wait_ge(s2.sem, s2.at(b, HEADS * TC))
                lay_out_parts(b + 1)
                sp.wait_ge(facc.sem, facc.at(b, (E + 1) * TC))
                sp.dma_start(out[bass.ds(b, 1)].rearrange("o (c p) d -> p (o c) d", p=P), h[:]).then_inc(stored.sem, 16)
                sp.wait_ge(stored.sem, stored.at(b, 16))
                sp.sem_inc(h_free3.sem, 1)
            sp.wait_ge(stored.sem, 16 * LAST)
            sp.wait_ge(h_back.sem, 16 * (LAST + 1))
            sp.wait_ge(y_back.sem, 16 * (LAST + 1))
            sp.wait_ge(parts_out.sem, 16 * 2 * (LAST + 1))
            sp.wait_ge(q_sent.sem, 16 * 6 * (LAST + 1))
            sp.wait_ge(k_sent.sem, 16 * 6 * (LAST + 1))
            sp.wait_ge(nm_out.sem, 16 * HG * LAST)

        ALL_LOADED = 16 * n_loads[0]
        ALL_LOADED2 = 16 * (2 * KT + HT)
        ALL_LOADED3 = 16 * n_loads3[0]

        @block.gpsimd
        def _(pool):
            pool.memset(ident[:], 0.0).then_inc(pool_set.sem, 1)
            pool.memset(onehot[:], 0.0).then_inc(pool_set.sem, 1)
            pool.memset(before[:], 1.0).then_inc(pool_set.sem, 1)
            pool.memset(tri[:], 1.0).then_inc(pool_set.sem, 1)
            pool.memset(neg_half[:], -0.5).then_inc(pool_set.sem, 1)
            pool.memset(blank[:, 0:D], 0.0).then_inc(pool_set.sem, 1)
            pool.iota(blank[:, D:D + 1].bitcast(I32), pattern=[[0, 1]], base=NB * T, channel_multiplier=1).then_inc(pool_set.sem, 1)
            pool.iota(token_i[:], pattern=[[P, TC]], base=0, channel_multiplier=1).then_inc(pool_set.sem, 1)
            pool.iota(falling_i[:], pattern=[[-1, E]], base=E, channel_multiplier=0).then_inc(pool_set.sem, 1)
            pool.wait_ge(pool_set.sem, 9)
            pool.affine_select(out=ident[:], in_=ident[:], compare_op=ALU.not_equal, fill=1.0, base=0,
                               pattern=[[-1, P]], channel_multiplier=1).then_inc(pool_set.sem, 1)
            pool.affine_select(out=before[:], in_=before[:], compare_op=ALU.is_gt, fill=0.0, base=0,
                               pattern=[[1, E], [-1, E]], channel_multiplier=0).then_inc(pool_set.sem, 1)
            pool.affine_select(out=tri[:], in_=tri[:], compare_op=ALU.is_gt, fill=0.0, base=0,
                               pattern=[[1, P]], channel_multiplier=-1).then_inc(pool_set.sem, 1)
            for r in range(3):
                pool.wait_ge(pool_set.sem, 12 + r)
                pool.affine_select(out=onehot[:], in_=onehot[:], compare_op=ALU.not_equal, fill=1.0,
                                   base=-32 * r, pattern=[[-1, 32], [0, P]],
                                   channel_multiplier=1).then_inc(pool_set.sem, 1)
            pool.tensor_copy(falling[:], falling_i[:]).then_inc(pool_set.sem, 1)
            pool.tensor_copy(token[:], token_i[:]).then_inc(pool_set.sem, 1)
            pool.memset(no_number[:], 0).then_inc(pool_set.sem, 1)
            pool.wait_ge(loaded.sem, ALL_LOADED)
            pool.wait_ge(pool_set.sem, POOL_SETS)
            pool.wait_ge(dve_set.sem, DVE_SETS)

            def rstd_of(norm, b, l):
                pool.wait_ge(norm.step.sem, norm.step.at(b, (2 * TC + 2) * (l + 1)))
                pool.tensor_tensor(rstd[:], vare[:], neg_half[:], ALU.pow).then_inc(norm.rstd.sem, 1)

            def gather_embedding(b, chunk):
                if chunk == 0:
                    if not (isinstance(b, int) and b == 0):
                        pool.wait_ge(h_ready.sem, h_ready.at(b, 0))
                        pool.wait_ge(gathered.sem, gathered.at(b, 0))
                    pool.tensor_copy(idx[:], idx_all[:, bass.ds(b * TC, TC)]).then_inc(idx_ready.sem, 1)
                    copied = in_register(pool, idx_ready.at(b, 1))
                    pool.wait_ge(pool_set.sem, POOL_SETS)
                    pool.wait_ge(idx_ready.sem, copied)
                pool.indirect_dma_start(
                    out=rows_in[:, chunk, :], out_offset=None, in_=emb,
                    in_offset=bass.IndirectOffsetOnAxis(ap=idx[:, chunk:chunk + 1].bitcast(U32), axis=0),
                ).then_inc(gathered.sem, 16)

            def drive_step(n, at):
                i = n % 2
                pool.wait_ge(b_copied.sem, at(b_copied, 1))
                if n >= 2:
                    pool.wait_ge(scanned.sem, at(scanned, -1))
                pool.tensor_tensor(drive[i][:], u[:], b_sb[i][:].unsqueeze(1).to_broadcast([P, M3, T]),
                                   ALU.mult).then_inc(driven.sem, 1)

            def softplus_sums(b):
                pool.wait_ge(dt_step.sem, dt_step.at(b, 1))
                pool.tensor_tensor(correction[:], work_b[:], correction[:], ALU.subtract).then_inc(dt_step.sem, 1)
                pool.wait_ge(sp_act.sem, sp_act.at(b, 4 * M3))
                pool.tensor_tensor(relu_x[:], relu_x[:], work_a[:], ALU.add).then_inc(dt_step.sem, 1)

            def first_drives(b):
                pool.wait_ge(dt_step.sem, dt_step.at(b, 5))
                for n in range(2):
                    drive_step(n, lambda s, k, n=n: s.at(b, n + k))

            for c in range(TC):
                gather_embedding(0, c)
            rstd_of(n1, 0, 0)
            softplus_sums(0)
            for c in range(TC):
                gather_embedding(1, c)
            first_drives(0)
            drive_step(2, lambda s, k: s.at(0, 2 + k))
            with pool.Fori(0, NB) as b:
                for n in range(3, 2 * U8):
                    drive_step(n, lambda s, k, n=n: s.at(b, n + k))
                    if n == 13:
                        rstd_of(n1, b + 1, 0)
                    elif 11 <= n < 16:
                        gather_embedding(b + 2, n - 11 if n < 13 else n - 12)
                with pool.Fori(2, NS // U8) as j:
                    for n in range(U8):
                        drive_step(n + U8, lambda s, k, n=n: s.at(b, n + k) + j * U8)
                softplus_sums(b + 1)
                first_drives(b + 1)
                rstd_of(n2, b, 0)
                drive_step(2, lambda s, k: s.at(b + 1, 2 + k))
                pool.wait_ge(numbered.sem, numbered.at(b, 1))
                placed = in_register(pool, route.at(b, 15))
                pool.wait_ge(pool_set.sem, POOL_SETS)
                pool.wait_ge(route.sem, placed)
                for c in range(TC):
                    pool.indirect_dma_start(
                        out=x_sorted, out_offset=bass.IndirectOffsetOnAxis(ap=slot[:, c:c + 1].bitcast(U32), axis=0),
                        in_=xr[:, c, :], in_offset=None).then_inc(x_saved.sem, 16)
            pool.wait_ge(gathered.sem, 16 * TC * (LAST + 2))

            group = [None]

            def copy_numbers(s, i, more):
                pool.wait_ge(xt_loaded[i].sem, loaded_upto(s, i, group, more))
                if not early(s, AHEAD):
                    pool.wait_ge(xt_saved.sem, xt_saved.at(s, 16 * (1 - AHEAD)))
                pool.tensor_tensor(xt_num[i][:], xt_in[i][:, D:D + 1].bitcast(I32), no_number[:], ALU.add).then_inc(xt_num_c.sem, 1)

            def turn(s, i, last):
                if last is None or last >= 2:
                    copy_numbers(s + 2, (i + 2) % AHEAD, (i + 2) // AHEAD)
                done = in_register(pool, xt_yc.at(s, 1))
                left = None if early(s, 1) else in_register(pool, xt_saved.at(s, 0))
                pool.wait_ge(pool_set.sem, POOL_SETS)
                pool.wait_ge(xt_num_c.sem, done)
                if left is not None:
                    pool.wait_ge(xt_saved.sem, left)
                pool.wait_ge(xt_yc.sem, done)
                pool.indirect_dma_start(
                    out=y_rows, out_offset=bass.IndirectOffsetOnAxis(ap=xt_num[i][:].bitcast(U32), axis=0),
                    in_=xt_y[i % 2][:], in_offset=None).then_inc(xt_saved.sem, 16)

            pool.wait_ge(tab.sem, TAB_STEPS)
            for s in range(2):
                copy_numbers(s, s, 0)
            tile_turns(pool, turn, group)

            pool.wait_ge(xt_saved.sem, 16 * NT)
            rstd_of(n3, 0, 0)
            with pool.Fori(0, NB) as b:
                rstd_of(n3, b + 1, 0)
                rstd_of(n4, b, 0)

        @block.scalar
        def _(act):
            act.wait_ge(loaded.sem, ALL_LOADED)
            act.activation(a_exp[:], a_log_sb[:], ACT.Exp).then_inc(act_set.sem, 1)
            act.wait_ge(dve_set.sem, DVE_SETS)

            def copy_transposed(norm, b, call, dst=xnT, banks=(psW[0:KP, 0, :], psW[0:KP, 1, :])):
                for k in range(KT):
                    act.wait_ge(norm.tr.sem, norm.tr.at(b, call * KT + k + 1))
                    act.activation(dst[:, k, :], banks[k], ACT.Copy).then_inc(norm.T.sem, 1)

            def decay_step(n, at):
                i = n % 2
                act.wait_ge(b_bc.sem, at(b_bc, 1))
                if n >= 2:
                    act.wait_ge(driven.sem, at(driven, -1))
                act.activation(b_sb[i][:], psB[:], ACT.Copy).then_inc(b_copied.sem, 1)
                if n >= 2:
                    act.wait_ge(scanned.sem, at(scanned, -1))
                for m in range(M3):
                    last = act.activation(decay[i][:, m, 1:T], dt[:, m, 1:T], ACT.Exp,
                                          scale=a_neg[:, m, n:n + 1])
                last.then_inc(decayed.sem, 1)

            def prepare(b, n):
                if n == 20:
                    copy_transposed(n1, b, 0, xnT, (psW[0:KP, 2, :], psW[0:KP, 0, :]))
                elif n in (25, 27, 29):
                    m = (n - 25) // 2
                    act.wait_ge(proj.sem, proj.at(b, m + 1))
                    act.activation(xs[:, m, TAPS - 1:], psW[:, m, :], ACT.Copy).then_inc(xs_ready.sem, 1)
                elif n in (26, 28, 30):
                    m = (n - 26) // 2
                    act.wait_ge(xs_ready.sem, xs_ready.at(b, m + 1))
                    act.activation(xc[:, m, :], xs[:, m, 0:T], ACT.Identity, scale=conv_wh[:, m, 0:1],
                                   bias=conv_bh[:, m:m + 1]).then_inc(conv_first.sem, 1)
                elif n in (33, 35, 37):
                    m = (n - 33) // 2
                    act.wait_ge(proj.sem, proj.at(b, M3 + m + 1))
                    act.activation(work_b[:, m, :], psW[:, m, :], ACT.Tanh, scale=0.5).then_inc(z_tanh.sem, 1)
                elif n in (40, 41, 42):
                    m = n - 40
                    act.wait_ge(conv.sem, conv.at(b, M3 * (TAPS - 2) + m + 1))
                    act.activation(work_a[:, m, :], xc[:, m, :], ACT.Tanh).then_inc(conv_tanh.sem, 1)
                elif n == 50:
                    first_part(b, 0)
                elif n == 57:
                    first_part(b, 1)
                elif n in (54, 55, 56):
                    m = n - 54
                    act.wait_ge(xp.sem, xp.at(b, XP_DT))
                    act.activation(relu_x[:, m, :], psW[:, 2, :], ACT.Relu, bias=dt_bias_sb[:, m:m + 1]).then_inc(sp_act.sem, 1)
                    act.activation(work_a[:, m, :], psW[:, 2, :], ACT.Abs, bias=dt_bias_sb[:, m:m + 1]).then_inc(sp_act.sem, 1)
                elif n in (58, 59, 60):
                    m = n - 58
                    act.wait_ge(sp_act.sem, sp_act.at(b, 2 * M3 + m))
                    act.activation(work_b[:, m, :], work_a[:, m, :], ACT.Exp, scale=-1.0).then_inc(sp_act.sem, 1)

            def first_part(b, o):
                s, bank, xp_done = SPLITS[o]
                act.wait_ge(xp.sem, xp.at(b, xp_done))
                act.activation(bc_s[:, s, :], bank, ACT.Copy).then_inc(first_part_s.sem, 1)

            def logarithms(b):
                act.wait_ge(sp_act.sem, sp_act.at(b, 3 * M3))
                for m in range(M3):
                    act.activation(work_a[:, m, :], work_b[:, m, :], ACT.Ln, bias=1.0).then_inc(sp_act.sem, 1)

            def first_decays(b):
                act.wait_ge(dt_step.sem, dt_step.at(b, 4))
                for n in range(2):
                    decay_step(n, lambda s, k, n=n: s.at(b, n + k))

            def take_gate(b):
                act.wait_ge(z_gate.sem, z_gate.at(b, M3))
                act.activation(gz[:], gz_next[:], ACT.Copy).then_inc(gz_ready.sem, 1)

            for n in range(NS):
                prepare(0, n)
            logarithms(0)
            take_gate(0)
            first_decays(0)
            decay_step(2, lambda s, k: s.at(0, 2 + k))
            with act.Fori(0, NB) as b:
                for n in range(3, NS):
                    decay_step(n, lambda s, k, n=n: s.at(b, n + k))
                    if n == 4:
                        act.wait_ge(h_free.sem, h_free.at(b, 1))
                        act.wait_ge(h_ready.sem, h_ready.at(b, 1))
                        act.activation(h[:], h_next[:], ACT.Copy).then_inc(h_copied.sem, 1)
                    if n in (7, 11):
                        first_part(b, 2 + (n - 7) // 4)
                    prepare(b + 1, n)
                logarithms(b + 1)
                first_decays(b + 1)
                copy_transposed(n2, b, 0)
                take_gate(b + 1)
                decay_step(2, lambda s, k: s.at(b + 1, 2 + k))
                act.wait_ge(route.sem, route.at(b, 7))
                act.activation(soft_e[:], soft[:], ACT.Exp).then_inc(route_exp.sem, 1)

            act.wait_ge(tab.sem, TAB_STEPS)

            def tile_copy(s, i):
                act.wait_ge(xt_tr.sem, xt_tr.at(s, 1))
                if not early(s, 2):
                    act.wait_ge(xt_hp.sem, xt_hp.at(s, -1))
                act.activation(xt_T[i][:], psY[0:KP, 0, 0:KT * P], ACT.Copy).then_inc(xt_c.sem, 1)

            def tile_tanh(s, i):
                act.wait_ge(xt_hp.sem, xt_hp.at(s, 1))
                if not early(s, 2):
                    act.wait_ge(xt_silu.sem, xt_silu.at(s, -1))
                act.activation(xt_th[i][:], psW[:, 0, :] if i == 0 else psW[:, 2, :], ACT.Tanh, scale=0.5).then_inc(xt_tanh.sem, 1)

            def tile_result(s, i):
                act.wait_ge(xt_out.sem, xt_out.at(s, 1))
                if not early(s, 2):
                    act.wait_ge(xt_saved.sem, xt_saved.at(s, -16))
                act.activation(xt_y[i][:], psY[:, 1 + i, 0:D], ACT.Copy).then_inc(xt_yc.sem, 1)

            def turn(s, i, last):
                i = i % 2
                if last is None or last >= 1:
                    tile_tanh(s + 1, 1 - i)
                if last is None or last >= 2:
                    tile_copy(s + 2, i)
                act.wait_ge(xt_htr.sem, xt_htr.at(s, 1))
                if not early(s, 2):
                    act.wait_ge(xt_out.sem, xt_out.at(s, -1))
                act.activation(xt_hT[i][:], psB[:], ACT.Copy).then_inc(xt_hc.sem, 1)
                if not early(s, 1):
                    tile_result(s - 1, 1 - i)

            tile_copy(0, 0)
            tile_copy(1, 1)
            tile_tanh(0, 0)
            tile_turns(act, turn, [None])
            tile_result(NT - 1, 1)

            act.wait_ge(loaded3.sem, ALL_LOADED3)
            act.wait_ge(dve_set3.sem, DVE_SETS3)
            front_banks = (psY[0:KP, 0, :], psY[0:KP, 1, :])
            copy_transposed(n3, 0, 0, xqT, front_banks)
            with act.Fori(0, NB) as b:
                def copy_maxima(g):
                    act.wait_ge(nm_tr.sem, nm_tr.at(b, g + 1))
                    if g >= 1:
                        act.wait_ge(nm_out.sem, nm_out.at(b, 16 * g))
                    act.activation(nm_T[:], psY[0:3 * HPG, 2, 0:T // 2].bitcast(BF16), ACT.Copy).then_inc(nm_c.sem, 1)

                copy_maxima(0)
                for hd in range(HEADS):
                    for c in range(TC):
                        q = hd * TC + c
                        act.wait_ge(s2.sem, s2.at(b, q + 1))
                        if hd >= 2 and c == 0:
                            act.wait_ge(pv.sem, pv.at(b, hd - 1))
                        act.activation(pT[hd % 2][:, c, :], psW[:, q % 3, :], ACT.Exp).then_inc(pexp.sem, 1)
                    if hd in MAXIMA_AFTER:
                        copy_maxima(MAXIMA_AFTER[hd])
                    if hd == 7:
                        copy_transposed(n3, b + 1, 0, xqT, front_banks)
                copy_transposed(n4, b, 0)
                copy_transposed(n4, b, 1)
                act.wait_ge(gate_mm.sem, gate_mm.at(b, 1))
                act.activation(gate_s[:], psY[:, 0, 0:TC * E].rearrange("p (c e) -> p c e", c=TC), ACT.Tanh,
                               scale=0.5).then_inc(gate_tanh.sem, 1)
                for e in range(E + 1):
                    act.wait_ge(fp.sem, fp.at(b, e + 1))
                    if e >= 3:
                        act.wait_ge(fsilu.sem, fsilu.at(b, e - 2))
                    act.activation(th[:, e % 3, :], psW[:, e % 2, :], ACT.Tanh, scale=0.5).then_inc(ftanh.sem, 1)

        @block.vector
        def _(dve):
            dve.memset(xs[:], 0.0).then_inc(dve_set.sem, 1)
            for i in range(2):
                dve.memset(decay[i][:], 0.0).then_inc(dve_set.sem, 1)
            dve.memset(ones[:], 1.0).then_inc(dve_set.sem, 1)
            dve.memset(prob_all[:], 1.0).then_inc(dve_set.sem, 1)
            dve.memset(count[:], 0.0).then_inc(dve_set.sem, 1)
            dve.memset(idx_all[:, NB * TC:], 0).then_inc(dve_set.sem, 1)
            dve.wait_ge(loaded.sem, ALL_LOADED)
            dve.wait_ge(pool_set.sem, POOL_SETS)
            dve.tensor_scalar(conv_wh[:], conv_w_sb[:], 0.5, None, ALU.mult).then_inc(dve_set.sem, 1)
            dve.tensor_scalar(conv_bh[:], conv_b_sb[:], 0.5, None, ALU.mult).then_inc(dve_set.sem, 1)
            for m in range(M3):
                dve.tensor_scalar(diag_d[:, m, :], ident[:], d_skip_sb[:, m:m + 1], None, ALU.mult).then_inc(dve_set.sem, 1)
                dve.tensor_copy(xproj_qr[:, m, :], xproj_q[:, m, :].to_broadcast([P, P])).then_inc(dve_set.sem, 1)
            dve.wait_ge(act_set.sem, 1)
            dve.tensor_scalar(a_neg[:], a_exp[:], -1.0, None, ALU.mult).then_inc(dve_set.sem, 1)
            dve.wait_ge(dve_set.sem, DVE_SETS)

            def layer_norm(norm, b, l, dst, src=h):
                moments(norm, b, l, src)
                normalise(norm, b, l, dst, src)

            def moments(norm, b, l, src):
                base = (2 * TC + 2) * l
                for c in range(TC):
                    dve.bn_stats(stats[:, c, :], src[:, c, :]).then_inc(norm.step.sem, 1)
                dve.wait_ge(norm.step.sem, norm.step.at(b, base + TC))
                dve.tensor_copy(stat_count[:], stats[:, TC - 1, 0:1]).then_inc(norm.step.sem, 1)
                for c in range(TC):
                    dve.bn_aggr(mv[:, c, :], stats[:, c, :]).then_inc(norm.step.sem, 1)
                dve.wait_ge(norm.step.sem, norm.step.at(b, base + 2 * TC + 1))
                dve.tensor_scalar(vare[:], mv[:, :, 1], EPS, None, ALU.add).then_inc(norm.step.sem, 1)

            def normalise(norm, b, l, dst, src):
                dve.wait_ge(norm.rstd.sem, norm.rstd.at(b, l + 1))
                for c in range(TC):
                    dve.tensor_scalar(dst[:, c, 0:D], src[:, c, :], mv[:, c, 0:1], rstd[:, c:c + 1],
                                      ALU.subtract, ALU.mult).then_inc(norm.xn.sem, 1)

            bc_e = lambda t: t[:].unsqueeze(2).to_broadcast([P, TC, E])

            def split_step(b, o, step):
                s, bank, _ = SPLITS[o]
                if not (isinstance(b, int) and o == 0 and step == 1):
                    dve.wait_ge(split.sem, split.at(b, 4 * o + step - 1))
                if step == 1:
                    dve.wait_ge(first_part_s.sem, first_part_s.at(b, o + 1))
                    dve.tensor_tensor(rest[0:64, 0, :], bank[0:64], bc_s[0:64, s, :], ALU.subtract).then_inc(split.sem, 1)
                elif step == 2:
                    dve.tensor_copy(bc_s[0:64, s, :], rest[0:64, 0, :]).then_inc(split.sem, 1)
                elif step == 3:
                    dve.tensor_tensor(rest[0:32, 1, :], rest[0:32, 0, :], bc_s[0:32, s, :], ALU.subtract).then_inc(split.sem, 1)
                elif step == 4:
                    dve.tensor_copy(bc_s[0:32, s, :], rest[0:32, 1, :]).then_inc(split.sem, 1)

            def prepare(b, n):
                if n == 9:
                    dve.wait_ge(gathered.sem, gathered.at(b, 16 * TC))
                    dve.tensor_tensor(h_next[:], rows_in[:], pos_sb[:], ALU.add).then_inc(h_ready.sem, 1)
                    dve.wait_ge(h_ready.sem, h_ready.at(b, 1))
                    moments(n1, b, 0, h_next)
                elif n == 15:
                    normalise(n1, b, 0, xn, h_next)
                elif 27 + M3 <= n < 27 + M3 * TAPS:
                    k, m = (n - 27) // M3, (n - 27) % M3
                    if k == 1:
                        dve.wait_ge(conv_first.sem, conv_first.at(b, m + 1))
                    else:
                        dve.wait_ge(conv.sem, conv.at(b, M3 * (k - 2) + m + 1))
                    dve.scalar_tensor_tensor(out=xc[:, m, :], in0=xs[:, m, k:k + T],
                                             scalar=conv_wh[:, m, k:k + 1], in1=xc[:, m, :],
                                             op0=ALU.mult, op1=ALU.add).then_inc(conv.sem, 1)
                elif n in (41, 42, 43):
                    m = n - 41
                    dve.wait_ge(conv_tanh.sem, conv_tanh.at(b, m + 1))
                    dve.scalar_tensor_tensor(out=xc[:, m, :], in0=work_a[:, m, :], scalar=1.0, in1=xc[:, m, :],
                                             op0=ALU.add, op1=ALU.mult).then_inc(xc_ready.sem, 1)
                elif 50 <= n < 54:
                    split_step(b, 0, n - 49)
                elif 56 <= n < 60:
                    split_step(b, 1, n - 55)
                if n in (34, 36, 38):
                    m = (n - 34) // 2
                    dve.wait_ge(z_tanh.sem, z_tanh.at(b, m + 1))
                    dve.scalar_tensor_tensor(out=gz_next[:, m, :], in0=work_b[:, m, :], scalar=1.0, in1=psW[:, m, :],
                                             op0=ALU.add, op1=ALU.mult).then_inc(z_gate.sem, 1)

            def rounding(b):
                dve.wait_ge(sp_act.sem, sp_act.at(b, 3 * M3))
                dve.tensor_scalar(correction[:], work_b[:], 1.0, -1.0, ALU.add, ALU.add).then_inc(dt_step.sem, 1)

            def finish_dt(b):
                dve.wait_ge(dt_step.sem, dt_step.at(b, 3))
                dve.tensor_tensor(dt[:], relu_x[:], correction[:], ALU.add).then_inc(dt_step.sem, 1)
                dve.wait_ge(dt_step.sem, dt_step.at(b, 4))
                dve.wait_ge(xc_ready.sem, xc_ready.at(b, M3))
                dve.tensor_tensor(u[:], dt[:], xc[:], ALU.mult).then_inc(dt_step.sem, 1)

            def weigh(n, at):
                dve.wait_ge(scanned.sem, at(scanned, 1))
                dve.wait_ge(c_bc.sem, at(c_bc, 1))
                dve.tensor_tensor(state[n % RING][:], state[n % RING][:], psC[:].unsqueeze(1).to_broadcast([P, M3, T]),
                                  ALU.mult).then_inc(weighed_s.sem, 1)

            def scan(n, at):
                dve.wait_ge(decayed.sem, at(decayed, 1))
                dve.wait_ge(driven.sem, at(driven, 1))
                if n >= RING:
                    dve.wait_ge(summed.sem, at(summed, 1 - RING))
                dve.tensor_tensor_scan(flat(state[n % RING]), flat(decay[n % 2]), flat(drive[n % 2]), 0.0,
                                       ALU.mult, ALU.add).then_inc(scanned.sem, 1)

            def first_scans(b):
                for n in range(2):
                    scan(n, lambda s, k, n=n: s.at(b, n + k))

            for n in range(NS):
                prepare(0, n)
            rounding(0)
            finish_dt(0)
            first_scans(0)
            with dve.Fori(0, NB) as b:
                for n in range(1, NS):
                    if n >= 2:
                        scan(n, lambda s, k, n=n: s.at(b, n + k))
                    weigh(n - 1, lambda s, k, n=n: s.at(b, n - 1 + k))
                    if n == 8:
                        dve.wait_ge(h_copied.sem, h_copied.at(b, 1))
                    if 6 <= n < 10:
                        split_step(b, 2, n - 5)
                    elif 10 <= n < 14:
                        split_step(b, 3, n - 9)
                    prepare(b + 1, n)
                    if n == 61:
                        rounding(b + 1)
                weigh(NS - 1, lambda s, k: s.at(b, NS - 1 + k))
                dve.wait_ge(gz_ready.sem, gz_ready.at(b, 1))
                dve.wait_ge(summed.sem, summed.at(b, NS))
                dve.scalar_tensor_tensor(out=gz[:], in0=psY[:], scalar=0.5, in1=gz[:],
                                         op0=ALU.mult, op1=ALU.mult).then_inc(gated.sem, 1)
                finish_dt(b + 1)
                for c2 in range(2):
                    dve.wait_ge(outp.sem, outp.at(b, c2 + 1))
                    dve.tensor_tensor(h[:, 2 * c2:2 * c2 + 2, :], h[:, 2 * c2:2 * c2 + 2, :],
                                      psW[:, c2, 0:2 * D].rearrange("p (c d) -> p c d", c=2), ALU.add).then_inc(resid1.sem, 1)
                dve.wait_ge(resid1.sem, resid1.at(b, 2))
                dve.wait_ge(xr_free.sem, xr_free.at(b, 1))
                dve.tensor_copy(xr[:, :, D:D + 1].bitcast(I32), token[:].unsqueeze(2)).then_inc(numbered.sem, 1)
                dve.wait_ge(numbered.sem, numbered.at(b, 1))
                dve.tensor_scalar(token[:], token[:], float(T), None, ALU.add).then_inc(numbered.sem, 1)
                layer_norm(n2, b, 0, xr)
                first_scans(b + 1)

                dve.wait_ge(route_mm.sem, route_mm.at(b, 1))
                dve.tensor_tensor(logit[:], psW[:, 2, 0:TC * E].rearrange("p (c e) -> p c e", c=TC),
                                  router_b_sb[:].unsqueeze(1).to_broadcast([P, TC, E]), ALU.add).then_inc(route.sem, 1)
                dve.wait_ge(route.sem, route.at(b, 1))
                dve.tensor_reduce(top[:], logit[:], AX.X, ALU.max).then_inc(route.sem, 1)
                dve.wait_ge(route.sem, route.at(b, 2))
                dve.tensor_tensor(tie[:], logit[:], bc_e(top), ALU.is_equal).then_inc(route.sem, 1)
                dve.wait_ge(route.sem, route.at(b, 3))
                dve.tensor_tensor(rev[:], tie[:], falling[:].unsqueeze(1).to_broadcast([P, TC, E]), ALU.mult).then_inc(route.sem, 1)
                dve.wait_ge(route.sem, route.at(b, 4))
                dve.tensor_reduce(first[:], rev[:], AX.X, ALU.max).then_inc(route.sem, 1)
                dve.wait_ge(route.sem, route.at(b, 5))
                dve.tensor_tensor(chosen[:], rev[:], bc_e(first), ALU.is_equal).then_inc(route.sem, 1)
                dve.tensor_tensor(soft[:], logit[:], bc_e(top), ALU.subtract).then_inc(route.sem, 1)
                dve.wait_ge(route.sem, route.at(b, 7))
                dve.tensor_copy(chosen_b[:], chosen[:]).then_inc(route.sem, 1)
                dve.wait_ge(route_exp.sem, route_exp.at(b, 1))
                dve.tensor_reduce(soft_s[:], soft_e[:], AX.X, ALU.add).then_inc(route.sem, 1)
                dve.wait_ge(route.sem, route.at(b, 9))
                dve.reciprocal(prob_all[:, bass.ds(b * TC, TC)], soft_s[:]).then_inc(route.sem, 1)
                dve.wait_ge(ranked.sem, ranked.at(b, 1))
                dve.tensor_tensor(ahead[:], psW[:, 2, P:P + TC * E].rearrange("p (c e) -> p c e", c=TC),
                                  count[:].unsqueeze(1).to_broadcast([P, TC, E]), ALU.add).then_inc(route.sem, 1)
                dve.wait_ge(route.sem, route.at(b, 11))
                dve.tensor_tensor(ahead[:], ahead[:], chosen[:], ALU.mult).then_inc(route.sem, 1)
                dve.tensor_scalar(region[:], first[:], -float(ROWS), float(E * ROWS), ALU.mult, ALU.add).then_inc(route.sem, 1)
                dve.wait_ge(route.sem, route.at(b, 13))
                dve.tensor_reduce(place[:], ahead[:], AX.X, ALU.add).then_inc(route.sem, 1)
                dve.wait_ge(route.sem, route.at(b, 14))
                dve.tensor_tensor(slot[:], place[:], region[:], ALU.add).then_inc(route.sem, 1)
                dve.tensor_tensor(count[:], count[:], psW[:, 2, P + TC * E:P + (TC + 1) * E], ALU.add).then_inc(route.sem, 1)
                dve.wait_ge(route.sem, route.at(b, 16))
                dve.wait_ge(numbered.sem, numbered.at(b, 2))

            step = [0]

            def tab_step(ins):
                step[0] += 1
                ins.then_inc(tab.sem, 1)
                dve.wait_ge(tab.sem, step[0])

            dve.wait_ge(x_saved.sem, 16 * TC * LAST)
            dve.wait_ge(h_saved.sem, 16 * LAST)
            dve.wait_ge(gathered.sem, 16 * TC * (LAST + 2))
            dve.wait_ge(decayed.sem, NS * LAST + 3)
            dve.wait_ge(driven.sem, NS * LAST + 3)
            dve.wait_ge(scanned.sem, NS * LAST + 2)
            e_of = lambda v: v.unsqueeze(1).to_broadcast([P, NT, E])
            s_of = lambda v: v.unsqueeze(2).to_broadcast([P, NT, E])
            tab_step(dve.tensor_tensor_scan(t_num, ones[:, 0:NT], ones[:, 0:NT], -1.0, ALU.mult, ALU.add))
            tab_step(dve.tensor_scalar(t_regions, falling[:], -float(ROWS), float(E * ROWS), ALU.mult, ALU.add))
            tab_step(dve.tensor_scalar(t_row, t_num, float(P), None, ALU.mult))
            tab_step(dve.tensor_tensor(t_cmp, e_of(count[:]), s_of(t_row), ALU.is_gt))
            tab_step(dve.tensor_reduce(t_full, t_cmp.rearrange("p s e -> p e s"), AX.X, ALU.add))
            tab_step(dve.tensor_tensor(t_pre, t_full.unsqueeze(1).to_broadcast([P, E, E]), before[:], ALU.mult))
            tab_step(dve.tensor_reduce(t_begin, t_pre, AX.X, ALU.add))
            tab_step(dve.tensor_tensor(t_end, t_begin, t_full, ALU.add))
            tab_step(dve.tensor_tensor(t_a, s_of(t_num), e_of(t_begin), ALU.is_ge))
            tab_step(dve.tensor_tensor(t_b, s_of(t_num), e_of(t_end), ALU.is_lt))
            tab_step(dve.tensor_tensor(t_a, t_a, t_b, ALU.mult))
            tab_step(dve.tensor_reduce(t_valid, t_a, AX.X, ALU.add))
            tab_step(dve.scalar_tensor_tensor(out=t_off, in0=t_begin, scalar=-float(P), in1=t_regions, op0=ALU.mult, op1=ALU.add))
            tab_step(dve.tensor_tensor(t_b, s_of(t_row), e_of(t_off), ALU.add))
            tab_step(dve.tensor_tensor(t_b, t_b, t_a, ALU.mult))
            tab_step(dve.tensor_reduce(t_row, t_b, AX.X, ALU.add))
            tab_step(dve.tensor_scalar(t_valid, t_valid, -float(E * ROWS), float(E * ROWS), ALU.mult, ALU.add))
            tab_step(dve.tensor_tensor(t_row, t_row, t_valid, ALU.add))
            tab_step(dve.tensor_scalar(t_off, falling[:], -1.0, float(E), ALU.mult, ALU.add))
            tab_step(dve.tensor_tensor(t_b, t_a, e_of(t_off), ALU.mult))
            tab_step(dve.tensor_reduce(t_exp, t_b, AX.X, ALU.add))
            tab_step(dve.tensor_tensor(t_tail, count[:], t_regions, ALU.add))
            tab_step(dve.tensor_copy(table_r[:], t_row[0:1, :]))
            tab_step(dve.tensor_copy(table_e[:], t_exp[0:1, :]))
            tab_step(dve.tensor_copy(tail[:], t_tail[0:1, :]))
            assert step[0] == TAB_STEPS

            def tile_hidden(s, i):
                h1, h2 = (psW[:, 0, :], psW[:, 1, :]) if i == 0 else (psW[:, 2, :], psC[:])
                dve.wait_ge(xt_tanh.sem, xt_tanh.at(s, 1))
                if not early(s, 1):
                    dve.wait_ge(xt_h.sem, xt_h.at(s, 0))
                dve.scalar_tensor_tensor(out=xt_sl[:], in0=xt_th[i][:], scalar=1.0, in1=h1,
                                         op0=ALU.add, op1=ALU.mult).then_inc(xt_silu.sem, 1)
                dve.wait_ge(xt_silu.sem, xt_silu.at(s, 1))
                if not early(s, 2):
                    dve.wait_ge(xt_htr.sem, xt_htr.at(s, -1))
                dve.scalar_tensor_tensor(out=xt_hid[i][:], in0=xt_sl[:], scalar=0.5, in1=h2,
                                         op0=ALU.mult, op1=ALU.mult).then_inc(xt_h.sem, 1)

            def turn(s, i, last):
                if last is None or last >= 1:
                    tile_hidden(s + 1, 1 - i % 2)

            tile_hidden(0, 0)
            tile_turns(dve, turn, [None])

            dve.wait_ge(xt_saved.sem, 16 * NT)
            dve.wait_ge(loaded3.sem, ALL_LOADED3)
            dve.memset(vA[:], 0.0).then_inc(dve_set3.sem, 1)
            dve.memset(ks[96:99, :, :], 1.0).then_inc(dve_set3.sem, 1)
            dve.memset(cw[:], 1.0).then_inc(dve_set3.sem, 1)
            dve.tensor_copy(identb[:], ident[:]).then_inc(dve_set3.sem, 1)
            dve.tensor_scalar(bqk_sb[:, 0, :], bqk_sb[:, 0, :], HD ** -0.5, None, ALU.mult).then_inc(dve_set3.sem, 1)
            dve.wait_ge(dve_set3.sem, 5)
            dve.memset(vA[:, :, :, HD:HD + 1], 1.0).then_inc(dve_set3.sem, 1)
            dve.wait_ge(dve_set3.sem, DVE_SETS3)

            def add_experts(b):
                dve.wait_ge(y_back.sem, y_back.at(b, 16))
                dve.tensor_copy(y_b[:], y_in[:]).then_inc(resid2.sem, 1)
                dve.tensor_copy(prob_cur[:], prob_all[:, bass.ds(b * TC, TC)]).then_inc(resid2.sem, 1)
                dve.wait_ge(resid2.sem, resid2.at(b, 2))
                dve.wait_ge(h_back.sem, h_back.at(b, 16))
                for c in range(TC):
                    dve.scalar_tensor_tensor(out=h_in[:, c, :], in0=y_b[:, c, :], scalar=prob_cur[:, c:c + 1], in1=h_in[:, c, :],
                                             op0=ALU.mult, op1=ALU.add).then_inc(resid2.sem, 1)
                dve.wait_ge(resid2.sem, resid2.at(b, 2 + TC))

            def split_first(b, which):
                base = 7 * which
                if which == 1:
                    dve.wait_ge(qk_step.sem, qk_step.at(b, base))
                for k in range(KT):
                    dve.wait_ge(qkp.sem, qkp.at(b, 2 * which + k + 1))
                    dve.tensor_scalar(qk_f[:, k, :], (Q_BANKS, K_BANKS)[which][k],
                                      HD ** -0.5 if which == 0 else 1.0, bqk_sb[:, which, k:k + 1],
                                      ALU.mult, ALU.add).then_inc(qk_step.sem, 1)
                dve.wait_ge(qk_step.sem, qk_step.at(b, base + 2))
                if which == 1:
                    dve.wait_ge(parts_out.sem, parts_out.at(b, 16))
                dve.tensor_copy(parts[:, 0, :, :], qk_f[:]).then_inc(qk_step.sem, 1)

            def split_rest(b, which):
                base = 7 * which
                dve.wait_ge(qk_step.sem, qk_step.at(b, base + 3))
                dve.tensor_tensor(qk_r[:], qk_f[:], parts[:, 0, :, :], ALU.subtract).then_inc(qk_step.sem, 1)
                dve.wait_ge(qk_step.sem, qk_step.at(b, base + 4))
                dve.tensor_copy(parts[:, 1, :, :], qk_r[:]).then_inc(qk_step.sem, 1)
                dve.wait_ge(qk_step.sem, qk_step.at(b, base + 5))
                dve.tensor_tensor(qk_f[:], qk_r[:], parts[:, 1, :, :], ALU.subtract).then_inc(qk_step.sem, 1)
                dve.wait_ge(qk_step.sem, qk_step.at(b, base + 6))
                dve.tensor_copy(parts[:, 2, :, :], qk_f[:]).then_inc(qk_step.sem, 1)

            def values(b):
                for c in range(TC):
                    if c % 2 == 0:
                        dve.wait_ge(vp.sem, vp.at(b, c // 2 + 1))
                    src = V_BANKS[c // 2][:, (c % 2) * D:(c % 2 + 1) * D]
                    dve.tensor_tensor(vA[:, c, :, 0:HD], src.rearrange("p (h d) -> p h d", d=HD),
                                      bv_sb[:].rearrange("p (h d) -> p h d", d=HD), ALU.add).then_inc(v_ready.sem, 1)

            def maximum(b, hd, c):
                dve.wait_ge(s1.sem, s1.at(b, hd * TC + c + 1))
                dve.tensor_reduce(neg_max[:, c, hd:hd + 1], scores_bank(hd, c), AX.X, ALU.max,
                                  negate=True).then_inc(mx.sem, 1)

            def split_maxima(b, g):
                heads = slice(HPG * g, HPG * (g + 1))
                dve.wait_ge(mx.sem, mx.at(b, HPG * (g + 1) * TC))
                dve.tensor_copy(nm_p[:, :, g, 0, :], neg_max[:, :, heads]).then_inc(nm_step.sem, 1)
                dve.wait_ge(nm_step.sem, nm_step.at(b, 5 * g + 1))
                dve.tensor_tensor(nm_r[:, :, heads], neg_max[:, :, heads], nm_p[:, :, g, 0, :], ALU.subtract).then_inc(nm_step.sem, 1)
                dve.wait_ge(nm_step.sem, nm_step.at(b, 5 * g + 2))
                dve.tensor_copy(nm_p[:, :, g, 1, :], nm_r[:, :, heads]).then_inc(nm_step.sem, 1)
                dve.wait_ge(nm_step.sem, nm_step.at(b, 5 * g + 3))
                dve.tensor_tensor(neg_max[:, :, heads], nm_r[:, :, heads], nm_p[:, :, g, 1, :], ALU.subtract).then_inc(nm_step.sem, 1)
                dve.wait_ge(nm_step.sem, nm_step.at(b, 5 * g + 4))
                dve.tensor_copy(nm_p[:, :, g, 2, :], neg_max[:, :, heads]).then_inc(nm_step.sem, 1)

            add_experts(0)
            moments(n3, 0, 0, h_in)
            normalise(n3, 0, 0, xn, h_in)
            for which in range(2):
                split_first(0, which)
                split_rest(0, which)
            values(0)
            for e in range(E + 1):
                for hd, c in early_tiles(e):
                    maximum(0, hd, c)
            with dve.Fori(0, NB) as b:
                for hd in range(EARLY_HEADS, HEADS):
                    for c in range(TC):
                        maximum(b, hd, c)
                    if hd == HPG - 1:
                        dve.wait_ge(h_free3.sem, h_free3.at(b, 1))
                        dve.tensor_tensor(h[:], h_in[:], bo_sb[:].unsqueeze(1).to_broadcast([P, TC, D]), ALU.add).then_inc(resid3.sem, 1)
                    if hd % HPG == HPG - 1:
                        split_maxima(b, hd // HPG)

                dve.wait_ge(resid3.sem, resid3.at(b, 1))
                add_experts(b + 1)
                moments(n3, b + 1, 0, h_in)
                normalise(n3, b + 1, 0, xn, h_in)
                for g in range(HG):
                    if g == 1:
                        split_first(b + 1, 0)
                        split_rest(b + 1, 0)
                    dve.wait_ge(pv.sem, pv.at(b, 4 * (g + 1)))
                    dve.tensor_copy(og[:, g, :], (psB, psC)[g % 2][:]).then_inc(og_c.sem, 1)
                o_bank = (psY[:, 0], psY[:, 1], psY[:, 2], psC[:])
                for c in range(TC):
                    o = o_bank[c][:, 0:HG * P].rearrange("p (h d) -> p h d", d=32)
                    dve.wait_ge(og_tr.sem, og_tr.at(b, c + 1))
                    dve.reciprocal(r_sum[:, c, :], o[:, :, HD]).then_inc(a_norm.sem, 1)
                    dve.wait_ge(a_norm.sem, a_norm.at(b, 2 * c + 1))
                    dve.tensor_tensor(xn[:, c, :].rearrange("p (h d) -> p h d", d=HD), o[:, :, 0:HD],
                                      r_sum[:, c, :].unsqueeze(2).to_broadcast([P, HEADS, HD]),
                                      ALU.mult).then_inc(a_norm.sem, 1)
                for c2 in range(2):
                    dve.wait_ge(ao.sem, ao.at(b, c2 + 1))
                    dve.tensor_tensor(h[:, 2 * c2:2 * c2 + 2, :], h[:, 2 * c2:2 * c2 + 2, :],
                                      psY[:, c2, 0:2 * D].rearrange("p (c d) -> p c d", c=2), ALU.add).then_inc(resid3.sem, 1)
                dve.wait_ge(resid3.sem, resid3.at(b, 3))
                layer_norm(n4, b, 0, xn)
                split_first(b + 1, 1)
                split_rest(b + 1, 1)
                values(b + 1)

                gate_count = [0]

                def gate_step(ins):
                    gate_count[0] += 1
                    ins.then_inc(gate.sem, 1)
                    dve.wait_ge(gate.sem, gate.at(b, gate_count[0]))

                def best_two(v, n, on):
                    vi = v.unsqueeze(3).to_broadcast([P, TC, n, n])
                    vj = v.unsqueeze(2).to_broadcast([P, TC, n, n])
                    gt, eq = cmp_gt[:, :, 0:n, 0:n], cmp_eq[:, :, 0:n, 0:n]
                    dve.tensor_tensor(gt, vj, vi, ALU.is_gt).then_inc(gate.sem, 1)
                    gate_count[0] += 1
                    gate_step(dve.tensor_tensor(eq, vj, vi, ALU.is_equal))
                    gate_step(dve.tensor_tensor(eq, eq, before[:, 0:n, 0:n].unsqueeze(1).to_broadcast([P, TC, n, n]), ALU.mult))
                    gate_step(dve.tensor_tensor(gt, gt, eq, ALU.add))
                    gate_step(dve.tensor_reduce(rank[:, :, 0:n], gt, AX.X, ALU.add))
                    gate_step(dve.tensor_scalar(on, rank[:, :, 0:n], 2.0, None, ALU.is_lt))

                dve.wait_ge(gate_tanh.sem, gate_tanh.at(b, 1))
                gate_step(dve.tensor_scalar(gate_s[:], gate_s[:], 0.5, 0.5, ALU.mult, ALU.add))
                gate_step(dve.tensor_tensor(gate_v[:], gate_s[:], gate_b_sb[:].unsqueeze(1).to_broadcast([P, TC, E]), ALU.add))
                gate_step(dve.tensor_tensor(group_v[:], gate_v[:, :, 0::2], gate_v[:, :, 1::2], ALU.add))
                best_two(group_v[:], 4, group_on[:])
                pair = lambda t: t[:].rearrange("p c (g e) -> p c g e", e=2)
                on4 = group_on[:].unsqueeze(3).to_broadcast([P, TC, 4, 2])
                gate_step(dve.tensor_tensor(pair(masked), pair(gate_v), on4, ALU.mult))
                gate_step(dve.tensor_scalar(group_v[:], group_on[:], -1.0, 1e30, ALU.add, ALU.mult))
                gate_step(dve.tensor_tensor(pair(masked), pair(masked),
                                            group_v[:].unsqueeze(3).to_broadcast([P, TC, 4, 2]), ALU.add))
                best_two(masked[:], E, cw[:, :, 0:E])
                gate_step(dve.tensor_tensor(cw[:, :, 0:E], cw[:, :, 0:E], gate_s[:], ALU.mult))
                gate_step(dve.tensor_reduce(w_sum[:], cw[:, :, 0:E], AX.X, ALU.add))
                gate_step(dve.tensor_scalar(w_sum[:], w_sum[:], 1e-6, None, ALU.add))
                gate_step(dve.reciprocal(w_inv[:], w_sum[:]))
                gate_step(dve.tensor_tensor(cw[:, :, 0:E], cw[:, :, 0:E], bc_e(w_inv), ALU.mult))
                assert gate_count[0] == gate.per, gate_count[0]

                def accumulate2(e):
                    dve.wait_ge(fout.sem, fout.at(b, e + 1))
                    for c in range(TC):
                        src = psY[:, 1 + c // 2, (c % 2) * D:(c % 2 + 1) * D]
                        if e >= 1:
                            dve.wait_ge(facc.sem, facc.at(b, TC * (e - 1) + c + 1))
                        dve.scalar_tensor_tensor(out=h[:, c, :], in0=src, scalar=cw[:, c, e:e + 1],
                                                 in1=h[:, c, :], op0=ALU.mult, op1=ALU.add).then_inc(facc.sem, 1)

                for e in range(E + 1):
                    dve.wait_ge(ftanh.sem, ftanh.at(b, e + 1))
                    if e >= 1:
                        dve.wait_ge(fhid.sem, fhid.at(b, e))
                    dve.scalar_tensor_tensor(out=sl[:], in0=th[:, e % 3, :], scalar=1.0, in1=psW[:, e % 2, :],
                                             op0=ALU.add, op1=ALU.mult).then_inc(fsilu.sem, 1)
                    dve.wait_ge(fsilu.sem, fsilu.at(b, e + 1))
                    if e >= 2:
                        dve.wait_ge(fout.sem, fout.at(b, e - 1))
                    h2 = psW[:, 2, :] if e % 2 == 0 else psY[:, 0, :]
                    dve.scalar_tensor_tensor(out=hid[e % 2][:], in0=sl[:], scalar=0.5, in1=h2,
                                             op0=ALU.mult, op1=ALU.mult).then_inc(fhid.sem, 1)
                    if e >= 1:
                        accumulate2(e - 1)
                    for hd, c in early_tiles(e):
                        maximum(b + 1, hd, c)
                accumulate2(E)
                dve.wait_ge(facc.sem, facc.at(b, (E + 1) * TC))

        @block.tensor
        def _(pe):
            pe.wait_ge(loaded.sem, ALL_LOADED)
            pe.wait_ge(pool_set.sem, POOL_SETS)
            pe.wait_ge(dve_set.sem, DVE_SETS)

            def transposes(norm, src, banks=(psW[0:KP, 0, :], psW[0:KP, 1, :])):
                for k in range(KT):
                    for c in range(TC):
                        mm = pe.transpose(banks[k][:, c * P:(c + 1) * P], src[:, c, k * KP:(k + 1) * KP], ident[:])
                    mm.then_inc(norm.tr.sem, 1)

            def logits(w, done, bank):
                for c in range(TC):
                    for k in range(KT):
                        mm = pe.matmul(bank[:, c * E:(c + 1) * E], xnT[:, k, c * P:(c + 1) * P], w[:, k, :],
                                       start=(k == 0), stop=(k == KT - 1))
                mm.then_inc(done, 1)

            def project_xc(b, which, dst, w, m, done):
                if which == XP_B0 and m == 0:
                    pe.wait_ge(xc_ready.sem, xc_ready.at(b, M3))
                    pe.wait_ge(z_gate.sem, z_gate.at(b, M3))
                mm = pe.matmul(dst, w[:, m, :], xc[:, m, :], start=(m == 0), stop=(m == M3 - 1))
                if m == M3 - 1:
                    mm.then_inc(xp.sem, 1)

            def prepare(b, n):
                if n == 15:
                    pe.wait_ge(n1.xn.sem, n1.xn.at(b, TC))
                    transposes(n1, xn, (psW[0:KP, 2, :], psW[0:KP, 0, :]))
                elif 19 <= n < 25 or 27 <= n < 33:
                    z = n >= 27
                    m, k = (n - (27 if z else 19)) // 2, (n - (27 if z else 19)) % 2
                    if not z and m == 0 and k == 0:
                        pe.wait_ge(n1.T.sem, n1.T.at(b, KT))
                    if z and k == 0:
                        pe.wait_ge(xs_ready.sem, xs_ready.at(b, m + 1))
                    col = (M3 * z + m) * P
                    mm = pe.matmul(psW[:, m, :], in_w_sb[:, k, col:col + P], xnT[:, k, :], start=(k == 0), stop=(k == KT - 1))
                    if k == KT - 1:
                        mm.then_inc(proj.sem, 1)
                elif 44 <= n < 47:
                    project_xc(b, XP_B0, psW[0:96, 0, :], xproj_bc[:, :, 0, :], n - 44, xp.sem)
                elif 47 <= n < 50:
                    project_xc(b, XP_DT, psW[:, 2, :], xproj_qr[:], n - 47, xp.sem)
                elif 50 <= n < 53:
                    project_xc(b, XP_C0, psW[0:96, 1, :], xproj_bc[:, :, 2, :], n - 50, xp.sem)

            def broadcast_b(n, at, half, row, follows):
                if follows:
                    pe.wait_ge(b_copied.sem, at(b_copied, 0))
                pe.matmul(psB[:], onehot[:, row, :], bc_s[:, half, :], start=True, stop=True).then_inc(b_bc.sem, 1)

            def broadcast_c(n, at, half, row):
                if n >= 1:
                    pe.wait_ge(weighed_s.sem, at(weighed_s, 0))
                pe.matmul(psC[:], onehot[:, row, :], bc_s[:, 2 + half, :], start=True, stop=True).then_inc(c_bc.sem, 1)

            def first_broadcasts(b):
                pe.wait_ge(split.sem, split.at(b, 8))
                for n in range(2):
                    if n == 1:
                        broadcast_c(0, None, 0, 0)
                    broadcast_b(n, lambda s, k, n=n: s.at(b, n + k), 0, n, n >= 1 or not isinstance(b, int))

            def third_broadcast(b):
                broadcast_b(2, lambda s, k: s.at(b, 2 + k), 0, 2, True)

            def open_sum():
                for m in range(M3):
                    pe.matmul(psY[:, m, :], diag_d[:, m, :], xc[:, m, :], start=True, stop=False, skip_group_check=True)

            for n in range(NS):
                prepare(0, n)
            first_broadcasts(0)
            open_sum()
            third_broadcast(0)
            with pe.Fori(0, NB) as b:
                def add_state(n, at):
                    pe.wait_ge(weighed_s.sem, at(weighed_s, 1))
                    for m in range(M3):
                        mm = pe.matmul(psY[:, m, :], ident[:], state[n % RING][:, m, :], start=False, stop=(n == NS - 1),
                                       skip_group_check=True)
                    mm.then_inc(summed.sem, 1)

                for n in range(NS):
                    at = lambda s, k, n=n: s.at(b, n + k)
                    if n + 2 == 32:
                        pe.wait_ge(split.sem, split.at(b, 16))
                    if 3 <= n + 2 < NS:
                        broadcast_b(n + 2, lambda s, k, n=n: s.at(b, n + 2 + k), (n + 2) // 32, (n + 2) % 32, True)
                    if n >= 1:
                        broadcast_c(n, at, n // 32, n % 32)
                        add_state(n - 1, lambda s, k, n=n: s.at(b, n - 1 + k))
                    if n < 3:
                        project_xc(b, XP_B1, psW[0:96, 0, :], xproj_bc[:, :, 1, :], n, xp.sem)
                    elif n < 6:
                        project_xc(b, XP_C1, psW[0:96, 1, :], xproj_bc[:, :, 3, :], n - 3, xp.sem)
                    prepare(b + 1, n)
                add_state(NS - 1, lambda s, k: s.at(b, NS - 1 + k))
                first_broadcasts(b + 1)
                pe.wait_ge(gated.sem, gated.at(b, 1))
                for c in range(TC):
                    for m in range(M3):
                        mm = pe.matmul(psW[:, c // 2, (c % 2) * D:(c % 2 + 1) * D], gz[:, m, c * P:(c + 1) * P],
                                       out_w_sb[:, m, :], start=(m == 0), stop=(m == M3 - 1))
                    if c % 2:
                        mm.then_inc(outp.sem, 1)
                open_sum()
                pe.wait_ge(n2.xn.sem, n2.xn.at(b, TC))
                transposes(n2, xr)
                third_broadcast(b + 1)
                pe.wait_ge(n2.T.sem, n2.T.at(b, KT))
                logits(router_w_sb, route_mm.sem, psW[:, 2, :])
                pe.wait_ge(route.sem, route.at(b, 8))
                for c in range(TC + 1):
                    for c1 in range(min(c, TC - 1) + 1):
                        mm = pe.matmul(psW[:, 2, P + c * E:P + (c + 1) * E], tri[:] if c1 == c else ones[:], chosen_b[:, c1, :],
                                       start=(c1 == 0), stop=(c1 == min(c, TC - 1)))
                mm.then_inc(ranked.sem, 1)

            pe.wait_ge(tab.sem, TAB_STEPS)
            pe.wait_ge(loaded2.sem, ALL_LOADED2)

            group = [None]

            def expert_of(s):
                return pe.value_load(table_e[0:1, bass.ds(s, 1)], min_val=0, max_val=E - 1)

            def tile_transpose(s, i, more):
                pe.wait_ge(xt_loaded[i].sem, loaded_upto(s, i, group, more))
                if not early(s, 1):
                    pe.wait_ge(xt_c.sem, xt_c.at(s, 0))
                for k in range(KT):
                    mm = pe.transpose(psY[0:KP, 0, k * P:(k + 1) * P], xt_in[i][:, k * KP:(k + 1) * KP], ident[:])
                mm.then_inc(xt_tr.sem, 1)

            def tile_products(s, i):
                e = expert_of(s)
                pe.wait_ge(xt_c.sem, xt_c.at(s, 1))
                if not early(s, 2):
                    pe.wait_ge(xt_h.sem, xt_h.at(s, -1))
                h1, h2 = (psW[:, 0, :], psW[:, 1, :]) if i == 0 else (psW[:, 2, :], psC[:])
                for w, dst in ((w1_sb, h1), (w2_sb, h2)):
                    for k in range(KT):
                        mm = pe.matmul(dst, xt_T[i][:, k * P:(k + 1) * P], w[:, k, bass.ds(e * HID, HID)],
                                       start=(k == 0), stop=(k == KT - 1))
                mm.then_inc(xt_hp.sem, 1)

            def tile_out(s, i):
                e = expert_of(s)
                pe.wait_ge(xt_hc.sem, xt_hc.at(s, 1))
                if not early(s, 2):
                    pe.wait_ge(xt_yc.sem, xt_yc.at(s, -1))
                for t in range(HT):
                    mm = pe.matmul(psY[:, 1 + i, 0:D], xt_hT[i][:, t * P:(t + 1) * P], w3_sb[:, t, bass.ds(e * D, D)],
                                   start=(t == 0), stop=(t == HT - 1))
                mm.then_inc(xt_out.sem, 1)

            def turn(s, i, last):
                if last is None or last >= 1:
                    tile_products(s + 1, 1 - i % 2)
                if last is None or last >= 2:
                    tile_transpose(s + 2, (i + 2) % AHEAD, (i + 2) // AHEAD)
                pe.wait_ge(xt_h.sem, xt_h.at(s, 1))
                if not early(s, 1):
                    pe.wait_ge(xt_hc.sem, xt_hc.at(s, 0))
                for t in range(HT):
                    mm = pe.transpose(psB[:, t * P:(t + 1) * P], xt_hid[i % 2][:, t * P:(t + 1) * P], ident[:])
                mm.then_inc(xt_htr.sem, 1)
                if not early(s, 1):
                    tile_out(s - 1, 1 - i % 2)

            tile_transpose(0, 0, 0)
            tile_transpose(1, 1, 0)
            tile_products(0, 0)
            tile_turns(pe, turn, group)
            tile_out(NT - 1, 1)

            pe.wait_ge(dve_set3.sem, DVE_SETS3)
            pe.wait_ge(loaded3.sem, ALL_LOADED3)
            pe.wait_ge(xt_yc.sem, NT)
            def front_transposes(b):
                pe.wait_ge(n3.xn.sem, n3.xn.at(b, TC))
                transposes(n3, xn, (psY[0:KP, 0, :], psY[0:KP, 1, :]))

            def project(b, which, step):
                if step == 0:
                    if which == 0:
                        pe.wait_ge(n3.T.sem, n3.T.at(b, KT))
                w, m, k = (wq_sb, wk_sb)[which], step // KT, step % KT
                mm = pe.matmul((Q_BANKS, K_BANKS)[which][m], w[:, k, m * KP:(m + 1) * KP], xqT[:, k, :], start=(k == 0), stop=(k == KT - 1))
                if k == KT - 1:
                    mm.then_inc(qkp.sem, 1)

            def project_values():
                for c in range(TC):
                    for k in range(KT):
                        mm = pe.matmul(V_BANKS[c // 2][:, (c % 2) * D:(c % 2 + 1) * D], xqT[:, k, c * P:(c + 1) * P],
                                       wv_sb[:, k, :], start=(k == 0), stop=(k == KT - 1))
                    if c % 2:
                        mm.then_inc(vp.sem, 1)

            def scores(b, hd, c):
                q = hd * TC + c
                if q == EARLY_HEADS * TC + 1:
                    pe.wait_ge(mx.sem, mx.at(b, q))
                elif q >= 2:
                    pe.wait_ge(mx.sem, mx.at(b, q - 1))
                pe.matmul(scores_bank(hd, c), qs[0:96, hd, c * P:(c + 1) * P], ks[0:96, hd, :],
                          start=True, stop=True).then_inc(s1.sem, 1)

            def laid_out(b):
                pe.wait_ge(q_sent.sem, q_sent.at(b, 16 * 6))
                pe.wait_ge(k_sent.sem, k_sent.at(b, 16 * 6))

            front_transposes(0)
            for which in range(2):
                for step in range(KT * KT):
                    project(0, which, step)
            project_values()
            laid_out(0)
            for e in range(E + 1):
                for hd, c in early_tiles(e):
                    scores(0, hd, c)
            with pe.Fori(0, NB) as b:

                def transpose_maxima(g):
                    split_up = in_register(pe, nm_step.at(b, 5 * (g + 1)))
                    pe.wait_ge(pool_set.sem, POOL_SETS)
                    if g >= 1:
                        pe.wait_ge(nm_c.sem, in_register(pe, nm_c.at(b, g)))
                    pe.wait_ge(nm_step.sem, split_up)
                    nm_ps = psY[0:3 * HPG, 2, 0:T // 2].bitcast(BF16)
                    for c in range(TC):
                        mm = pe.transpose(nm_ps[:, c * P:(c + 1) * P], nm_p[:, c, g, :, :].rearrange("p r h -> p (r h)"), identb[:])
                    mm.then_inc(nm_tr.sem, 1)

                def scores_less_maximum(hd, c):
                    q = hd * TC + c
                    if q >= 3:
                        pe.wait_ge(pexp.sem, pexp.at(b, q - 2))
                    pe.matmul(psW[:, q % 3, :], ks[0:99, hd, c * P:(c + 1) * P], qs[0:99, hd, :],
                              start=True, stop=True).then_inc(s2.sem, 1)

                def weighted_values(hd, kc):
                    g, r = hd // HPG, 32 * (hd % HPG)
                    pe.wait_ge(pexp.sem, pexp.at(b, TC * hd + kc + 1))
                    if hd == 8 and kc == 0:
                        pe.wait_ge(og_c.sem, og_c.at(b, 1))
                    mm = pe.matmul((psB, psC)[g % 2][r:r + 32, :], vA[:, kc, hd, :], pT[hd % 2][:, kc, :],
                                   start=(kc == 0), stop=(kc == TC - 1))
                    if kc == TC - 1:
                        mm.then_inc(pv.sem, 1)

                for hd in range(EARLY_HEADS, 2 * HPG):
                    for c in range(TC):
                        scores(b, hd, c)
                    if hd == HPG:
                        transpose_maxima(0)
                pe.wait_ge(v_ready.sem, v_ready.at(b, TC))
                for hd in range(HEADS):
                    if hd % HPG == 0:
                        pe.wait_ge(nm_sent.sem, nm_sent.at(b, 16 * (hd // HPG + 1)))
                    for c in range(TC):
                        scores_less_maximum(hd, c)
                        if hd < HPG:
                            scores(b, hd + 2 * HPG, c)
                        if hd >= 1:
                            weighted_values(hd - 1, c)
                        if hd == 9:
                            project(b + 1, 0, c)
                    if hd in MAXIMA_AFTER:
                        transpose_maxima(MAXIMA_AFTER[hd])
                    if hd == 6:
                        front_transposes(b + 1)
                for kc in range(TC):
                    weighted_values(HEADS - 1, kc)
                pe.wait_ge(og_c.sem, og_c.at(b, HG))
                pe.wait_ge(qk_step.sem, qk_step.at(b + 1, 2))
                o_bank = (psY[:, 0], psY[:, 1], psY[:, 2], psC[:])
                for c in range(TC):
                    for g in range(HG):
                        mm = pe.transpose(o_bank[c][:, g * P:(g + 1) * P], og[:, g, c * P:(c + 1) * P], ident[:])
                    mm.then_inc(og_tr.sem, 1)
                pe.wait_ge(a_norm.sem, a_norm.at(b, 2 * TC))
                transposes(n4, xn)
                pe.wait_ge(n4.T.sem, n4.T.at(b, KT))
                for c in range(TC):
                    for k in range(KT):
                        mm = pe.matmul(psY[:, c // 2, (c % 2) * D:(c % 2 + 1) * D], xnT[:, k, c * P:(c + 1) * P],
                                       wo_sb[:, k, :], start=(k == 0), stop=(k == KT - 1))
                    if c % 2:
                        mm.then_inc(ao.sem, 1)
                for step in range(KT * KT):
                    project(b + 1, 1, step)
                project_values()
                pe.wait_ge(n4.xn.sem, n4.xn.at(b, TC))
                transposes(n4, xn)
                pe.wait_ge(n4.T.sem, n4.T.at(b, 2 * KT))
                logits(gate_w_sb, gate_mm.sem, psY[:, 0, :])

                def expert_out2(e):
                    pe.wait_ge(fhid.sem, fhid.at(b, e + 1))
                    if e >= 1:
                        pe.wait_ge(facc.sem, facc.at(b, TC * e))
                    for c in range(TC):
                        mm = pe.matmul(psY[:, 1 + c // 2, (c % 2) * D:(c % 2 + 1) * D],
                                       hid[e % 2][:, c * P:(c + 1) * P], f2_sb[:, e, :], start=True, stop=True)
                    mm.then_inc(fout.sem, 1)

                pe.wait_ge(v_ready.sem, v_ready.at(b + 1, TC))
                pe.wait_ge(gate_tanh.sem, gate_tanh.at(b, 1))
                for e in range(E + 1):
                    if e >= 2:
                        pe.wait_ge(fhid.sem, fhid.at(b, e - 1))
                    h2 = psW[:, 2, :] if e % 2 == 0 else psY[:, 0, :]
                    for w, dst in ((f1_sb, psW[:, e % 2, :]), (f3_sb, h2)):
                        for k in range(KT):
                            mm = pe.matmul(dst, w[:, k, e, :], xnT[:, k, :], start=(k == 0), stop=(k == KT - 1))
                    mm.then_inc(fp.sem, 1)
                    if e == EARLY_EXPERT:
                        laid_out(b + 1)
                    for hd, c in early_tiles(e):
                        scores(b + 1, hd, c)
                    if e >= 1:
                        expert_out2(e - 1)
                expert_out2(E)


def kernel(x, L0_tok_W_emb, L0_tok_W_pos, L0_attn_in_w, L0_attn_conv_w, L0_attn_conv_b, L0_attn_xproj_w,
           L0_attn_A_log, L0_attn_dt_bias, L0_attn_D, L0_attn_out_w, L0_ffn_router_w, L0_ffn_router_b,
           L0_ffn_w1, L0_ffn_w2, L0_ffn_w3, L1_attn_W_qkv, L1_attn_b_qkv, L1_attn_W_out, L1_attn_b_out,
           L1_ffn_gate_weight, L1_ffn_gate_bias, L1_ffn_w1, L1_ffn_w2, L1_ffn_w3,
           L1_ffn_sw1, L1_ffn_sw2, L1_ffn_sw3):
    import concourse.bacc as bacc
    from concourse.bass_utils import run_bass_kernel_spmd

    W, bias = np.asarray(L1_attn_W_qkv), np.asarray(L1_attn_b_qkv)
    by_tile = lambda v, p=P: np.asarray(v).reshape(-1, p).T
    ffn = lambda w, s: np.concatenate([np.asarray(w), np.asarray(s)[None]], 0).transpose(0, 2, 1)
    arrays = {
        "tok": np.asarray(x).reshape(NB * TC, P).T,
        "emb": np.asarray(L0_tok_W_emb).T,
        "pos": L0_tok_W_pos, "in_w": L0_attn_in_w, "conv_w": np.asarray(L0_attn_conv_w).reshape(DI, TAPS),
        "conv_b": by_tile(L0_attn_conv_b), "xproj_w": L0_attn_xproj_w,
        "xproj_dt": by_tile(np.asarray(L0_attn_xproj_w)[:, 2 * NS]), "a_log": L0_attn_A_log,
        "dt_bias": by_tile(L0_attn_dt_bias), "d_skip": by_tile(L0_attn_D), "out_w": L0_attn_out_w,
        "router_w": L0_ffn_router_w, "router_b": L0_ffn_router_b,
        "w1": L0_ffn_w1, "w2": L0_ffn_w2, "w3": L0_ffn_w3,
        "wq": W[:, 0:D], "wk": W[:, D:2 * D], "wv": W[:, 2 * D:],
        "bq": by_tile(bias[0:D], KP), "bk": by_tile(bias[D:2 * D], KP), "bv": bias[2 * D:],
        "wo": L1_attn_W_out, "bo": L1_attn_b_out,
        "gate_w": np.asarray(L1_ffn_gate_weight).T, "gate_b": L1_ffn_gate_bias,
        "f1": ffn(L1_ffn_w1, L1_ffn_sw1), "f3": ffn(L1_ffn_w3, L1_ffn_sw3), "f2": ffn(L1_ffn_w2, L1_ffn_sw2),
    }
    arrays = {k: np.ascontiguousarray(a) for k, a in arrays.items()}
    nc = bacc.Bacc("TRN2", target_bir_lowering=False, num_devices=1)
    args = [nc.dram_tensor(k, a.shape, mybir.dt.from_np(a.dtype), kind="ExternalInput").ap()
            for k, a in arrays.items()]
    out = nc.dram_tensor("y", (NB, T, D), F32, kind="ExternalOutput").ap()
    tower(nc, *args, out)
    r = run_bass_kernel_spmd(nc, [arrays], core_ids=[0])
    return r.results[0]["y"]
```
